# Optimizing a Trainium2 kernel written in Bass

```python
import numpy as np
import jax
import jax.numpy as jnp

def _softmax(x, axis=-1):
    return jax.nn.softmax(x, axis=axis)

def _gelu(x):
    return jax.nn.gelu(x, approximate=True)

def _silu(x):
    return jax.nn.silu(x)

def _sigmoid(x):
    return jax.nn.sigmoid(x)

def _layernorm(x, axis=-1, eps=1e-05):
    m = jnp.mean(x, axis=axis, keepdims=True)
    v = jnp.var(x, axis=axis, keepdims=True)
    return (x - m) / jnp.sqrt(v + eps)

def _scatter_add(tgt, idx, src, axis=0):
    return tgt.at[idx].add(src)

def _segment_sum(src, seg, n):
    return jax.ops.segment_sum(src, seg, n)
kernel_name = 'mk_gnn_resnorm_d4_gnn_r32_b5ff90'

def setup_inputs(seed: int=0):
    np.random.seed(seed)
    _w = jnp.asarray

    def _rec_inputs():
        import jax
        import jax.numpy as jnp
        _gk = jax.random.key(seed)
        x = -0.000202 + 1 * jax.random.normal(jax.random.fold_in(_gk, 1), (3125, 64), jnp.float32)
        src = jax.random.randint(jax.random.fold_in(_gk, 2), (100000,), 0, 3125, jnp.int32)
        dst = jax.random.randint(jax.random.fold_in(_gk, 3), (100000,), 0, 3125, jnp.int32)
        _o = jnp.argsort(dst, stable=True)
        src = src[_o]
        dst = dst[_o]
        edge_attr_32 = -5.3897e-05 + 0.999841 * jax.random.normal(jax.random.fold_in(_gk, 11), (100000, 32), jnp.float32)
        edge_weight = jax.random.uniform(jax.random.fold_in(_gk, 13), (100000,), jnp.float32, 0.0, 0.999999)
        return (x, src, dst, edge_attr_32, edge_weight)
    x, src, dst, edge_attr_32, edge_weight = _rec_inputs()

    def _L0_gnn_setup():
        import jax, jax.numpy as jnp
        import numpy as np
        N_NODES = 3125
        N_EDGES = 50000
        D_FEAT = 64
        key = jax.random.key(seed)
        k1, k2, k3 = jax.random.split(key, 3)
        x = jax.random.normal(k1, (N_NODES, D_FEAT), dtype=jnp.float32)
        edge_index = jax.random.randint(k2, (2, N_EDGES), 0, N_NODES, dtype=jnp.int64)
        edge_attr = jax.random.uniform(k3, (N_EDGES,), dtype=jnp.float32)
        return {'x': x, 'edge_index': edge_index, 'edge_attr': edge_attr}
    _L0_gnn_all = _L0_gnn_setup()
    _L0_gnn_in = {k: v for k, v in _L0_gnn_all.items() if k in ()}
    del _L0_gnn_all

    def _L1_gnn_setup():
        import jax, jax.numpy as jnp
        import numpy as np
        N, E = (50000, 25000)
        D_NODE, D_EDGE, H = (64, 32, 4)
        D_H = D_NODE // H
        LN_EPS = 1e-05
        key = jax.random.key(seed)
        ks = jax.random.split(key, 16)
        s = 1.0 / np.sqrt(D_NODE)
        inp = {'node_features': jax.random.normal(ks[0], (N, D_NODE), jnp.float32), 'edge_features': jax.random.normal(ks[1], (E, D_EDGE), jnp.float32), 'edge_index': jax.random.randint(ks[2], (2, E), 0, N, jnp.int64), 'Wq': jax.random.normal(ks[3], (D_NODE, D_NODE), jnp.float32) * s, 'bq': jnp.zeros((D_NODE,), jnp.float32), 'Wk': jax.random.normal(ks[4], (D_NODE, D_NODE), jnp.float32) * s, 'bk': jnp.zeros((D_NODE,), jnp.float32), 'Wv': jax.random.normal(ks[5], (D_NODE, D_NODE), jnp.float32) * s, 'bv': jnp.zeros((D_NODE,), jnp.float32), 'We': jax.random.normal(ks[6], (H, D_EDGE), jnp.float32) * (1.0 / np.sqrt(D_EDGE)), 'be': jnp.zeros((H,), jnp.float32), 'Wo': jax.random.normal(ks[7], (D_NODE, D_NODE), jnp.float32) * s, 'bo': jnp.zeros((D_NODE,), jnp.float32), 'ln_gamma': jnp.ones((D_NODE,), jnp.float32), 'ln_beta': jnp.zeros((D_NODE,), jnp.float32), 'log_temp': jnp.zeros((H,), jnp.float32)}
        return inp
    _L1_gnn_all = _L1_gnn_setup()
    _L1_gnn_in = {k: v for k, v in _L1_gnn_all.items() if k in ('Wq', 'bq', 'Wk', 'bk', 'Wv', 'bv', 'We', 'be', 'Wo', 'bo', 'ln_gamma', 'ln_beta', 'log_temp')}
    del _L1_gnn_all

    def _L2_gnn_setup():
        import jax, jax.numpy as jnp
        import numpy as np
        NEG_SLOPE = 0.2
        key = jax.random.key(seed)
        ks = jax.random.split(key, 5)
        N, E, Din, Dout = (3125, 50000, 64, 64)
        x = jax.random.normal(ks[0], (N, Din), dtype=jnp.float32)
        edge_index = jax.random.randint(ks[1], (2, E), 0, N, dtype=jnp.int64)
        W_l = jax.random.normal(ks[2], (Din, Dout), dtype=jnp.float32) / np.sqrt(Din)
        W_r = jax.random.normal(ks[3], (Din, Dout), dtype=jnp.float32) / np.sqrt(Din)
        att = jax.random.normal(ks[4], (Dout,), dtype=jnp.float32) / np.sqrt(Dout)
        bias = jnp.zeros((Dout,), dtype=jnp.float32)
        return {'x': x, 'edge_index': edge_index, 'W_l': W_l, 'W_r': W_r, 'att': att, 'bias': bias}
    _L2_gnn_all = _L2_gnn_setup()
    _L2_gnn_in = {k: v for k, v in _L2_gnn_all.items() if k in ('W_l', 'W_r', 'att', 'bias')}
    del _L2_gnn_all

    def _L3_gnn_setup():
        import jax, jax.numpy as jnp
        import numpy as np
        N = 3125
        E = 50000

        def _gcn_layer(x, row, col, W, b):
            agg = jax.ops.segment_sum(x[col], row, num_segments=N)
            deg = jax.ops.segment_sum(jnp.ones((row.shape[0],), x.dtype), row, num_segments=N)
            deg = jnp.clip(deg, 1.0, None)[:, None]
            return (agg / deg + x) @ W + b
        key = jax.random.key(seed)
        ks = jax.random.split(key, 6)
        x = jax.random.normal(ks[0], (N, 64), dtype=jnp.float32)
        edge_index = jax.random.randint(ks[1], (2, E), 0, N, dtype=jnp.int64)
        W1 = jax.random.normal(ks[2], (64, 128), dtype=jnp.float32) * 0.1
        b1 = jax.random.normal(ks[3], (128,), dtype=jnp.float32) * 0.1
        W2 = jax.random.normal(ks[4], (128, 64), dtype=jnp.float32) * 0.1
        b2 = jax.random.normal(ks[5], (64,), dtype=jnp.float32) * 0.1
        return {'x': x, 'edge_index': edge_index, 'W1': W1, 'b1': b1, 'W2': W2, 'b2': b2}
    _L3_gnn_all = _L3_gnn_setup()
    _L3_gnn_in = {k: v for k, v in _L3_gnn_all.items() if k in ('W1', 'b1', 'W2', 'b2')}
    del _L3_gnn_all
    return {'x': x, 'src': src, 'dst': dst, 'edge_attr_32': edge_attr_32, 'edge_weight': edge_weight, 'L1_gnn_Wq': _L1_gnn_in['Wq'], 'L1_gnn_bq': _L1_gnn_in['bq'], 'L1_gnn_Wk': _L1_gnn_in['Wk'], 'L1_gnn_bk': _L1_gnn_in['bk'], 'L1_gnn_Wv': _L1_gnn_in['Wv'], 'L1_gnn_bv': _L1_gnn_in['bv'], 'L1_gnn_We': _L1_gnn_in['We'], 'L1_gnn_be': _L1_gnn_in['be'], 'L1_gnn_Wo': _L1_gnn_in['Wo'], 'L1_gnn_bo': _L1_gnn_in['bo'], 'L1_gnn_ln_gamma': _L1_gnn_in['ln_gamma'], 'L1_gnn_ln_beta': _L1_gnn_in['ln_beta'], 'L1_gnn_log_temp': _L1_gnn_in['log_temp'], 'L2_gnn_W_l': _L2_gnn_in['W_l'], 'L2_gnn_W_r': _L2_gnn_in['W_r'], 'L2_gnn_att': _L2_gnn_in['att'], 'L2_gnn_bias': _L2_gnn_in['bias'], 'L3_gnn_W1': _L3_gnn_in['W1'], 'L3_gnn_b1': _L3_gnn_in['b1'], 'L3_gnn_W2': _L3_gnn_in['W2'], 'L3_gnn_b2': _L3_gnn_in['b2']}

def reference(x, src, dst, edge_attr_32, edge_weight, L1_gnn_Wq, L1_gnn_bq, L1_gnn_Wk, L1_gnn_bk, L1_gnn_Wv, L1_gnn_bv, L1_gnn_We, L1_gnn_be, L1_gnn_Wo, L1_gnn_bo, L1_gnn_ln_gamma, L1_gnn_ln_beta, L1_gnn_log_temp, L2_gnn_W_l, L2_gnn_W_r, L2_gnn_att, L2_gnn_bias, L3_gnn_W1, L3_gnn_b1, L3_gnn_W2, L3_gnn_b2):
    import jax
    import jax.numpy as jnp

    def _L0_gnn_ref(x, edge_index, edge_attr):
        import jax, jax.numpy as jnp
        import numpy as np
        N_NODES = 3125
        N_EDGES = 50000
        D_FEAT = 64
        row, col = (edge_index[0], edge_index[1])
        B = jnp.exp(-edge_attr)
        msgs = B[:, None] * x[col]
        out = jax.ops.segment_sum(msgs, row, num_segments=N_NODES)
        return out

    def _L1_gnn_ref(node_features, edge_features, edge_index, Wq, bq, Wk, bk, Wv, bv, We, be, Wo, bo, ln_gamma, ln_beta, log_temp):
        import jax, jax.numpy as jnp
        import numpy as np
        N, E = (50000, 25000)
        D_NODE, D_EDGE, H = (64, 32, 4)
        D_H = D_NODE // H
        LN_EPS = 1e-05
        n = node_features.shape[0]
        x = node_features
        Q = (x @ Wq.T + bq).reshape(n, H, D_H)
        K = (x @ Wk.T + bk).reshape(n, H, D_H)
        V = (x @ Wv.T + bv).reshape(n, H, D_H)
        src, tgt = (edge_index[0], edge_index[1])
        scores = jnp.einsum('ehd,ehd->eh', Q[tgt], K[src]) / np.float32(np.sqrt(D_H))
        scores = scores + (edge_features @ We.T + be)
        scores = scores * jnp.exp(log_temp)
        mx = jax.ops.segment_max(scores, tgt, num_segments=n)
        mx = jnp.maximum(mx, -1000000000.0)
        ex = jnp.exp(scores - mx[tgt])
        denom = jax.ops.segment_sum(ex, tgt, num_segments=n)
        attn = ex / (denom[tgt] + 1e-10)
        out = jax.ops.segment_sum(V[src] * attn[:, :, None], tgt, num_segments=n)
        out = out.reshape(n, D_NODE) @ Wo.T + bo
        y = x + out
        mu = jnp.mean(y, axis=-1, keepdims=True)
        var = jnp.mean((y - mu) ** 2, axis=-1, keepdims=True)
        return (y - mu) / jnp.sqrt(var + LN_EPS) * ln_gamma + ln_beta

    def _L2_gnn_ref(x, edge_index, W_l, W_r, att, bias):
        import jax, jax.numpy as jnp
        import numpy as np
        NEG_SLOPE = 0.2
        N = x.shape[0]
        loop = jnp.arange(N, dtype=edge_index.dtype)
        src = jnp.concatenate([edge_index[0], loop])
        dst = jnp.concatenate([edge_index[1], loop])
        x_l = x @ W_l
        x_r = x @ W_r
        e = jax.nn.leaky_relu(x_l[src] + x_r[dst], NEG_SLOPE) @ att
        e_max = jax.ops.segment_max(e, dst, num_segments=N)
        e_exp = jnp.exp(e - e_max[dst])
        denom = jax.ops.segment_sum(e_exp, dst, num_segments=N)
        alpha = e_exp / denom[dst]
        out = jax.ops.segment_sum(alpha[:, None] * x_l[src], dst, num_segments=N)
        return out + bias

    def _L3_gnn_ref(x, edge_index, W1, b1, W2, b2):
        import jax, jax.numpy as jnp
        import numpy as np
        N = 3125
        E = 50000

        def _gcn_layer(x, row, col, W, b):
            agg = jax.ops.segment_sum(x[col], row, num_segments=N)
            deg = jax.ops.segment_sum(jnp.ones((row.shape[0],), x.dtype), row, num_segments=N)
            deg = jnp.clip(deg, 1.0, None)[:, None]
            return (agg / deg + x) @ W + b
        row, col = (edge_index[0], edge_index[1])
        h = jax.nn.relu(_gcn_layer(x, row, col, W1, b1))
        h = _gcn_layer(h, row, col, W2, b2)
        return h
    edge_index = jnp.stack([src, dst])
    x = _layernorm(x + _L0_gnn_ref(x, edge_index, edge_weight), axis=-1)
    x = _layernorm(x + _L1_gnn_ref(x, edge_attr_32, edge_index, L1_gnn_Wq, L1_gnn_bq, L1_gnn_Wk, L1_gnn_bk, L1_gnn_Wv, L1_gnn_bv, L1_gnn_We, L1_gnn_be, L1_gnn_Wo, L1_gnn_bo, L1_gnn_ln_gamma, L1_gnn_ln_beta, L1_gnn_log_temp), axis=-1)
    x = _layernorm(x + _L2_gnn_ref(x, edge_index, L2_gnn_W_l, L2_gnn_W_r, L2_gnn_att, L2_gnn_bias), axis=-1)
    x = _layernorm(x + _L3_gnn_ref(x, edge_index, L3_gnn_W1, L3_gnn_b1, L3_gnn_W2, L3_gnn_b2), axis=-1)
    return x

_drawn_inputs = setup_inputs


def setup_inputs(seed=0):
    import zlib

    import numpy as np

    out = dict(_drawn_inputs(seed))
    spreads = {'L1_gnn_bq': (0.0, 0.622),
     'L1_gnn_bk': (0.0, 0.8),
     'L1_gnn_bv': (0.0, 0.1),
     'L1_gnn_be': (0.0, 0.8),
     'L1_gnn_bo': (0.0, 0.1),
     'L1_gnn_ln_gamma': (1.0, 0.2),
     'L1_gnn_ln_beta': (0.0, 0.1),
     'L1_gnn_log_temp': (0.0, 0.673),
     'L2_gnn_bias': (0.0, 0.1)}
    factors = {}
    for name, (base, spread) in spreads.items():
        noise = np.random.default_rng([zlib.crc32(name.encode()), seed]).standard_normal(out[name].shape)
        drawn = base * np.exp(spread * noise) if base else spread * noise
        out[name] = jnp.asarray(drawn.astype(out[name].dtype))
    for name, factor in factors.items():
        out[name] = (out[name] * factor).astype(out[name].dtype)
    return out
```

```python
import concourse.bass as bass
from concourse import mybir
from contextlib import ExitStack

F32 = mybir.dt.float32
I32 = mybir.dt.int32
ALU = mybir.AluOpType
ACT = mybir.ActivationFunctionType
AX = mybir.AxisListType

NODES, EDGES, D, DE, HEADS, HID = 3125, 100000, 64, 32, 4, 128
DH = D // HEADS
P = 128
NT = -(-NODES // P)
NPAD = NT * P
GROUP = 2 * P
GROUPS = -(-EDGES // GROUP)
EPAD = GROUPS * GROUP
CHUNK = EPAD // P
BODY = 4
TB = 2 * BODY
CELLS = -(-(GROUPS + NT - 1) // (2 * BODY)) * 2 * BODY
STEPS = CELLS // BODY
TILES = 2 * CELLS
CB = -(-CELLS // P)
REC = 4
HALF = 17
BIG = 1.0e30
EPS = 1e-5


def serial(eng, sem, base=0):
    n = [0]

    def step(ins):
        n[0] += 1
        ins.then_inc(sem, 1)
        eng.wait_ge(sem, base + n[0])
    return step


def gnn(nc, x, src, dst, weight, efT, wqkv, bqkv, weT, be, woT, bo, gamma, beta, log_temp,
        wlr, att, bias2, w1, b1, w2, b2, out):
    top = ExitStack()
    with top:
        used = {}

        def fresh(name):
            used[name] = used.get(name, 0) + 1
            return f"{name}_{used[name]}"

        def sbuf(name, shape, dt=F32, ctx=top):
            return ctx.enter_context(nc.sbuf_tensor(fresh(name), shape, dt))

        def psum(name, shape, ctx):
            return ctx.enter_context(nc.psum_tensor(fresh(name), shape, F32))

        live = {}

        def sem(name, ctx):
            if id(ctx) not in live:
                live[id(ctx)] = []

                def release():
                    nc.clear_and_free_semaphores(live.pop(id(ctx)))
                    nc.all_engine_barrier()
                ctx.callback(release)
            live[id(ctx)].append(nc.alloc_semaphore(fresh(name)))
            return live[id(ctx)][-1]

        def dram(name, shape, dt=F32):
            return nc.dram_tensor(name, shape, dt, kind="Internal").ap()

        rec_dram = {"dst": dram("rec_by_dst", [EPAD, REC]), "src": dram("rec_by_src", [EPAD, REC])}
        loc_dram = {o: dram(f"loc_{o}", [CELLS, GROUP]) for o in ("dst", "src")}
        key_dram = dram("clamped_dst", [CELLS, GROUP])
        k_dram = {o: dram(f"k_{o}", [CB * P], I32) for o in ("dst", "src")}
        n_dram = {o: dram(f"n_{o}", [CB * P], I32) for o in ("dst", "src")}

        ident = sbuf("ident", [P, P])
        ones = sbuf("ones", [P, P])
        before = sbuf("before", [P, P])
        lane = sbuf("lane", [P, P])
        part = sbuf("part", [P, 1])
        gather_id = {o: sbuf(f"gather_id_{o}", [P, TILES]) for o in ("dst", "src")}
        loc = {o: sbuf(f"loc_sb_{o}", [P, TILES]) for o in ("dst", "src")}
        w_src = sbuf("w_src", [P, TILES])
        n_row = {o: sbuf(f"n_row_{o}", [1, CELLS], I32) for o in ("dst", "src")}
        k_row = sbuf("k_row", [1, CELLS], I32)

        def setup():
            with ExitStack() as c, nc.Block() as block:
                made, done = sem("iota_made", c), sem("consts", c)

                @block.gpsimd
                def _(pool):
                    nc.gpsimd.iota(lane[:], [[1, P]], base=0, channel_multiplier=0,
                                   allow_small_or_imprecise_dtypes=True).then_inc(made, 1)
                    nc.gpsimd.iota(part[:], [[1, 1]], base=0, channel_multiplier=1,
                                   allow_small_or_imprecise_dtypes=True).then_inc(made, 1)

                @block.vector
                def _(dve):
                    nc.vector.memset(ones[:], 1.0)
                    dve.wait_ge(made, 2)
                    nc.vector.tensor_scalar(ident[:], lane[:], part[:], None, ALU.is_equal)
                    nc.vector.tensor_scalar(before[:], lane[:], part[:], None, ALU.is_gt).then_inc(done, 1)

        def rank_and_scatter():
            with ExitStack() as c:
                rec = sbuf("rec", [P, CHUNK, REC], ctx=c)
                place = sbuf("place", [P, CHUNK], I32, ctx=c)
                with ExitStack() as r:
                    s_i = sbuf("src_i", [P, CHUNK], I32, ctx=r)
                    d_i = sbuf("dst_i", [P, CHUNK], I32, ctx=r)
                    w_f = sbuf("w_f", [P, CHUNK], ctx=r)
                    tile = sbuf("src_tile", [P, CHUNK], ctx=r)
                    hit = sbuf("hit", [P, CHUNK], ctx=r)
                    run = sbuf("run", [P, CHUNK], ctx=r)
                    rank = sbuf("rank", [P, CHUNK], ctx=r)
                    count = sbuf("count", [P, NT], ctx=r)
                    total = sbuf("total", [P, NT], ctx=r)
                    upto = sbuf("upto", [P, NT], ctx=r)
                    base = sbuf("base", [P, NT], ctx=r)
                    ahead = psum("ahead", [P, 512], r)
                    with nc.Block() as block:
                        loaded = [sem(f"loaded{i}", r) for i in range(3)]
                        filled, stored = sem("rec_filled", r), sem("rec_stored", r)
                        ew, counted, summed = sem("exp_w", r), sem("counted", r), sem("summed", r)
                        own, own_l, own_p = sem("dve_own", r), sem("dve_loop", r), sem("dve_place", r)

                        @block.sync
                        def _(sp):
                            for i, (to, frm) in enumerate(((s_i, src), (d_i, dst), (w_f, weight))):
                                sp.dma_start(to[:], frm.rearrange("(p j) -> p j", p=P)).then_inc(loaded[i], 16)
                            sp.wait_ge(filled, 1)
                            sp.wait_ge(ew, 1)
                            sp.dma_start(rec_dram["dst"].rearrange("(p j) r -> p (j r)", p=P),
                                         rec[:].rearrange("p j r -> p (j r)")).then_inc(stored, 16)
                            sp.wait_ge(stored, 16)

                        @block.scalar
                        def _(act):
                            act.wait_ge(loaded[2], 16)
                            nc.scalar.activation(rec[:, :, 2], w_f[:], ACT.Exp, scale=-1.0).then_inc(ew, 1)

                        @block.vector
                        def _(dve):
                            step = serial(dve, own)
                            step(nc.vector.memset(rec[:, :, 3], 0.0))
                            step(nc.vector.memset(rank[:], 0.0))
                            dve.wait_ge(loaded[0], 16)
                            step(nc.vector.tensor_copy(rec[:, :, 0], s_i[:]))
                            dve.wait_ge(loaded[1], 16)
                            nc.vector.tensor_copy(rec[:, :, 1], d_i[:]).then_inc(filled, 1)
                            step(nc.vector.tensor_single_scalar(s_i[:], s_i[:], 7, op=ALU.arith_shift_right))
                            step(nc.vector.tensor_copy(tile[:], s_i[:]))
                            with dve.Fori(0, NT) as v:
                                s = serial(dve, own_l, v * 5)
                                s(nc.vector.tensor_scalar(hit[:], tile[:], lane[:, bass.ds(v, 1)], None, ALU.is_equal))
                                s(nc.vector.tensor_tensor_scan(run[:], hit[:], hit[:], 0.0, ALU.add, ALU.max))
                                s(nc.vector.tensor_copy(count[:, bass.ds(v, 1)], run[:, CHUNK - 1:CHUNK]))
                                s(nc.vector.tensor_tensor(hit[:], hit[:], run[:], ALU.mult))
                                s(nc.vector.tensor_tensor(rank[:], rank[:], hit[:], ALU.add))
                            dve.sem_inc(counted, 1)
                            dve.wait_ge(summed, 1)
                            step(nc.vector.tensor_copy(total[:], ahead[:, 64:64 + NT]))
                            step(nc.vector.tensor_tensor_scan(upto[:], total[:], total[:], 0.0, ALU.add, ALU.max))
                            step(nc.vector.tensor_tensor(upto[:], upto[:], total[:], ALU.subtract))
                            step(nc.vector.scalar_tensor_tensor(base[:], upto[:], -1.0, ahead[:, 0:NT], ALU.add, ALU.add))
                            with dve.Fori(0, NT) as v:
                                s = serial(dve, own_p, v * 2)
                                s(nc.vector.tensor_scalar(hit[:], tile[:], lane[:, bass.ds(v, 1)],
                                                          base[:, bass.ds(v, 1)], ALU.is_equal, ALU.mult))
                                s(nc.vector.tensor_tensor(rank[:], rank[:], hit[:], ALU.add))
                            step(nc.vector.tensor_copy(place[:], rank[:]))

                        @block.tensor
                        def _(pe):
                            pe.wait_ge(counted, 1)
                            nc.tensor.matmul(ahead[:, 0:NT], before[:], count[:], start=True, stop=True)
                            nc.tensor.matmul(ahead[:, 64:64 + NT], ones[:], count[:], start=True,
                                             stop=True).then_inc(summed, 1)
                with ExitStack() as r, nc.Block() as block:
                    ids = sbuf("place_slot", [P, 2, HALF], I32, ctx=r)
                    rows = sbuf("rec_slot", [P, 2, HALF, REC], ctx=r)
                    copied = [sem(f"copied{h}", r) for h in range(2)]
                    sent = [sem(f"sent{h}", r) for h in range(2)]
                    taken = sem("taken", r)
                    LOOPS = CHUNK // (2 * HALF)

                    @block.scalar
                    def _(act):
                        with act.Fori(0, LOOPS) as i:
                            for h in range(2):
                                act.wait_ge(sent[h], i * (16 * HALF))
                                at = i * (2 * HALF) + h * HALF
                                nc.scalar.copy(ids[:, h, :], place[:, bass.ds(at, HALF)]).then_inc(copied[h], 1)
                                nc.scalar.copy(rows[:, h, :, :], rec[:, bass.ds(at, HALF), :]).then_inc(copied[h], 1)

                    @block.gpsimd
                    def _(pool):
                        with pool.Fori(0, LOOPS) as i:
                            for h in range(2):
                                pool.wait_ge(copied[h], i * 2 + 2)
                                pool.sem_inc(taken, 1)
                                for t in range(HALF):
                                    pool.indirect_dma_start(
                                        out=rec_dram["src"], out_offset=bass.IndirectOffsetOnAxis(ap=ids[:, h, t:t + 1], axis=0),
                                        in_=rows[:, h, t, :], in_offset=None).then_inc(sent[h], 16)
                        for h in range(2):
                            pool.wait_ge(sent[h], LOOPS * 16 * HALF)

        def prepare(order):
            key_col, other_col = (0, 1) if order == "src" else (1, 0)
            recs = rec_dram[order]
            with ExitStack() as c, nc.Block() as block:
                last = sbuf("last_key", [P, CB], ctx=c)
                last_i = sbuf("last_i", [P, CB], I32, ctx=c)
                diag = sbuf("diag", [P, CB, P], ctx=c)
                ends = sbuf("ends", [P, CB * P], ctx=c)
                kk = sbuf("kk", [P, CB * P], ctx=c)
                less = sbuf("less", [P, CB * P], ctx=c)
                cell = sbuf("cell", [P, CB], ctx=c)
                k_f = sbuf("k_f", [P, CB], ctx=c)
                n_f = sbuf("n_f", [P, CB], ctx=c)
                n_c = sbuf("n_c", [P, CB], ctx=c)
                k_i = sbuf("k_i", [P, CB], I32, ctx=c)
                n_i = sbuf("n_i", [P, CB], I32, ctx=c)
                R = sbuf("cell_recs", [P, CB, GROUP, REC], ctx=c)
                L = sbuf("cell_loc", [P, CB, GROUP], ctx=c)
                K = sbuf("cell_key", [P, CB, GROUP], ctx=c)
                V = sbuf("cell_valid", [P, CB, GROUP], ctx=c)
                pB = psum("ends_all", [P, CB * P], c)
                pT = [psum(f"turned{i}", [P, 512], c) for i in range(4)]
                loaded, iotas, own = sem("last_loaded", c), sem("iotas", c), sem("own", c)
                cleared = sem("last_cleared", c)
                diag_made, spread = sem("diag_made", c), sem("spread", c)
                k_made, got = sem("k_made", c), [sem(f"got{b}", c) for b in range(CB)]
                rows_made, turned, freed = sem("rows_made", c), sem("turned", c), sem("freed", c)
                put, back = [sem(f"put{i}", c) for i in range(4)], sem("back", c)
                rows_in = [min(P, CELLS - b * P) for b in range(CB)]
                full = GROUPS // P
                rest = GROUPS - full * P
                turns = [(b, g, q) for b in range(CB) for g in range(2) for q in range(3 if order == "src" else 2)]

                @block.sync
                def _(sp):
                    ends_v = recs.rearrange("(k e) r -> k (e r)", e=GROUP)[:, (GROUP - 1) * REC + key_col:(GROUP - 1) * REC + key_col + 1]
                    sp.wait_ge(cleared, 1)
                    with nc.allow_non_contiguous_dma(reason="one key of each group"):
                        for b in range(CB):
                            m = P if b < full else rest
                            sp.dma_start(last[:m, b:b + 1], ends_v[b * P:b * P + m, :]).then_inc(loaded, 16)
                    sp.wait_ge(k_made, 1)
                    with nc.allow_non_contiguous_dma(reason="one word of each cell"):
                        sp.dma_start(k_dram[order].rearrange("(b p) -> p b", p=P), k_i[:]).then_inc(put[0], 16)
                        sp.dma_start(n_dram[order].rearrange("(b p) -> p b", p=P), n_i[:]).then_inc(put[1], 16)
                    sp.wait_ge(put[0], 16)
                    sp.wait_ge(put[1], 16)
                    if order == "dst":
                        sp.dma_start(k_row[:], k_dram[order][0:CELLS].rearrange("(a k) -> a k", a=1)).then_inc(back, 16)
                    sp.dma_start(n_row[order][:], n_dram[order][0:CELLS].rearrange("(a k) -> a k", a=1)).then_inc(back, 16)
                    sp.wait_ge(rows_made, 1)
                    if order == "dst":
                        for b in range(CB):
                            m = rows_in[b]
                            sp.dma_start(loc_dram[order][b * P:b * P + m, :], L[:m, b, :]).then_inc(put[2], 16)
                            sp.dma_start(key_dram[b * P:b * P + m, :], K[:m, b, :]).then_inc(put[3], 16)
                        sp.wait_ge(put[2], 16 * CB)
                        sp.wait_ge(put[3], 16 * CB)
                    sp.wait_ge(back, 32 if order == "dst" else 16)

                @block.gpsimd
                def _(pool):
                    nc.gpsimd.iota(kk[:], [[1, CB * P]], base=0, channel_multiplier=0,
                                   allow_small_or_imprecise_dtypes=True).then_inc(iotas, 1)
                    nc.gpsimd.iota(cell[:], [[P, CB]], base=0, channel_multiplier=1,
                                   allow_small_or_imprecise_dtypes=True).then_inc(iotas, 1)
                    pool.wait_ge(k_made, 1)
                    view = recs.rearrange("(k e) r -> k (e r)", e=GROUP)
                    for b in range(CB):
                        m = rows_in[b]
                        pool.indirect_dma_start(
                            out=R[:m, b, :, :].rearrange("p e r -> p (e r)"), out_offset=None, in_=view,
                            in_offset=bass.IndirectOffsetOnAxis(ap=k_i[:m, b:b + 1], axis=0)).then_inc(got[b], 16)

                @block.vector
                def _(dve):
                    step = serial(dve, own)
                    nc.vector.memset(last[:], 0.0).then_inc(cleared, 1)
                    dve.wait_ge(loaded, 16 * CB)
                    step(nc.vector.tensor_copy(last_i[:], last[:]))
                    step(nc.vector.tensor_single_scalar(last_i[:], last_i[:], 7, op=ALU.arith_shift_right))
                    step(nc.vector.tensor_copy(last[:], last_i[:]))
                    for b in range(CB):
                        ins = nc.vector.tensor_scalar(diag[:, b, :], ident[:], last[:, b:b + 1], None, ALU.mult)
                    ins.then_inc(diag_made, 1)
                    dve.wait_ge(iotas, 2)
                    dve.wait_ge(spread, 1)
                    step(nc.vector.tensor_tensor(ends[:], pB[:], kk[:], ALU.add))
                    step(nc.vector.memset(ends[:, GROUPS:], 1.0e6))
                    for b in range(CB):
                        step(nc.vector.tensor_scalar(less[:], ends[:], cell[:, b:b + 1], None, ALU.is_lt))
                        step(nc.vector.tensor_reduce(k_f[:, b:b + 1], less[:], AX.X, ALU.add))
                    step(nc.vector.tensor_scalar(k_f[:], k_f[:], float(GROUPS - 1), None, ALU.min))
                    step(nc.vector.tensor_tensor(n_f[:], cell[:], k_f[:], ALU.subtract))
                    step(nc.vector.tensor_scalar(n_c[:], n_f[:], float(NT - 1), None, ALU.min))
                    step(nc.vector.tensor_copy(n_i[:], n_c[:]))
                    nc.vector.tensor_copy(k_i[:], k_f[:]).then_inc(k_made, 1)
                    step(nc.vector.tensor_scalar(n_f[:], n_f[:], float(P), None, ALU.mult))
                    step(nc.vector.memset(L[:], -1.0))
                    for b in range(CB):
                        m = rows_in[b]
                        dve.wait_ge(got[b], 16)
                        step(nc.vector.tensor_scalar(L[:m, b, :], R[:m, b, :, key_col], n_f[:m, b:b + 1], None, ALU.subtract))
                        step(nc.vector.tensor_scalar(K[:m, b, :], L[:m, b, :], 0.0, float(P - 1), ALU.max, ALU.min))
                        step(nc.vector.tensor_tensor(V[:m, b, :], L[:m, b, :], K[:m, b, :], ALU.is_equal))
                        step(nc.vector.scalar_tensor_tensor(L[:m, b, :], L[:m, b, :], 1.0, V[:m, b, :], ALU.add, ALU.mult))
                        step(nc.vector.tensor_scalar(L[:m, b, :], L[:m, b, :], -1.0, None, ALU.add))
                        step(nc.vector.tensor_scalar(K[:m, b, :], K[:m, b, :], n_f[:m, b:b + 1], None, ALU.add))
                    dve.sem_inc(rows_made, 1)
                    for i, (b, g, q) in enumerate(turns):
                        m = rows_in[b]
                        dve.wait_ge(turned, i + 1)
                        to = (gather_id[order], loc[order], w_src)[q]
                        to = to[:].rearrange("p (c g) -> p c g", g=2)[:, b * P:b * P + m, g]
                        nc.vector.tensor_copy(to, pT[i % 4][:, 0:m]).then_inc(freed, 1)

                @block.tensor
                def _(pe):
                    pe.wait_ge(diag_made, 1)
                    nc.tensor.matmul(pB[:], ones[:], diag[:].rearrange("p b q -> p (b q)"), start=True,
                                     stop=True).then_inc(spread, 1)
                    pe.wait_ge(rows_made, 1)
                    for i, (b, g, q) in enumerate(turns):
                        m = rows_in[b]
                        half = slice(g * P, (g + 1) * P)
                        if i >= 4:
                            pe.wait_ge(freed, i - 3)
                        frm = (R[:m, b, half, other_col], L[:m, b, half], R[:m, b, half, 2])[q]
                        nc.tensor.transpose(pT[i % 4][:, 0:m], frm, ident[:m, :m]).then_inc(turned, 1)


        def aggregate(order, acc, cols, table=None, stream=None, weights=None, extra=None):
            with ExitStack() as c, nc.Block() as block:
                rows = sbuf("rows", [P, 2, TB, D], ctx=c)
                ids = sbuf("id_slot", [P, 2, TB], I32, ctx=c)
                hot = sbuf("hot", [P, 2, TB, P], ctx=c)
                mixed = sbuf("mixed", [P, 2, TB, cols], ctx=c) if weights is not None else rows
                part_sum = psum("part_sum", [P, 2, BODY, P], c)
                ids_made = [sem(f"ids_made{h}", c) for h in range(2)]
                arrived = [sem(f"arrived{h}", c) for h in range(2)]
                hot_made = [sem(f"hot_made{h}", c) for h in range(2)]
                mixed_made = [sem(f"mixed_made{h}", c) for h in range(2)]
                beside = [sem(f"beside{h}", c) for h in range(2)]
                summed = [sem(f"summed{h}", c) for h in range(2)]
                added = [sem(f"added{h}", c) for h in range(2)]
                cleared, taken, own = sem("cleared", c), sem("taken", c), sem("own", c)
                rows_used = mixed_made if weights is not None else summed
                PER = 16 * TB if table is not None else 16
                n_extra = 0 if extra is None else extra.shape[2]

                if table is not None:
                    @block.gpsimd
                    def _(pool):
                        with pool.Fori(0, STEPS // 2) as i:
                            for h in range(2):
                                pool.wait_ge(ids_made[h], i + 1)
                                pool.wait_ge(rows_used[h], i)
                                pool.sem_inc(taken, 1)
                                for t in range(TB):
                                    pool.indirect_dma_start(
                                        out=rows[:, h, t, :], out_offset=None, in_=table,
                                        in_offset=bass.IndirectOffsetOnAxis(ap=ids[:, h, t:t + 1], axis=0)
                                    ).then_inc(arrived[h], 16)
                else:
                    @block.sync
                    def _(sp):
                        with sp.Fori(0, STEPS // 2) as i:
                            for h in range(2):
                                sp.wait_ge(rows_used[h], i)
                                at = (i * 2 + h) * (TB * D)
                                sp.dma_start(rows[:, h, :, :].rearrange("p t d -> p (t d)"),
                                             stream[:, bass.ds(at, TB * D)]).then_inc(arrived[h], 16)

                if table is not None or n_extra:
                    @block.scalar
                    def _(act):
                        with act.Fori(0, STEPS // 2) as i:
                            for h in range(2):
                                at = (i * 2 + h) * TB
                                if table is not None:
                                    act.wait_ge(arrived[h], i * PER)
                                    nc.scalar.copy(ids[:, h, :], gather_id[order][:, bass.ds(at, TB)]).then_inc(ids_made[h], 1)
                                if n_extra:
                                    act.wait_ge(summed[h], i)
                                    nc.scalar.copy(mixed[:, h, :, D:D + n_extra],
                                                   extra[:, bass.ds(at, TB), :]).then_inc(beside[h], 1)

                @block.vector
                def _(dve):
                    nc.vector.memset(acc[:], 0.0).then_inc(cleared, 1)
                    if cols > D + n_extra:
                        nc.vector.memset(mixed[:, :, :, D + n_extra:cols], 1.0).then_inc(cleared, 1)
                        dve.wait_ge(cleared, 2)
                    dve.wait_ge(cleared, 1)
                    with dve.Fori(0, STEPS // 2) as i:
                        step = serial(dve, own, i * (2 * BODY))
                        for h in range(2):
                            at = (i * 2 + h) * TB
                            dve.wait_ge(summed[h], i)
                            for t in range(TB):
                                ins = nc.vector.tensor_scalar(hot[:, h, t, :], lane[:], loc[order][:, bass.ds(at + t, 1)],
                                                              None, ALU.is_equal)
                            ins.then_inc(hot_made[h], 1)
                            if weights is not None:
                                dve.wait_ge(arrived[h], i * PER + PER)
                                wt = weights[:, bass.ds(at, TB), :]
                                k = wt.shape[2]
                                nc.vector.tensor_tensor(
                                    mixed[:, h, :, 0:D].rearrange("p t (k d) -> p t k d", k=k),
                                    rows[:, h, :, :].rearrange("p t (k d) -> p t k d", k=k),
                                    wt.unsqueeze(3).to_broadcast([P, TB, k, D // k]), ALU.mult).then_inc(mixed_made[h], 1)
                            dve.wait_ge(summed[h], i + 1)
                            for b in range(BODY):
                                n = dve.value_load(n_row[order][0:1, bass.ds((i * 2 + h) * BODY + b, 1)], min_val=0, max_val=NT - 1)
                                to = acc[:, bass.ds(n, 1), 0:cols].rearrange("p a c -> p (a c)")
                                ins = nc.vector.tensor_tensor(to, to, part_sum[:, h, b, 0:cols], ALU.add)
                                step(ins)
                            dve.sem_inc(added[h], 1)

                @block.tensor
                def _(pe):
                    with pe.Fori(0, STEPS // 2) as i:
                        for h in range(2):
                            pe.wait_ge(hot_made[h], i + 1)
                            if weights is not None:
                                pe.wait_ge(mixed_made[h], i + 1)
                            else:
                                pe.wait_ge(arrived[h], i * PER + PER)
                            if n_extra:
                                pe.wait_ge(beside[h], i + 1)
                            pe.wait_ge(added[h], i)
                            for t in range(TB):
                                ins = nc.tensor.matmul(part_sum[:, h, t // 2, 0:cols], hot[:, h, t, :],
                                                       mixed[:, h, t, 0:cols], start=t % 2 == 0, stop=t % 2 == 1)
                            ins.then_inc(summed[h], 1)

        def edge_scores(S, table, width, kept_from, near, near_cols, finish, ef=False):
            with ExitStack() as c, nc.Block() as block:
                rows = sbuf("rows", [P, 2, TB, width], ctx=c)
                ids = sbuf("id_slot", [P, 2, TB], I32, ctx=c)
                loc_all = sbuf("loc_all", [P, 2, TB * P], ctx=c)
                hotT = sbuf("hotT", [P, 2, TB, P], ctx=c)
                a = sbuf("score_a", [P, 2, TB, D], ctx=c)
                b = sbuf("score_b", [P, 2, TB, D], ctx=c)
                efs = sbuf("ef_slot", [DE, 2, BODY, GROUP], ctx=c) if ef else None
                picked = psum("picked", [P, 2, TB, near_cols if near_cols <= D else 2 * D], c)
                bias = psum("ef_bias", [P, 2, 512], c) if ef else None
                ids_made = [sem(f"ids_made{h}", c) for h in range(2)]
                arrived = [sem(f"arrived{h}", c) for h in range(2)]
                loc_in = [sem(f"loc_in{h}", c) for h in range(2)]
                ef_in = [sem(f"ef_in{h}", c) for h in range(2)]
                hot_made = [sem(f"hot_made{h}", c) for h in range(2)]
                products = [sem(f"products{h}", c) for h in range(2)]
                scored = [sem(f"scored{h}", c) for h in range(2)]
                kept = [sem(f"kept{h}", c) for h in range(2)]
                taken, own = sem("taken", c), sem("own", c)
                loc_flat = loc_dram["dst"].rearrange("(a c) e -> a (c e)", a=1)

                @block.gpsimd
                def _(pool):
                    with pool.Fori(0, STEPS // 2) as i:
                        for h in range(2):
                            pool.wait_ge(ids_made[h], i + 1)
                            pool.wait_ge(scored[h], i)
                            pool.wait_ge(kept[h], i * 16)
                            pool.sem_inc(taken, 1)
                            for t in range(TB):
                                pool.indirect_dma_start(
                                    out=rows[:, h, t, :], out_offset=None, in_=table,
                                    in_offset=bass.IndirectOffsetOnAxis(ap=ids[:, h, t:t + 1], axis=0)
                                ).then_inc(arrived[h], 16)

                @block.sync
                def _(sp):
                    with sp.Fori(0, STEPS // 2) as i:
                        for h in range(2):
                            j = i * 2 + h
                            sp.wait_ge(hot_made[h], i)
                            sp.dma_start(loc_all[:, h, :], loc_flat[:, bass.ds(j * (TB * P), TB * P)].to_broadcast([P, TB * P])
                                         ).then_inc(loc_in[h], 16)
                            if ef:
                                sp.wait_ge(products[h], i)
                                for q in range(BODY):
                                    k = sp.value_load(k_row[0:1, bass.ds(j * BODY + q, 1)], min_val=0, max_val=GROUPS - 1)
                                    sp.dma_start(efs[:, h, q, :], efT[:, bass.ds(k * GROUP, GROUP)]).then_inc(ef_in[h], 16)

                @block.scalar
                def _(act):
                    with act.Fori(0, STEPS // 2) as i:
                        for h in range(2):
                            at = (i * 2 + h) * TB
                            act.wait_ge(arrived[h], i * (16 * TB))
                            nc.scalar.copy(ids[:, h, :], gather_id["dst"][:, bass.ds(at, TB)]).then_inc(ids_made[h], 1)
                        for h in range(2):
                            at = (i * 2 + h) * TB
                            act.wait_ge(arrived[h], i * (16 * TB) + 16 * TB)
                            act.dma_start(kept_rows[:, bass.ds(at * D, TB * D)].rearrange("p (t d) -> p t d", t=TB),
                                          rows[:, h, :, kept_from:kept_from + D]).then_inc(kept[h], 16)
                    for h in range(2):
                        act.wait_ge(kept[h], (STEPS // 2) * 16)

                @block.vector
                def _(dve):
                    with dve.Fori(0, STEPS // 2) as i:
                        step = serial(dve, own, i * (2 * finish.steps))
                        for h in range(2):
                            at = (i * 2 + h) * TB
                            dve.wait_ge(loc_in[h], i * 16 + 16)
                            dve.wait_ge(products[h], i)
                            nc.vector.tensor_scalar(hotT[:, h, :, :].rearrange("p t e -> p (t e)"), loc_all[:, h, :],
                                                    part[:], None, ALU.is_equal).then_inc(hot_made[h], 1)
                            dve.wait_ge(arrived[h], i * (16 * TB) + 16 * TB)
                            dve.wait_ge(products[h], i + 1)
                            finish(step, picked[:, h, :, :], rows[:, h, :, :], a[:, h, :, :], b[:, h, :, :],
                                   bias[:, h, 0:TB * HEADS] if ef else None, at)
                            dve.sem_inc(scored[h], 1)

                @block.tensor
                def _(pe):
                    with pe.Fori(0, STEPS // 2) as i:
                        for h in range(2):
                            pe.wait_ge(hot_made[h], i + 1)
                            pe.wait_ge(scored[h], i)
                            if ef:
                                pe.wait_ge(ef_in[h], i * (16 * BODY) + 16 * BODY)
                            for q in range(BODY):
                                n = pe.value_load(n_row["dst"][0:1, bass.ds((i * 2 + h) * BODY + q, 1)], min_val=0, max_val=NT - 1)
                                for g in range(2):
                                    t = 2 * q + g
                                    ins = nc.tensor.matmul(picked[:, h, t, 0:near_cols], hotT[:, h, t, :],
                                                           near[:, bass.ds(n, 1), 0:near_cols].rearrange("p a c -> p (a c)"),
                                                           start=True, stop=True)
                                    if ef:
                                        ins = nc.tensor.matmul(bias[:, h, t * HEADS:(t + 1) * HEADS],
                                                               efs[:, h, q, g * P:(g + 1) * P], weT_s[:],
                                                               start=True, stop=True)
                            ins.then_inc(products[h], 1)

        def softmax_exp(S, H, SE=None, SX=None, floor=None):
            NB = -(-TILES * H // P)
            W = NB * P
            TP = P // H
            NCH = NB * TP
            tail = TILES - (NB - 1) * TP
            with ExitStack() as c:
                def big(name):
                    return sbuf(name, [P, NB, P], ctx=c)
                ST, KT, LT, fwd, bwd, t1, t2 = (big(n) for n in ("ST", "KT", "LT", "fwd", "bwd", "t1", "t2"))
                ET = big("ET") if SE is not None else None
                ends = sbuf("chunk_ends", [P, 4, NB], ctx=c)
                pack = sbuf("pack", [NB, 4, H, TP], ctx=c)
                chunk = sbuf("chunk", [H, 4, NCH], ctx=c)
                links = sbuf("links", [H, 4, NCH], ctx=c)
                scans = sbuf("scans", [H, 2, NCH], ctx=c)
                carry = sbuf("carry", [H, 2, NCH], ctx=c)
                back = sbuf("carry_back", [NB, 2, H, TP], ctx=c)
                back_p = sbuf("carry_perm", [NB, 2, P], ctx=c)
                chunk_dram = dram(f"chunk_dram{H}", [4, H, NCH])
                carry_dram = dram(f"carry_dram{H}", [2, H, NCH])
                flat = lambda t: t[:].rearrange("p b e -> p (b e)")
                with nc.Block() as block:
                    PB = 4
                    pT = psum("pT", [P, PB, 512], c)
                    cleared, keys_in, turned, freed = (sem(n, c) for n in ("cleared", "keys_in", "turned", "freed"))
                    ends_made, packed, sent, chunk_in = (sem(n, c) for n in ("ends_made", "packed", "sent", "chunk_in"))
                    carry_made, carry_out, carry_in, perm_made = (sem(n, c) for n in ("carry_made", "carry_out", "carry_in", "perm_made"))
                    maxed, exped, own = (sem(n, c) for n in ("maxed", "exped", "own"))
                    jobs = [(S, b) for b in range(NB)] + ([(SE, b) for b in range(NB)] if SE is not None else [])
                    n_in = len(jobs)
                    width = lambda b: P if b < NB - 1 else tail * H

                    @block.sync
                    def _(sp):
                        sp.wait_ge(cleared, 1)
                        for frm, to in ((key_dram, KT), (loc_dram["dst"], LT)):
                            rows = frm.rearrange("c (g e) -> (c g) e", g=2)
                            for h in range(H):
                                lead = slice(h, P, H)
                                if NB > 1:
                                    sp.dma_start(to[lead, 0:NB - 1, :], rows[0:(NB - 1) * TP, :].rearrange("(b t) e -> t b e", t=TP)
                                                 ).then_inc(keys_in, 16)
                                lead = slice(h, h + (tail - 1) * H + 1, H)
                                sp.dma_start(to[lead, NB - 1, :], rows[(NB - 1) * TP:TILES, :]).then_inc(keys_in, 16)
                        sp.wait_ge(packed, 1)
                        sp.dma_start(chunk_dram.rearrange("q h (b t) -> b q h t", t=TP), pack[:]).then_inc(sent, 16)
                        sp.wait_ge(sent, 16)
                        sp.dma_start(chunk[:], chunk_dram.rearrange("q h c -> h q c")).then_inc(chunk_in, 16)
                        sp.wait_ge(carry_made, 1)
                        sp.dma_start(carry_dram.rearrange("q h c -> h q c"), carry[:]).then_inc(carry_out, 16)
                        sp.wait_ge(carry_out, 16)
                        sp.dma_start(back[:], carry_dram.rearrange("q h (b t) -> b q h t", t=TP)).then_inc(carry_in, 16)

                    @block.vector
                    def _(dve):
                        v = nc.vector
                        step = serial(dve, own)
                        step(v.memset(LT[:], -1.0))
                        step(v.memset(ST[:], -BIG))
                        if SE is not None:
                            step(v.memset(ET[:], -BIG))
                        v.memset(KT[:], -5.0).then_inc(cleared, 1)
                        for i, (_, b) in enumerate(jobs):
                            w = width(b)
                            dve.wait_ge(turned, i + 1)
                            to = ST if i < NB else ET
                            v.tensor_copy(to[0:w, b, :], pT[0:w, i % PB, 0:P]).then_inc(freed, 1)
                        dve.wait_ge(freed, n_in)
                        dve.wait_ge(keys_in, 16 * 4 * H)
                        step(v.tensor_scalar(LT[:], LT[:], 0.0, -BIG, ALU.is_lt, ALU.mult))
                        if SE is not None:
                            step(v.tensor_tensor(t2[:], ST[:], ET[:], ALU.max))
                            step(v.tensor_tensor(t2[:], t2[:], LT[:], ALU.add))
                            held = t2
                        else:
                            step(v.tensor_tensor(ST[:], ST[:], LT[:], ALU.add))
                            held = ST
                        step(v.memset(t1[:, :, 0:1], 1.0))
                        step(v.tensor_tensor(t1[:, :, 1:P], KT[:, :, 1:P], KT[:, :, 0:P - 1], ALU.not_equal))
                        step(v.tensor_scalar(t1[:], t1[:], -BIG, None, ALU.mult))
                        step(v.tensor_tensor_scan(flat(fwd), flat(t1), flat(held), -BIG, ALU.add, ALU.max))
                        step(v.memset(t1[:, :, P - 1:P], 1.0))
                        step(v.tensor_tensor(t1[:, :, 0:P - 1], KT[:, :, 0:P - 1], KT[:, :, 1:P], ALU.not_equal))
                        step(v.tensor_scalar(t1[:], t1[:], -BIG, None, ALU.mult))
                        step(v.tensor_tensor_scan(flat(bwd)[:, ::-1], flat(t1)[:, ::-1], flat(held)[:, ::-1], -BIG, ALU.add, ALU.max))
                        step(v.tensor_copy(ends[:, 0, :], KT[:, :, 0]))
                        step(v.tensor_copy(ends[:, 1, :], KT[:, :, P - 1]))
                        step(v.tensor_copy(ends[:, 2, :], fwd[:, :, P - 1]))
                        step(v.tensor_copy(ends[:, 3, :], bwd[:, :, 0]))
                        dve.sem_inc(ends_made, 1)
                        for q in range(4):
                            dve.wait_ge(turned, n_in + q + 1)
                            step(v.tensor_copy(pack[:, q, :, :], pT[0:NB, q, 0:P].rearrange("p (t h) -> p h t", h=H)))
                        dve.sem_inc(packed, 1)
                        step(v.tensor_tensor(fwd[:], fwd[:], bwd[:], ALU.max))
                        step(v.tensor_tensor(bwd[:], KT[:], KT[:, :, 0:1].to_broadcast([P, NB, P]), ALU.not_equal))
                        step(v.tensor_scalar(bwd[:], bwd[:], -BIG, None, ALU.mult))
                        step(v.tensor_tensor(t1[:], KT[:], KT[:, :, P - 1:P].to_broadcast([P, NB, P]), ALU.not_equal))
                        step(v.tensor_scalar(t1[:], t1[:], -BIG, None, ALU.mult))
                        dve.wait_ge(chunk_in, 16)
                        K0, K1, LF, FB = (chunk[:, q, :] for q in range(4))
                        m = NCH - 1
                        step(v.memset(links[:], 1.0))
                        step(v.tensor_tensor(links[:, 0, 1:], K1[:, 1:], K1[:, 0:m], ALU.not_equal))
                        step(v.tensor_tensor(links[:, 1, 1:], K0[:, 1:], K1[:, 0:m], ALU.not_equal))
                        step(v.tensor_tensor(links[:, 2, 0:m], K0[:, 0:m], K0[:, 1:], ALU.not_equal))
                        step(v.tensor_tensor(links[:, 3, 0:m], K1[:, 0:m], K0[:, 1:], ALU.not_equal))
                        step(v.tensor_scalar(links[:], links[:], -BIG, None, ALU.mult))
                        step(v.tensor_tensor_scan(scans[:, 0, :], links[:, 0, :], LF, -BIG, ALU.add, ALU.max))
                        step(v.tensor_tensor_scan(scans[:, 1, ::-1], links[:, 2, ::-1], FB[:, ::-1], -BIG, ALU.add, ALU.max))
                        step(v.memset(carry[:], -BIG))
                        step(v.tensor_tensor(carry[:, 0, 1:], scans[:, 0, 0:m], links[:, 1, 1:], ALU.add))
                        step(v.tensor_tensor(carry[:, 1, 0:m], scans[:, 1, 1:], links[:, 3, 0:m], ALU.add))
                        dve.sem_inc(carry_made, 1)
                        dve.wait_ge(carry_in, 16)
                        for q in range(2):
                            step(v.tensor_copy(back_p[:, q, :].rearrange("p (t h) -> p h t", h=H), back[:, q, :, :]))
                        dve.sem_inc(perm_made, 1)
                        for q, near_run in ((0, bwd), (1, t1)):
                            dve.wait_ge(turned, n_in + 4 + q + 1)
                            step(v.tensor_tensor(near_run[:], near_run[:],
                                                 pT[:, q, 0:NB].unsqueeze(2).to_broadcast([P, NB, P]), ALU.add))
                            step(v.tensor_tensor(fwd[:], fwd[:], near_run[:], ALU.max))
                        if floor is not None:
                            step(v.tensor_scalar(fwd[:], fwd[:], floor, None, ALU.max))
                        step(v.tensor_tensor(ST[:], ST[:], fwd[:], ALU.subtract))
                        if SE is not None:
                            step(v.tensor_tensor(ET[:], ET[:], fwd[:], ALU.subtract))
                            step(v.tensor_scalar(ST[:], ST[:], 0.0, None, ALU.min))
                            step(v.tensor_scalar(ET[:], ET[:], 0.0, None, ALU.min))
                        dve.sem_inc(maxed, 1)
                        for i, (_, b) in enumerate(jobs):
                            w = width(b)
                            dve.wait_ge(turned, n_in + 6 + i + 1)
                            to = S if i < NB else SX
                            v.tensor_copy(to[:].rearrange("p t h -> p (t h)")[:, b * P:b * P + w], pT[:, i % PB, 0:w]).then_inc(freed, 1)

                    @block.scalar
                    def _(act):
                        act.wait_ge(maxed, 1)
                        nc.scalar.activation(ST[:], ST[:], ACT.Exp).then_inc(exped, 1)
                        if SE is not None:
                            nc.scalar.activation(ET[:], ET[:], ACT.Exp).then_inc(exped, 1)

                    @block.tensor
                    def _(pe):
                        for i, (frm, b) in enumerate(jobs):
                            w = width(b)
                            if i >= PB:
                                pe.wait_ge(freed, i - PB + 1)
                            nc.tensor.transpose(pT[0:w, i % PB, 0:P], frm[:].rearrange("p t h -> p (t h)")[:, b * P:b * P + w],
                                                ident[:]).then_inc(turned, 1)
                        pe.wait_ge(ends_made, 1)
                        pe.wait_ge(freed, n_in)
                        for q in range(4):
                            nc.tensor.transpose(pT[0:NB, q, 0:P], ends[:, q, :], ident[:]).then_inc(turned, 1)
                        pe.wait_ge(perm_made, 1)
                        for q in range(2):
                            nc.tensor.transpose(pT[:, q, 0:NB], back_p[:, q, :], ident[:NB, :NB]).then_inc(turned, 1)
                        pe.wait_ge(exped, 1 if SE is None else 2)
                        for i, (_, b) in enumerate(jobs):
                            w = width(b)
                            if i >= PB:
                                pe.wait_ge(freed, n_in + i - PB + 1)
                            frm = ST if i < NB else ET
                            nc.tensor.transpose(pT[:, i % PB, 0:w], frm[0:w, b, :], ident[:w, :w]).then_inc(turned, 1)

        def project(x_in, width, w, n_out, to, bias=None, relu=False):
            BT = 5
            STR = 1 << (n_out - 1).bit_length()
            with ExitStack() as c, nc.Block() as block:
                xs = sbuf("x_slot", [P, BT, width], ctx=c)
                xT = sbuf("xT", [width, BT, P], ctx=c)
                pT = psum("pT", [P, BT, P], c)
                pO = psum("pO", [P, BT, STR], c)
                slot, turned, copied, made, own = (sem(s, c) for s in ("slot", "turned", "copied", "made", "own"))
                begun = sem("begun", c)

                @block.vector
                def _(dve):
                    with dve.Fori(0, NT // BT) as i:
                        nc.vector.tensor_copy(xs[:], x_in[:, bass.ds(i * BT, BT), 0:width]).then_inc(slot, 1)
                        dve.wait_ge(turned, i + 1)
                        nc.vector.tensor_copy(xT[:], pT[0:width, :, :]).then_inc(copied, 1)
                        dve.wait_ge(made, i + 1)
                        o = to[:, bass.ds(i * BT, BT), 0:n_out]
                        if bias is None:
                            nc.vector.tensor_copy(o, pO[:, :, 0:n_out]).then_inc(own, 1)
                        else:
                            nc.vector.tensor_tensor(o, pO[:, :, 0:n_out],
                                                    bias[:].unsqueeze(1).to_broadcast([P, BT, n_out]), ALU.add).then_inc(own, 1)
                        dve.wait_ge(own, i + 1)
                    if relu:
                        nc.vector.tensor_scalar(to[:], to[:], 0.0, None, ALU.max).then_inc(own, 1)
                        dve.wait_ge(own, NT // BT + 1)

                @block.tensor
                def _(pe):
                    with pe.Fori(0, NT // BT) as i:
                        pe.wait_ge(slot, i + 1)
                        pe.sem_inc(begun, 1)
                        for t in range(BT):
                            ins = nc.tensor.transpose(pT[0:width, t, :], xs[:, t, :], ident[:])
                        ins.then_inc(turned, 1)
                        pe.wait_ge(copied, i + 1)
                        pe.wait_ge(own, i)
                        for t in range(BT):
                            ins = nc.tensor.matmul(pO[:, t, 0:n_out], xT[:, t, :], w[:], start=True, stop=True)
                        ins.then_inc(made, 1)

        def wide(v):
            return v.unsqueeze(2).to_broadcast([P, NT, D])

        def rowwise(v, m=D):
            return v.unsqueeze(1).to_broadcast([P, NT, m])

        def layernorm(step, X, sq, mean, var, affine=None):
            v = nc.vector
            step(v.tensor_reduce(mean[:], X[:], AX.X, ALU.add))
            step(v.tensor_scalar(mean[:], mean[:], 1.0 / D, None, ALU.mult))
            step(v.tensor_tensor(X[:], X[:], wide(mean[:]), ALU.subtract))
            step(v.tensor_tensor(sq[:], X[:], X[:], ALU.mult))
            step(v.tensor_reduce(var[:], sq[:], AX.X, ALU.add))
            step(v.tensor_scalar(var[:], var[:], 1.0 / D, EPS, ALU.mult, ALU.add))
            step.root()
            step(v.reciprocal(var[:], var[:]))
            step(v.tensor_tensor(X[:], X[:], wide(var[:]), ALU.mult))
            if affine is not None:
                step(v.tensor_tensor(X[:], X[:], rowwise(affine[0][:]), ALU.mult))
                step(v.tensor_tensor(X[:], X[:], rowwise(affine[1][:]), ALU.add))

        def node_math(body, norms=1):
            with ExitStack() as c, nc.Block() as block:
                sq = sbuf("node_sq", [P, NT, D], ctx=c)
                a, b = sbuf("node_a", [P, NT], ctx=c), sbuf("node_b", [P, NT], ctx=c)
                own, var_ready, root_ready = sem("own", c), sem("var_ready", c), sem("root_ready", c)

                @block.vector
                def _(dve):
                    step = serial(dve, own)
                    asked = [0]

                    def root():
                        asked[0] += 1
                        dve.sem_inc(var_ready, 1)
                        dve.wait_ge(root_ready, asked[0])
                    step.root = root
                    body(step, sq, a, b)

                @block.scalar
                def _(act):
                    for i in range(norms):
                        act.wait_ge(var_ready, i + 1)
                        nc.scalar.activation(b[:], b[:], ACT.Sqrt).then_inc(root_ready, 1)

        def store(pairs):
            with ExitStack() as c, nc.Block() as block:
                kept = [sem("kept", c) for _ in pairs]

                @block.sync
                def _(sp):
                    for (to, frm), s in zip(pairs, kept):
                        sp.dma_start(to, frm).then_inc(s, 16)
                    for s in kept:
                        sp.wait_ge(s, 16)

        def load_weights(X, pairs):
            with ExitStack() as c, nc.Block() as block:
                s = sem("weights_in", c)

                @block.sync
                def _(sp):
                    sp.dma_start(X[:], x.rearrange("(t p) d -> p t d", p=P)).then_inc(s, 16)
                    for to, frm in pairs:
                        sp.dma_start(to[:], frm).then_inc(s, 16)
                    sp.wait_ge(s, 16 * (len(pairs) + 1))

        nodes_dram = {k: dram(f"nodes_{k}", [NPAD, w]) for k, w in (("x3", D), ("y2", D), ("kv", 2 * D), ("xl", D))}
        kept_rows = dram("kept_rows", [P, TILES * D])
        dma_rows = lambda t, a, b: t[:, :, a:b]

        X = sbuf("X", [P, NT, D])
        acc = sbuf("acc", [P, NT, D + HEADS])
        deg = sbuf("deg", [P, NT])

        def bc(v):
            return v.to_broadcast([P, v.shape[1]])
        wq_s, bq_s = sbuf("wqkv_s", [D, 3 * D]), sbuf("bqkv_s", [P, 3 * D])
        weT_s, be_s, lt_s = sbuf("weT_s", [DE, HEADS]), sbuf("be_s", [P, HEADS]), sbuf("lt_s", [P, HEADS])
        wo_s, bo_s, ga_s, bt_s = sbuf("wo_s", [D, D]), sbuf("bo_s", [P, D]), sbuf("ga_s", [P, D]), sbuf("bt_s", [P, D])
        wlr_s, att_s, bias2_s = sbuf("wlr_s", [D, 2 * D]), sbuf("att_s", [P, D]), sbuf("bias2_s", [P, D])
        w1_s, b1_s, w2_s, b2_s = sbuf("w1_s", [D, HID]), sbuf("b1_s", [P, HID]), sbuf("w2_s", [HID, D]), sbuf("b2_s", [P, D])

        setup()
        load_weights(X, [(wq_s, wqkv), (bq_s, bc(bqkv)), (weT_s, weT), (be_s, bc(be)), (lt_s, bc(log_temp)), (wo_s, woT),
                         (bo_s, bc(bo)), (ga_s, bc(gamma)), (bt_s, bc(beta)), (wlr_s, wlr), (att_s, bc(att)),
                         (bias2_s, bc(bias2)), (w1_s, w1), (b1_s, bc(b1)), (w2_s, w2), (b2_s, bc(b2))])
        rank_and_scatter()
        prepare("dst")
        prepare("src")

        aggregate("src", acc, D + 1, table=x, weights=w_src[:].unsqueeze(2))

        def layer0(step, sq, a, b):
            step(nc.vector.tensor_scalar(deg[:], acc[:, :, D], 1.0, None, ALU.max))
            step(nc.vector.reciprocal(deg[:], deg[:]))
            step(nc.vector.tensor_tensor(X[:], X[:], acc[:, :, 0:D], ALU.add))
            layernorm(step, X, sq, a, b)
        node_math(layer0)

        node_view = lambda k: nodes_dram[k].rearrange("(t p) d -> p t d", p=P)
        with ExitStack() as c:
            S = sbuf("S", [P, TILES, HEADS], ctx=c)
            with ExitStack() as c1:
                qkv = sbuf("qkv", [P, NT, 3 * D], ctx=c1)
                project(X, D, wq_s, 3 * D, qkv, bias=bq_s)
                store([(node_view("kv"), qkv[:, :, D:3 * D])])

                def attention(step, picked, rows, a, b, bias, at):
                    v = nc.vector
                    step(v.tensor_tensor(a, picked, rows[:, :, 0:D], ALU.mult))
                    step(v.tensor_reduce(b[:, :, 0:HEADS], a.rearrange("p t (h d) -> p t h d", h=HEADS), AX.X, ALU.add))
                    step(v.scalar_tensor_tensor(S[:, bass.ds(at, TB), :], b[:, :, 0:HEADS], DH ** -0.5,
                                                bias.rearrange("p (t h) -> p t h", h=HEADS), ALU.mult, ALU.add))
                attention.steps = 3
                edge_scores(S, nodes_dram["kv"], 2 * D, D, qkv, D, attention, ef=True)

            with ExitStack() as b_, nc.Block() as block:
                own, temp = sem("own", b_), sem("temp", b_)

                @block.scalar
                def _(act):
                    nc.scalar.activation(lt_s[:], lt_s[:], ACT.Exp).then_inc(temp, 1)

                @block.vector
                def _(dve):
                    step = serial(dve, own)
                    heads = lambda t: t[:].unsqueeze(1).to_broadcast([P, TILES, HEADS])
                    step(nc.vector.tensor_tensor(S[:], S[:], heads(be_s), ALU.add))
                    dve.wait_ge(temp, 1)
                    step(nc.vector.tensor_tensor(S[:], S[:], heads(lt_s), ALU.mult))
            softmax_exp(S, HEADS, floor=-1.0e9)
            aggregate("dst", acc, D + HEADS, stream=kept_rows, weights=S, extra=S)
        with ExitStack() as c:
            O = sbuf("O", [P, NT, D], ctx=c)
            den = sbuf("den", [P, NT, HEADS], ctx=c)

            def attended(step, sq, a, b):
                v = nc.vector
                step(v.tensor_scalar(den[:], acc[:, :, D:D + HEADS], 1e-10, None, ALU.add))
                step(v.reciprocal(den[:], den[:]))
                for h in range(HEADS):
                    part_h = slice(h * DH, (h + 1) * DH)
                    step(v.tensor_tensor(O[:, :, part_h], acc[:, :, part_h], den[:, :, h:h + 1].to_broadcast([P, NT, DH]), ALU.mult))
            node_math(attended, norms=0)
            Z = sbuf("Z", [P, NT, D], ctx=c)
            project(O, D, wo_s, D, Z, bias=bo_s)

            def layer1(step, sq, a, b):
                v = nc.vector
                step(v.tensor_tensor(Z[:], Z[:], X[:], ALU.add))
                layernorm(step, Z, sq, a, b, affine=(ga_s, bt_s))
                step(v.tensor_tensor(X[:], X[:], Z[:], ALU.add))
                layernorm(step, X, sq, a, b)
            node_math(layer1, norms=2)

        with ExitStack() as c:
            near = sbuf("xr_self", [P, NT, D + 1], ctx=c)
            xl = sbuf("xl", [P, NT, D], ctx=c)
            S = sbuf("S2", [P, TILES, 1], ctx=c)
            SE = sbuf("SE", [P, TILES, 1], ctx=c)
            with ExitStack() as c1:
                lr = sbuf("lr", [P, NT, 2 * D], ctx=c1)
                project(X, D, wlr_s, 2 * D, lr)

                def own_scores(step, sq, a, b):
                    v = nc.vector
                    step(v.tensor_copy(xl[:], lr[:, :, 0:D]))
                    step(v.tensor_copy(near[:, :, 0:D], lr[:, :, D:2 * D]))
                    step(v.tensor_tensor(sq[:], lr[:, :, 0:D], lr[:, :, D:2 * D], ALU.add))
                    step(v.scalar_tensor_tensor(sq[:], sq[:], 0.2, sq[:], ALU.mult, ALU.max))
                    step(v.tensor_tensor(sq[:], sq[:], rowwise(att_s[:]), ALU.mult))
                    step(v.tensor_reduce(near[:, :, D], sq[:], AX.X, ALU.add))
                node_math(own_scores, norms=0)
                store([(node_view("xl"), xl[:])])

            def gat(step, picked, rows, a, b, bias, at):
                v = nc.vector
                step(v.tensor_tensor(a, picked[:, :, 0:D], rows, ALU.add))
                step(v.scalar_tensor_tensor(b, a, 0.2, a, ALU.mult, ALU.max))
                step(v.tensor_tensor(a, b, att_s[:].unsqueeze(1).to_broadcast([P, TB, D]), ALU.mult))
                step(v.tensor_reduce(S[:, bass.ds(at, TB), 0], a, AX.X, ALU.add))
                step(v.tensor_copy(SE[:, bass.ds(at, TB), 0], picked[:, :, D]))
            gat.steps = 5
            edge_scores(S, nodes_dram["xl"], D, 0, near, D + 1, gat)
            SX = sbuf("SX", [P, TILES, 2], ctx=c)
            softmax_exp(S, 1, SE=SE, SX=SE)
            with ExitStack() as b_, nc.Block() as block:
                own = sem("own", b_)

                @block.vector
                def _(dve):
                    step = serial(dve, own)
                    step(nc.vector.tensor_copy(SX[:, :, 0:1], S[:]))
                    step(nc.vector.tensor_copy(SX[:, :, 1:2], SE[:]))
            aggregate("dst", acc, D + 3, stream=kept_rows, weights=S, extra=SX)
            own_w = sbuf("own_w", [P, NT], ctx=c)

            def layer2(step, sq, a, b):
                v = nc.vector
                step(v.tensor_scalar(a[:], acc[:, :, D + 2], 1.0, None, ALU.max))
                step(v.reciprocal(a[:], a[:]))
                step(v.tensor_tensor(own_w[:], acc[:, :, D + 1], a[:], ALU.mult))
                step(v.tensor_scalar(a[:], acc[:, :, D + 2], 0.0, None, ALU.is_equal))
                step(v.tensor_tensor(own_w[:], own_w[:], a[:], ALU.add))
                step(v.tensor_tensor(b[:], acc[:, :, D], own_w[:], ALU.add))
                step(v.reciprocal(b[:], b[:]))
                step(v.tensor_tensor(sq[:], xl[:], wide(own_w[:]), ALU.mult))
                step(v.tensor_tensor(sq[:], sq[:], acc[:, :, 0:D], ALU.add))
                step(v.tensor_tensor(sq[:], sq[:], wide(b[:]), ALU.mult))
                step(v.tensor_tensor(sq[:], sq[:], rowwise(bias2_s[:]), ALU.add))
                step(v.tensor_tensor(X[:], X[:], sq[:], ALU.add))
                layernorm(step, X, sq, a, b)
            node_math(layer2)

        node_table = lambda k: nodes_dram[k].rearrange("(t p) d -> p t d", p=P)
        store([(node_table("x3"), X[:])])
        aggregate("src", acc, D, table=nodes_dram["x3"])
        with ExitStack() as c:
            Y = sbuf("Y", [P, NT, D], ctx=c)
            Hd = sbuf("H", [P, NT, HID], ctx=c)

            def mean3(step, sq, a, b):
                step(nc.vector.tensor_tensor(Y[:], acc[:, :, 0:D], wide(deg[:]), ALU.mult))
                step(nc.vector.tensor_tensor(Y[:], Y[:], X[:], ALU.add))
            node_math(mean3, norms=0)
            project(Y, D, w1_s, HID, Hd, bias=b1_s, relu=True)
            project(Hd, HID, w2_s, D, Y)
            store([(node_table("y2"), Y[:])])
            aggregate("src", acc, D, table=nodes_dram["y2"])

            def last3(step, sq, a, b):
                step(nc.vector.tensor_tensor(sq[:], acc[:, :, 0:D], wide(deg[:]), ALU.mult))
                step(nc.vector.tensor_tensor(Y[:], Y[:], sq[:], ALU.add))
                step(nc.vector.tensor_tensor(Y[:], Y[:], rowwise(b2_s[:]), ALU.add))
                step(nc.vector.tensor_tensor(X[:], X[:], Y[:], ALU.add))
                layernorm(step, X, sq, a, b)
            node_math(last3)
        full = NODES // P
        store([(out[0:full * P, :].rearrange("(t p) d -> p t d", p=P), X[:, 0:full, :]),
               (out[full * P:NODES, :], X[0:NODES - full * P, full, :])])


def layout(inp):
    import numpy as np
    a = {k: np.ascontiguousarray(v) for k, v in inp.items()}

    def padded(v, n, fill):
        o = np.full((n,) + v.shape[1:], fill, v.dtype)
        o[:v.shape[0]] = v
        return o
    g1, g2, g3 = "L1_gnn_", "L2_gnn_", "L3_gnn_"
    row = lambda v: np.ascontiguousarray(v.reshape(1, -1))
    return {
        "x_in": padded(a["x"], NPAD, 0),
        "src_in": padded(a["src"], EPAD, NPAD - 1),
        "dst_in": padded(a["dst"], EPAD, NPAD - 1),
        "weight_in": padded(a["edge_weight"], EPAD, 0),
        "efT_in": np.ascontiguousarray(padded(a["edge_attr_32"], EPAD, 0).T),
        "wqkv_in": np.ascontiguousarray(np.concatenate([a[g1 + "Wq"].T, a[g1 + "Wk"].T, a[g1 + "Wv"].T], 1)),
        "bqkv_in": row(np.concatenate([a[g1 + "bq"], a[g1 + "bk"], a[g1 + "bv"]])),
        "weT_in": np.ascontiguousarray(a[g1 + "We"].T),
        "be_in": row(a[g1 + "be"]),
        "woT_in": np.ascontiguousarray(a[g1 + "Wo"].T),
        "bo_in": row(a[g1 + "bo"]),
        "gamma_in": row(a[g1 + "ln_gamma"]),
        "beta_in": row(a[g1 + "ln_beta"]),
        "log_temp_in": row(a[g1 + "log_temp"]),
        "wlr_in": np.ascontiguousarray(np.concatenate([a[g2 + "W_l"], a[g2 + "W_r"]], 1)),
        "att_in": row(a[g2 + "att"]),
        "bias2_in": row(a[g2 + "bias"]),
        "w1_in": a[g3 + "W1"],
        "b1_in": row(a[g3 + "b1"]),
        "w2_in": a[g3 + "W2"],
        "b2_in": row(a[g3 + "b2"]),
    }


def kernel(**inputs):
    import numpy as np
    import concourse.bacc as bacc
    from concourse.bass_utils import run_bass_kernel_spmd as run
    nc = bacc.Bacc("TRN2", target_bir_lowering=False, num_devices=1)
    arrays = layout(inputs)
    args = [nc.dram_tensor(n, a.shape, mybir.dt.from_np(a.dtype), kind="ExternalInput").ap() for n, a in arrays.items()]
    out = nc.dram_tensor("out", (NODES, D), F32, kind="ExternalOutput").ap()
    gnn(nc, *args, out)
    r = run(nc, [arrays], core_ids=[0])
    return r.results[0]["out"]
```

```python
import concourse.bass as bass
from concourse import mybir
from contextlib import ExitStack

F32 = mybir.dt.float32
I32 = mybir.dt.int32
ALU = mybir.AluOpType
ACT = mybir.ActivationFunctionType
AX = mybir.AxisListType

NODES, EDGES, D, DE, HEADS, HID = 3125, 100000, 64, 32, 4, 128
DH = D // HEADS
P = 128
NT = -(-NODES // P)
NPAD = NT * P
GROUP = 2 * P
GROUPS = -(-EDGES // GROUP)
EPAD = GROUPS * GROUP
CHUNK = EPAD // P
BODY = 4
TB = 2 * BODY
CELLS = -(-(GROUPS + NT - 1) // (2 * BODY)) * 2 * BODY
STEPS = CELLS // BODY
TILES = 2 * CELLS
CB = -(-CELLS // P)
REC = 4
NS = 4
MSG = D + 4
NOWHERE = float(1 << 18)
BIG = 1.0e30
EPS = 1e-5


def serial(eng, sem, base=0):
    n = [0]

    def step(ins):
        n[0] += 1
        ins.then_inc(sem, 1)
        eng.wait_ge(sem, base + n[0])
    return step


def gnn(nc, x, src, dst, weight, efT, wqkv, bqkv, weT, be, woT, bo, gamma, beta, log_temp,
        wlr, att, bias2, w1, b1, w2, b2, out):
    top = ExitStack()
    with top:
        used = {}

        def fresh(name):
            used[name] = used.get(name, 0) + 1
            return f"{name}_{used[name]}"

        def sbuf(name, shape, dt=F32, ctx=top):
            return ctx.enter_context(nc.sbuf_tensor(fresh(name), shape, dt))

        def psum(name, shape, ctx):
            return ctx.enter_context(nc.psum_tensor(fresh(name), shape, F32))

        live = {}

        def sem(name, ctx):
            if id(ctx) not in live:
                live[id(ctx)] = []

                def release():
                    nc.clear_and_free_semaphores(live.pop(id(ctx)))
                    nc.all_engine_barrier()
                ctx.callback(release)
            live[id(ctx)].append(nc.alloc_semaphore(fresh(name)))
            return live[id(ctx)][-1]

        def dram(name, shape, dt=F32):
            return nc.dram_tensor(name, shape, dt, kind="Internal").ap()

        rec_dram = dram("rec_by_dst", [EPAD, REC])
        msg_dram = dram("msg_by_src", [EPAD, MSG])
        loc_dram = dram("loc_by_cell", [CELLS, GROUP])
        key_dram = dram("clamped_dst", [CELLS, GROUP])
        k_dram = {o: dram(f"k_{o}", [CB * P], I32) for o in ("dst", "src")}
        n_dram = {o: dram(f"n_{o}", [CB * P], I32) for o in ("dst", "src")}

        ident = sbuf("ident", [P, P])
        ones = sbuf("ones", [P, P])
        before = sbuf("before", [P, P])
        lane = sbuf("lane", [P, P])
        part = sbuf("part", [P, 1])
        gather_id = {o: sbuf(f"gather_id_{o}", [P, TILES + NS * TB]) for o in ("dst", "src")}
        loc = {o: sbuf(f"loc_sb_{o}", [P, TILES]) for o in ("dst", "src")}
        k_i = sbuf("k_i", [P, CB], I32)
        k_f = sbuf("k_f", [P, CB])
        n_f = sbuf("n_f", [P, CB])
        n_all = sbuf("n_all", [P, CELLS])
        n_row = {o: sbuf(f"n_row_{o}", [1, BODY + CELLS], I32) for o in ("dst", "src")}
        k_row = {o: sbuf(f"k_row_{o}", [1, CELLS], I32) for o in ("dst", "src")}

        def setup():
            with ExitStack() as c, nc.Block() as block:
                made, done = sem("iota_made", c), sem("consts", c)

                @block.gpsimd
                def _(pool):
                    nc.gpsimd.iota(lane[:], [[1, P]], base=0, channel_multiplier=0,
                                   allow_small_or_imprecise_dtypes=True).then_inc(made, 1)
                    nc.gpsimd.iota(part[:], [[1, 1]], base=0, channel_multiplier=1,
                                   allow_small_or_imprecise_dtypes=True).then_inc(made, 1)

                @block.vector
                def _(dve):
                    nc.vector.memset(ones[:], 1.0)
                    for o in ("dst", "src"):
                        nc.vector.memset(n_row[o][:, 0:BODY], 0)
                        nc.vector.memset(gather_id[o][:, TILES:], 0.0)
                    dve.wait_ge(made, 2)
                    nc.vector.tensor_scalar(ident[:], lane[:], part[:], None, ALU.is_equal)
                    nc.vector.tensor_scalar(before[:], lane[:], part[:], None, ALU.is_gt).then_inc(done, 1)

        def rank():
            with ExitStack() as r:
                rec = sbuf("rec", [P, CHUNK, REC], ctx=r)
                s_i = sbuf("src_i", [P, CHUNK], I32, ctx=r)
                d_i = sbuf("dst_i", [P, CHUNK], I32, ctx=r)
                w_f = sbuf("w_f", [P, CHUNK], ctx=r)
                tile = sbuf("src_tile", [P, CHUNK], ctx=r)
                hit = sbuf("hit", [P, CHUNK], ctx=r)
                run = sbuf("run", [P, CHUNK], ctx=r)
                place = sbuf("place", [P, CHUNK], ctx=r)
                count = sbuf("count", [P, NT], ctx=r)
                total = sbuf("total", [P, NT], ctx=r)
                upto = sbuf("upto", [P, NT], ctx=r)
                base = sbuf("base", [P, NT], ctx=r)
                ahead = psum("ahead", [P, 512], r)
                with nc.Block() as block:
                    loaded = [sem(f"loaded{i}", r) for i in range(3)]
                    filled, stored = sem("rec_filled", r), sem("rec_stored", r)
                    ew, counted, summed = sem("exp_w", r), sem("counted", r), sem("summed", r)
                    own, own_l, own_p = sem("dve_own", r), sem("dve_count", r), sem("dve_place", r)

                    @block.sync
                    def _(sp):
                        for i, (to, frm) in enumerate(((s_i, src), (d_i, dst), (w_f, weight))):
                            sp.dma_start(to[:], frm.rearrange("(p j) -> p j", p=P)).then_inc(loaded[i], 16)
                        sp.wait_ge(filled, 1)
                        sp.wait_ge(ew, 1)
                        sp.dma_start(rec_dram.rearrange("(p j) r -> p (j r)", p=P),
                                     rec[:].rearrange("p j r -> p (j r)")).then_inc(stored, 16)
                        sp.wait_ge(stored, 16)

                    @block.scalar
                    def _(act):
                        act.wait_ge(loaded[2], 16)
                        nc.scalar.activation(rec[:, :, 2], w_f[:], ACT.Exp, scale=-1.0).then_inc(ew, 1)

                    @block.vector
                    def _(dve):
                        step = serial(dve, own)
                        step(nc.vector.memset(place[:], 0.0))
                        dve.wait_ge(loaded[0], 16)
                        step(nc.vector.tensor_copy(rec[:, :, 0], s_i[:]))
                        dve.wait_ge(loaded[1], 16)
                        step(nc.vector.tensor_copy(rec[:, :, 1], d_i[:]))
                        step(nc.vector.tensor_single_scalar(s_i[:], s_i[:], 7, op=ALU.arith_shift_right))
                        step(nc.vector.tensor_copy(tile[:], s_i[:]))
                        with dve.Fori(0, NT) as v:
                            s = serial(dve, own_l, v * 2)
                            s(nc.vector.tensor_scalar(hit[:], tile[:], lane[:, bass.ds(v, 1)], None, ALU.is_equal))
                            s(nc.vector.tensor_reduce(count[:, bass.ds(v, 1)], hit[:], AX.X, ALU.add))
                        dve.sem_inc(counted, 1)
                        dve.wait_ge(summed, 1)
                        step(nc.vector.tensor_copy(total[:], ahead[:, 64:64 + NT]))
                        step(nc.vector.tensor_tensor_scan(upto[:], total[:], total[:], 0.0, ALU.add, ALU.max))
                        step(nc.vector.tensor_tensor(upto[:], upto[:], total[:], ALU.subtract))
                        step(nc.vector.scalar_tensor_tensor(base[:], upto[:], -1.0, ahead[:, 0:NT], ALU.add, ALU.add))
                        with dve.Fori(0, NT) as v:
                            s = serial(dve, own_p, v * 4)
                            s(nc.vector.tensor_scalar(hit[:], tile[:], lane[:, bass.ds(v, 1)], None, ALU.is_equal))
                            s(nc.vector.tensor_tensor_scan(run[:], ones[:, 0:1].to_broadcast([P, CHUNK]), hit[:], base[:, bass.ds(v, 1)], ALU.mult, ALU.add))
                            s(nc.vector.tensor_tensor(hit[:], hit[:], run[:], ALU.mult))
                            s(nc.vector.tensor_tensor(place[:], place[:], hit[:], ALU.add))
                        nc.vector.tensor_copy(rec[:, :, 3], place[:]).then_inc(filled, 1)

                    @block.tensor
                    def _(pe):
                        pe.wait_ge(counted, 1)
                        nc.tensor.matmul(ahead[:, 0:NT], before[:], count[:], start=True, stop=True)
                        nc.tensor.matmul(ahead[:, 64:64 + NT], ones[:], count[:], start=True,
                                         stop=True).then_inc(summed, 1)

        def staircase(order, keys):
            with ExitStack() as c, nc.Block() as block:
                last = sbuf("last_key", [P, CB], ctx=c)
                last_i = sbuf("last_i", [P, CB], I32, ctx=c)
                diag = sbuf("diag", [P, CB, P], ctx=c)
                ends = sbuf("ends", [P, CB * P], ctx=c)
                kk = sbuf("kk", [P, CB * P], ctx=c)
                less = sbuf("less", [P, CB * P], ctx=c)
                cell = sbuf("cell", [P, CB], ctx=c)
                n_c = sbuf("n_c", [P, CB], ctx=c)
                n_i = sbuf("n_i", [P, CB], I32, ctx=c)
                n_r = sbuf("n_r", [1, CELLS], ctx=c)
                pB = psum("ends_all", [P, CB * P], c)
                pN = psum("n_all", [P, CB * P], c)
                loaded, iotas, own = sem("last_loaded", c), sem("iotas", c), sem("own", c)
                cleared = sem("last_cleared", c)
                diag_made, spread = sem("diag_made", c), sem("spread", c)
                k_made, row_made, n_spread = sem("k_made", c), sem("row_made", c), sem("n_spread", c)
                put, back = [sem(f"put{i}", c) for i in range(2)], sem("back", c)
                full = GROUPS // P
                rest = GROUPS - full * P

                @block.sync
                def _(sp):
                    sp.wait_ge(cleared, 1)
                    with nc.allow_non_contiguous_dma(reason="one key of each group"):
                        for b in range(CB):
                            m = P if b < full else rest
                            sp.dma_start(last[:m, b:b + 1], keys[b * P:b * P + m, :]).then_inc(loaded, 16)
                    sp.wait_ge(k_made, 1)
                    with nc.allow_non_contiguous_dma(reason="one word of each cell"):
                        sp.dma_start(k_dram[order].rearrange("(b p) -> p b", p=P), k_i[:]).then_inc(put[0], 16)
                        sp.dma_start(n_dram[order].rearrange("(b p) -> p b", p=P), n_i[:]).then_inc(put[1], 16)
                    sp.wait_ge(put[0], 16)
                    sp.wait_ge(put[1], 16)
                    sp.dma_start(k_row[order][:], k_dram[order][0:CELLS].rearrange("(a k) -> a k", a=1)).then_inc(back, 16)
                    sp.dma_start(n_row[order][:, BODY:], n_dram[order][0:CELLS].rearrange("(a k) -> a k", a=1)).then_inc(back, 16)
                    sp.wait_ge(back, 32)

                @block.gpsimd
                def _(pool):
                    nc.gpsimd.iota(kk[:], [[1, CB * P]], base=0, channel_multiplier=0,
                                   allow_small_or_imprecise_dtypes=True).then_inc(iotas, 1)
                    nc.gpsimd.iota(cell[:], [[P, CB]], base=0, channel_multiplier=1,
                                   allow_small_or_imprecise_dtypes=True).then_inc(iotas, 1)

                @block.vector
                def _(dve):
                    step = serial(dve, own)
                    nc.vector.memset(last[:], 0.0).then_inc(cleared, 1)
                    dve.wait_ge(loaded, 16 * CB)
                    step(nc.vector.tensor_copy(last_i[:], last[:]))
                    step(nc.vector.tensor_single_scalar(last_i[:], last_i[:], 7, op=ALU.arith_shift_right))
                    step(nc.vector.tensor_copy(last[:], last_i[:]))
                    for b in range(CB):
                        ins = nc.vector.tensor_scalar(diag[:, b, :], ident[:], last[:, b:b + 1], None, ALU.mult)
                    ins.then_inc(diag_made, 1)
                    dve.wait_ge(iotas, 2)
                    dve.wait_ge(spread, 1)
                    step(nc.vector.tensor_tensor(ends[:], pB[:], kk[:], ALU.add))
                    step(nc.vector.memset(ends[:, GROUPS:], 1.0e6))
                    for b in range(CB):
                        step(nc.vector.tensor_scalar(less[:], ends[:], cell[:, b:b + 1], None, ALU.is_lt))
                        step(nc.vector.tensor_reduce(k_f[:, b:b + 1], less[:], AX.X, ALU.add))
                    step(nc.vector.tensor_scalar(k_f[:], k_f[:], float(GROUPS - 1), None, ALU.min))
                    step(nc.vector.tensor_tensor(n_f[:], cell[:], k_f[:], ALU.subtract))
                    step(nc.vector.tensor_scalar(n_c[:], n_f[:], float(NT - 1), None, ALU.min))
                    step(nc.vector.tensor_copy(n_i[:], n_c[:]))
                    step(nc.vector.tensor_copy(k_i[:], k_f[:]))
                    step(nc.vector.tensor_scalar(n_f[:], n_f[:], float(P), None, ALU.mult))
                    for b in range(CB):
                        ins = nc.vector.tensor_scalar(diag[:, b, :], ident[:], n_f[:, b:b + 1], None, ALU.mult)
                    ins.then_inc(k_made, 1)
                    dve.wait_ge(n_spread, 1)
                    step(nc.vector.tensor_copy(n_all[:], pN[:, 0:CELLS]))

                @block.tensor
                def _(pe):
                    pe.wait_ge(diag_made, 1)
                    nc.tensor.matmul(pB[:], ones[:], diag[:].rearrange("p b q -> p (b q)"), start=True,
                                     stop=True).then_inc(spread, 1)
                    pe.wait_ge(k_made, 1)
                    nc.tensor.matmul(pN[:], ones[:], diag[:].rearrange("p b q -> p (b q)"), start=True,
                                     stop=True).then_inc(n_spread, 1)

        def rows_by_cell():
            with ExitStack() as c, nc.Block() as block:
                R = sbuf("cell_recs", [P, CB, GROUP, REC], ctx=c)
                L = sbuf("cell_loc", [P, CB, GROUP], ctx=c)
                K = sbuf("cell_key", [P, CB, GROUP], ctx=c)
                V = sbuf("cell_valid", [P, CB, GROUP], ctx=c)
                pT = [psum(f"turned{i}", [P, 512], c) for i in range(4)]
                got = [sem(f"got{b}", c) for b in range(CB)]
                rows_made, turned, freed, own = sem("rows_made", c), sem("turned", c), sem("freed", c), sem("own", c)
                put = [sem(f"put{i}", c) for i in range(2)]
                rows_in = [min(P, CELLS - b * P) for b in range(CB)]
                turns = [(b, g, q) for b in range(CB) for g in range(2) for q in range(5)]

                @block.sync
                def _(sp):
                    sp.wait_ge(rows_made, 1)
                    for b in range(CB):
                        m = rows_in[b]
                        sp.dma_start(loc_dram[b * P:b * P + m, :], L[:m, b, :]).then_inc(put[0], 16)
                        sp.dma_start(key_dram[b * P:b * P + m, :], K[:m, b, :]).then_inc(put[1], 16)
                    sp.wait_ge(put[0], 16 * CB)
                    sp.wait_ge(put[1], 16 * CB)

                @block.gpsimd
                def _(pool):
                    view = rec_dram.rearrange("(k e) r -> k (e r)", e=GROUP)
                    for b in range(CB):
                        m = rows_in[b]
                        pool.indirect_dma_start(
                            out=R[:m, b, :, :].rearrange("p e r -> p (e r)"), out_offset=None, in_=view,
                            in_offset=bass.IndirectOffsetOnAxis(ap=k_i[:m, b:b + 1], axis=0)).then_inc(got[b], 16)

                @block.vector
                def _(dve):
                    v = nc.vector
                    step = serial(dve, own)
                    for b in range(CB):
                        m = rows_in[b]
                        dve.wait_ge(got[b], 16)
                        Lb, Kb, Vb, Rp = L[:m, b, :], K[:m, b, :], V[:m, b, :], R[:m, b, :, 3]
                        step(v.tensor_scalar(Lb, R[:m, b, :, 1], n_f[:m, b:b + 1], None, ALU.subtract))
                        step(v.tensor_scalar(Kb, Lb, 0.0, float(P - 1), ALU.max, ALU.min))
                        step(v.tensor_tensor(Vb, Lb, Kb, ALU.is_equal))
                        step(v.scalar_tensor_tensor(Lb, Lb, 1.0, Vb, ALU.add, ALU.mult))
                        step(v.tensor_scalar(Lb, Lb, -1.0, None, ALU.add))
                        step(v.tensor_scalar(Kb, Kb, n_f[:m, b:b + 1], None, ALU.add))
                        step(v.scalar_tensor_tensor(Rp, Rp, -NOWHERE, Vb, ALU.add, ALU.mult))
                        step(v.tensor_scalar(Rp, Rp, NOWHERE, None, ALU.add))
                    dve.sem_inc(rows_made, 1)
                    for i, (b, g, q) in enumerate(turns):
                        m = rows_in[b]
                        dve.wait_ge(turned, i + 1)
                        to = (gather_id["dst"][:, 0:TILES], loc["dst"][:], w_dst[:], place_dst[:], ends_dst[:, :, 1])[q]
                        to = to.rearrange("p (c g) -> p c g", g=2)[:, b * P:b * P + m, g]
                        v.tensor_copy(to, pT[i % 4][:, 0:m]).then_inc(freed, 1)
                    dve.wait_ge(freed, len(turns))
                    step(v.tensor_copy(ends_dst[:, :, 0], gather_id["dst"][:, 0:TILES]))

                @block.tensor
                def _(pe):
                    pe.wait_ge(rows_made, 1)
                    for i, (b, g, q) in enumerate(turns):
                        m = rows_in[b]
                        half = slice(g * P, (g + 1) * P)
                        if i >= 4:
                            pe.wait_ge(freed, i - 3)
                        frm = (R[:m, b, half, 0], L[:m, b, half], R[:m, b, half, 2], R[:m, b, half, 3], K[:m, b, half])[q]
                        nc.tensor.transpose(pT[i % 4][:, 0:m], frm, ident[:m, :m]).then_inc(turned, 1)

        def messages():
            with ExitStack() as c, nc.Block() as block:
                rows = sbuf("message", [P, NS, TB, MSG], ctx=c)
                ids = sbuf("place_slot", [P, NS, TB], I32, ctx=c)
                loc_all = sbuf("loc_all", [P, NS, TB * P], ctx=c)
                hotT = sbuf("hotT", [P, NS, TB, P], ctx=c)
                picked = psum("picked", [P, NS, TB, D], c)
                ring = lambda name: [sem(f"{name}{s}", c) for s in range(NS)]
                loc_in, hot_made, products, filled, beside, sent = map(
                    ring, ("loc_in", "hot_made", "products", "filled", "beside", "sent"))
                taken, cleared = sem("taken", c), sem("cleared", c)
                loc_flat = loc_dram.rearrange("(a c) e -> a (c e)", a=1)

                @block.sync
                def _(sp):
                    with sp.Fori(0, STEPS // NS) as i:
                        for s in range(NS):
                            sp.wait_ge(hot_made[s], i + 1)
                            sp.dma_start(loc_all[:, s, :], loc_flat[:, bass.ds((i * NS + s) * (TB * P), TB * P)]
                                         .to_broadcast([P, TB * P])).then_inc(loc_in[s], 16)

                @block.vector
                def _(dve):
                    for s in range(NS):
                        dve.sem_inc(hot_made[s], 1)
                        dve.sem_inc(filled[s], 1)
                    nc.vector.memset(rows[:, :, :, D:D + 1], 1.0).then_inc(cleared, 1)
                    nc.vector.memset(rows[:, :, :, D + 3:MSG], 0.0).then_inc(cleared, 1)
                    dve.wait_ge(cleared, 2)

                    def fill(i, s):
                        at = (i * NS + s) * TB
                        dve.wait_ge(products[s], i + 2)
                        dve.wait_ge(beside[s], i * 2 + 2)
                        nc.vector.tensor_tensor(rows[:, s, :, 0:D], picked[:, s, :, :],
                                                w_dst[:, bass.ds(at, TB)].unsqueeze(2).to_broadcast([P, TB, D]),
                                                ALU.mult).then_inc(filled[s], 1)
                    with dve.Fori(0, STEPS // NS) as i:
                        for s in range(NS):
                            dve.wait_ge(loc_in[s], i * 16 + 16)
                            dve.wait_ge(products[s], i + 1)
                            nc.vector.tensor_scalar(hotT[:, s, :, :].rearrange("p t e -> p (t e)"), loc_all[:, s, :],
                                                    part[:], None, ALU.is_equal).then_inc(hot_made[s], 1)
                            if s > 0:
                                fill(i, s - 1)
                        fill(i, NS - 1)

                @block.tensor
                def _(pe):
                    for s in range(NS):
                        pe.sem_inc(products[s], 1)
                    with pe.Fori(0, STEPS // NS) as i:
                        for s in range(NS):
                            pe.wait_ge(hot_made[s], i + 2)
                            pe.wait_ge(filled[s], i + 1)
                            for q in range(BODY):
                                n = pe.value_load(n_row["dst"][0:1, bass.ds((i * NS + s) * BODY + (BODY + q), 1)], min_val=0, max_val=NT - 1)
                                for g in range(2):
                                    ins = nc.tensor.matmul(picked[:, s, 2 * q + g, :], hotT[:, s, 2 * q + g, :],
                                                           X[:, bass.ds(n, 1), :].rearrange("p a c -> p (a c)"),
                                                           start=True, stop=True)
                            ins.then_inc(products[s], 1)

                @block.scalar
                def _(act):
                    def body(i):
                        for s in range(NS):
                            at = (i * NS + s) * TB
                            if not (isinstance(i, int) and i == 0):
                                act.wait_ge(sent[s], i * (16 * TB))
                            nc.scalar.copy(ids[:, s, :], place_dst[:, bass.ds(at, TB)]).then_inc(beside[s], 1)
                            nc.scalar.copy(rows[:, s, :, D + 1:D + 3], ends_dst[:, bass.ds(at, TB), :]).then_inc(beside[s], 1)
                    body(0)
                    with act.Fori(1, STEPS // NS) as i:
                        body(i)

                @block.gpsimd
                def _(pool):
                    with pool.Fori(0, STEPS // NS) as i:
                        for s in range(NS):
                            pool.wait_ge(beside[s], i * 2 + 2)
                            pool.wait_ge(filled[s], i + 2)
                            pool.sem_inc(taken, 1)
                            for t in range(TB):
                                pool.indirect_dma_start(
                                    out=msg_dram, out_offset=bass.IndirectOffsetOnAxis(ap=ids[:, s, t:t + 1], axis=0),
                                    in_=rows[:, s, t, :], in_offset=None, bounds_check=EPAD - 1,
                                    oob_is_err=False).then_inc(sent[s], 16)
                    for s in range(NS):
                        pool.wait_ge(sent[s], (STEPS // NS) * (16 * TB))

        def aggregate(order, acc, cols, table=None, stream=None, weights=None, extra=None):
            by_group = table is None and stream is None
            with ExitStack() as c, nc.Block() as block:
                rows = sbuf("rows", [P, NS, TB, MSG if by_group else D], ctx=c)
                ids = sbuf("id_slot", [P, NS, TB], I32, ctx=c)
                hot = sbuf("hot", [P, NS, TB, P], ctx=c)
                mixed = sbuf("mixed", [P, NS, TB, cols], ctx=c) if weights is not None else rows
                part_sum = psum("part_sum", [P, NS, BODY, P], c)
                ring = lambda name: [sem(f"{name}{s}", c) for s in range(NS)]
                ids_made, arrived, hot_made, mixed_made, beside, summed = map(
                    ring, ("ids_made", "arrived", "hot_made", "mixed_made", "beside", "summed"))
                added = ring("added")
                cleared, taken, own, own_add = (sem(n, c) for n in ("cleared", "taken", "own", "own_add"))
                accs = sbuf("accs", [P, BODY, NT, cols], ctx=c)
                PER = 16 * TB if table is not None else 16 * BODY if by_group else 16
                n_extra = 0 if extra is None else extra.shape[2]
                LOOPS = STEPS // NS

                if table is not None:
                    @block.gpsimd
                    def _(pool):
                        with pool.Fori(0, LOOPS) as i:
                            for s in range(NS):
                                pool.wait_ge(ids_made[s], i + 1)
                                pool.sem_inc(taken, 1)
                                for t in range(TB):
                                    pool.indirect_dma_start(
                                        out=rows[:, s, t, :], out_offset=None, in_=table,
                                        in_offset=bass.IndirectOffsetOnAxis(ap=ids[:, s, t:t + 1], axis=0)
                                    ).then_inc(arrived[s], 16)

                    @block.scalar
                    def _(act):
                        with act.Fori(0, LOOPS) as i:
                            for s in range(NS):
                                at = (i * NS + s) * TB
                                act.wait_ge(summed[s], i + 1)
                                nc.scalar.copy(ids[:, s, :], gather_id[order][:, bass.ds(at, TB)]).then_inc(ids_made[s], 1)
                elif by_group:
                    @block.sync
                    def _(sp):
                        groups = msg_dram.rearrange("(k g p) r -> p (k g) r", g=2, p=P)
                        with sp.Fori(0, LOOPS) as i:
                            for s in range(NS):
                                sp.wait_ge(summed[s], i + 1)
                                for q in range(BODY):
                                    k = sp.value_load(k_row[order][0:1, bass.ds((i * NS + s) * BODY + q, 1)], min_val=0, max_val=GROUPS - 1)
                                    sp.dma_start(rows[:, s, 2 * q:2 * q + 2, :], groups[:, bass.ds(k * 2, 2), :]).then_inc(arrived[s], 16)
                else:
                    @block.sync
                    def _(sp):
                        with sp.Fori(0, LOOPS) as i:
                            for s in range(NS):
                                sp.wait_ge(mixed_made[s], i + 1)
                                at = (i * NS + s) * (TB * D)
                                sp.dma_start(rows[:, s, :, :].rearrange("p t d -> p (t d)"),
                                             stream[:, bass.ds(at, TB * D)]).then_inc(arrived[s], 16)

                    @block.gpsimd
                    def _(pool):
                        for s in range(NS):
                            pool.sem_inc(mixed_made[s], 1)
                        with pool.Fori(0, LOOPS) as i:
                            for s in range(NS):
                                pool.wait_ge(arrived[s], i * PER + PER)
                                pool.wait_ge(summed[s], i + 1)
                                wt = weights[:, bass.ds((i * NS + s) * TB, TB), :]
                                k = wt.shape[2]
                                nc.gpsimd.tensor_tensor(
                                    mixed[:, s, :, 0:D].rearrange("p t (k d) -> p t k d", k=k),
                                    rows[:, s, :, :].rearrange("p t (k d) -> p t k d", k=k),
                                    wt.unsqueeze(3).to_broadcast([P, TB, k, D // k]), ALU.mult).then_inc(mixed_made[s], 1)

                    @block.scalar
                    def _(act):
                        with act.Fori(0, LOOPS) as i:
                            for s in range(NS):
                                at = (i * NS + s) * TB
                                act.wait_ge(summed[s], i + 1)
                                nc.scalar.copy(mixed[:, s, :, D:D + n_extra],
                                               extra[:, bass.ds(at, TB), :]).then_inc(beside[s], 1)

                @block.vector
                def _(dve):
                    nc.vector.memset(accs[:], 0.0).then_inc(cleared, 1)
                    nc.vector.memset(part_sum[:, NS - 1, :, :], 0.0).then_inc(cleared, 1)
                    if not by_group and cols > D + n_extra:
                        nc.vector.memset(mixed[:, :, :, D + n_extra:cols], 1.0).then_inc(cleared, 1)
                        dve.wait_ge(cleared, 3)
                    dve.wait_ge(cleared, 2)
                    for s in range(NS - 1):
                        dve.sem_inc(added[s], 1)

                    def add(j, s, uses):
                        ns = [dve.value_load(n_row[order][0:1, bass.ds(j * BODY + b, 1)], min_val=0, max_val=NT - 1)
                              for b in range(BODY)]
                        dve.wait_ge(summed[s], uses)
                        for b in range(BODY):
                            to = accs[:, b, bass.ds(ns[b], 1), :].rearrange("p a c -> p (a c)")
                            nc.vector.tensor_tensor(to, to, part_sum[:, s, b, 0:cols], ALU.add).then_inc(own_add, 1)

                    def body(i):
                        step = serial(dve, own, i * NS)
                        for s in range(NS):
                            at = (i * NS + s) * TB
                            dve.wait_ge(summed[s], i + 1)
                            if by_group:
                                dve.wait_ge(arrived[s], i * PER + PER)
                                cells = n_all[:, bass.ds((i * NS + s) * BODY, BODY)].unsqueeze(2).to_broadcast([P, BODY, 2])
                                nc.vector.tensor_copy(gather_id[order][:, bass.ds(at, TB)], rows[:, s, :, D + 2])
                                step(nc.vector.tensor_tensor(
                                    loc[order][:, bass.ds(at, TB)].rearrange("p (b g) -> p b g", g=2),
                                    rows[:, s, :, D + 1].rearrange("p (b g) -> p b g", g=2), cells, ALU.subtract))
                            nc.vector.tensor_tensor(hot[:, s, :, :], lane[:].unsqueeze(1).to_broadcast([P, TB, P]),
                                                    loc[order][:, bass.ds(at, TB)].unsqueeze(2).to_broadcast([P, TB, P]),
                                                    ALU.is_equal).then_inc(hot_made[s], 1)
                            add(i * NS + s, (s - 1) % NS, i + 1 if s == 0 else i + 2)
                            dve.wait_ge(own_add, (i * NS + s + 1) * BODY)
                            dve.sem_inc(added[(s - 1) % NS], 1)
                    with dve.Fori(0, LOOPS) as i:
                        body(i)
                    add(LOOPS * NS, NS - 1, LOOPS + 1)
                    dve.wait_ge(own_add, (LOOPS * NS + 1) * BODY)
                    last = serial(dve, cleared, 2 if by_group or cols <= D + n_extra else 3)
                    last(nc.vector.tensor_tensor(accs[:, 0, :, :], accs[:, 0, :, :], accs[:, 1, :, :], ALU.add))
                    last(nc.vector.tensor_tensor(accs[:, 2, :, :], accs[:, 2, :, :], accs[:, 3, :, :], ALU.add))
                    last(nc.vector.tensor_tensor(acc[:, :, 0:cols], accs[:, 0, :, :], accs[:, 2, :, :], ALU.add))

                @block.tensor
                def _(pe):
                    for s in range(NS):
                        pe.sem_inc(summed[s], 1)
                    with pe.Fori(0, LOOPS) as i:
                        for s in range(NS):
                            pe.wait_ge(hot_made[s], i + 1)
                            pe.wait_ge(arrived[s], i * PER + PER)
                            if weights is not None:
                                pe.wait_ge(mixed_made[s], i + 2)
                                pe.wait_ge(beside[s], i + 1)
                            pe.wait_ge(added[s], i + 1)
                            for t in range(TB):
                                ins = nc.tensor.matmul(part_sum[:, s, t // 2, 0:cols], hot[:, s, t, :],
                                                       mixed[:, s, t, 0:cols], start=t % 2 == 0, stop=t % 2 == 1)
                            ins.then_inc(summed[s], 1)

        def edge_scores(table, width, kept_from, near, near_cols, finish, ef=False):
            with ExitStack() as c, nc.Block() as block:
                rows = sbuf("rows", [P, NS, TB, width], ctx=c)
                ids = sbuf("id_slot", [P, NS, TB], I32, ctx=c)
                loc_all = sbuf("loc_all", [P, NS, TB * P], ctx=c)
                hotT = sbuf("hotT", [P, NS, TB, P], ctx=c)
                a = sbuf("score_a", [P, TB, D], ctx=c)
                b = sbuf("score_b", [P, TB, D], ctx=c)
                efs = sbuf("ef_slot", [DE, NS, BODY, GROUP], ctx=c) if ef else None
                NP = 2
                picked = psum("picked", [P, NP, TB, near_cols if near_cols <= D else 2 * D], c)
                bias = psum("ef_bias", [P, NP, 512], c) if ef else None
                ring = lambda name, n=NS: [sem(f"{name}{s}", c) for s in range(n)]
                ids_made, arrived, loc_in, ef_in, hot_made, products, kept = map(
                    ring, ("ids_made", "arrived", "loc_in", "ef_in", "hot_made", "products", "kept"))
                scored = ring("scored", NP)
                taken, own = sem("taken", c), sem("own", c)
                loc_flat = loc_dram.rearrange("(a c) e -> a (c e)", a=1)
                LOOPS = STEPS // NS
                USES = NS // NP

                @block.gpsimd
                def _(pool):
                    with pool.Fori(0, LOOPS) as i:
                        for s in range(NS):
                            pool.wait_ge(ids_made[s], i + 1)
                            pool.sem_inc(taken, 1)
                            for t in range(TB):
                                pool.indirect_dma_start(
                                    out=rows[:, s, t, :], out_offset=None, in_=table,
                                    in_offset=bass.IndirectOffsetOnAxis(ap=ids[:, s, t:t + 1], axis=0)
                                ).then_inc(arrived[s], 16)

                @block.sync
                def _(sp):
                    with sp.Fori(0, LOOPS) as i:
                        for s in range(NS):
                            j = i * NS + s
                            sp.wait_ge(hot_made[s], i + 1)
                            sp.dma_start(loc_all[:, s, :], loc_flat[:, bass.ds(j * (TB * P), TB * P)].to_broadcast([P, TB * P])
                                         ).then_inc(loc_in[s], 16)
                            if ef:
                                sp.wait_ge(products[s], i + 1)
                                for q in range(BODY):
                                    k = sp.value_load(k_row["dst"][0:1, bass.ds(j * BODY + q, 1)], min_val=0, max_val=GROUPS - 1)
                                    sp.dma_start(efs[:, s, q, :], efT[:, bass.ds(k * GROUP, GROUP)]).then_inc(ef_in[s], 16)

                @block.scalar
                def _(act):
                    with act.Fori(0, LOOPS) as i:
                        for s in range(NS):
                            at = (i * NS + s) * TB
                            act.wait_ge(arrived[s], i * (16 * TB) + 16 * TB)
                            act.dma_start(kept_rows[:, bass.ds(at * D, TB * D)].rearrange("p (t d) -> p t d", t=TB),
                                          rows[:, s, :, kept_from:kept_from + D]).then_inc(kept[s], 16)

                @block.vector
                def _(dve):
                    for s in range(NS):
                        dve.sem_inc(hot_made[s], 1)
                        nc.vector.tensor_copy(ids[:, s, :], gather_id["dst"][:, s * TB:(s + 1) * TB]).then_inc(ids_made[s], 1)
                    for s in range(NP):
                        dve.sem_inc(scored[s], 1)
                    with dve.Fori(0, LOOPS) as i:
                        step = serial(dve, own, i * (NS * finish.steps))

                        def score(s):
                            dve.wait_ge(arrived[s], i * (16 * TB) + 16 * TB)
                            dve.wait_ge(products[s], i + 2)
                            finish(step, picked[:, s % NP, :, :], rows[:, s, :, :], a[:], b[:],
                                   bias[:, s % NP, 0:TB * HEADS] if ef else None, (i * NS + s) * TB)
                            dve.sem_inc(scored[s % NP], 1)

                        def release(s):
                            dve.wait_ge(kept[s], i * 16 + 16)
                            nc.vector.tensor_copy(ids[:, s, :], gather_id["dst"][:, bass.ds((i * NS + (s + NS)) * TB, TB)]
                                                  ).then_inc(ids_made[s], 1)
                        for s in range(NS):
                            dve.wait_ge(loc_in[s], i * 16 + 16)
                            dve.wait_ge(products[s], i + 1)
                            nc.vector.tensor_scalar(hotT[:, s, :, :].rearrange("p t e -> p (t e)"), loc_all[:, s, :],
                                                    part[:], None, ALU.is_equal).then_inc(hot_made[s], 1)
                            if s > 0:
                                score(s - 1)
                            if s > 1:
                                release(s - 2)
                        score(NS - 1)
                        release(NS - 2)
                        release(NS - 1)

                @block.tensor
                def _(pe):
                    for s in range(NS):
                        pe.sem_inc(products[s], 1)
                    with pe.Fori(0, LOOPS) as i:
                        for s in range(NS):
                            pe.wait_ge(hot_made[s], i + 2)
                            pe.wait_ge(scored[s % NP], i * USES + s // NP + 1)
                            if ef:
                                pe.wait_ge(ef_in[s], i * (16 * BODY) + 16 * BODY)
                            for q in range(BODY):
                                n = pe.value_load(n_row["dst"][0:1, bass.ds((i * NS + s) * BODY + (BODY + q), 1)], min_val=0, max_val=NT - 1)
                                for g in range(2):
                                    t = 2 * q + g
                                    ins = nc.tensor.matmul(picked[:, s % NP, t, 0:near_cols], hotT[:, s, t, :],
                                                           near[:, bass.ds(n, 1), 0:near_cols].rearrange("p a c -> p (a c)"),
                                                           start=True, stop=True)
                                    if ef:
                                        ins = nc.tensor.matmul(bias[:, s % NP, t * HEADS:(t + 1) * HEADS],
                                                               efs[:, s, q, g * P:(g + 1) * P], weT_s[:],
                                                               start=True, stop=True)
                            ins.then_inc(products[s], 1)

        def softmax_exp(S, H, SE=None, SX=None, floor=None):
            NB = -(-TILES * H // P)
            W = NB * P
            TP = P // H
            NCH = NB * TP
            tail = TILES - (NB - 1) * TP
            with ExitStack() as c:
                def big(name):
                    return sbuf(name, [P, NB, P], ctx=c)
                ST, KT, LT, fwd, bwd, t1, t2 = (big(n) for n in ("ST", "KT", "LT", "fwd", "bwd", "t1", "t2"))
                ET = big("ET") if SE is not None else None
                ends = sbuf("chunk_ends", [P, 4, NB], ctx=c)
                pack = sbuf("pack", [NB, 4, H, TP], ctx=c)
                chunk = sbuf("chunk", [H, 4, NCH], ctx=c)
                links = sbuf("links", [H, 4, NCH], ctx=c)
                scans = sbuf("scans", [H, 2, NCH], ctx=c)
                carry = sbuf("carry", [H, 2, NCH], ctx=c)
                back = sbuf("carry_back", [NB, 2, H, TP], ctx=c)
                back_p = sbuf("carry_perm", [NB, 2, P], ctx=c)
                chunk_dram = dram(f"chunk_dram{H}", [4, H, NCH])
                carry_dram = dram(f"carry_dram{H}", [2, H, NCH])
                flat = lambda t: t[:].rearrange("p b e -> p (b e)")
                with nc.Block() as block:
                    PB = 4
                    pT = psum("pT", [P, PB, 512], c)
                    cleared, keys_in, turned, freed = (sem(n, c) for n in ("cleared", "keys_in", "turned", "freed"))
                    ends_made, packed, sent, chunk_in = (sem(n, c) for n in ("ends_made", "packed", "sent", "chunk_in"))
                    carry_made, carry_out, carry_in, perm_made = (sem(n, c) for n in ("carry_made", "carry_out", "carry_in", "perm_made"))
                    maxed, exped, own = (sem(n, c) for n in ("maxed", "exped", "own"))
                    jobs = [(S, b) for b in range(NB)] + ([(SE, b) for b in range(NB)] if SE is not None else [])
                    n_in = len(jobs)
                    width = lambda b: P if b < NB - 1 else tail * H

                    @block.sync
                    def _(sp):
                        sp.wait_ge(cleared, 1)
                        for frm, to in ((key_dram, KT), (loc_dram, LT)):
                            rows = frm.rearrange("c (g e) -> (c g) e", g=2)
                            for h in range(H):
                                lead = slice(h, P, H)
                                if NB > 1:
                                    sp.dma_start(to[lead, 0:NB - 1, :], rows[0:(NB - 1) * TP, :].rearrange("(b t) e -> t b e", t=TP)
                                                 ).then_inc(keys_in, 16)
                                lead = slice(h, h + (tail - 1) * H + 1, H)
                                sp.dma_start(to[lead, NB - 1, :], rows[(NB - 1) * TP:TILES, :]).then_inc(keys_in, 16)
                        sp.wait_ge(packed, 1)
                        sp.dma_start(chunk_dram.rearrange("q h (b t) -> b q h t", t=TP), pack[:]).then_inc(sent, 16)
                        sp.wait_ge(sent, 16)
                        sp.dma_start(chunk[:], chunk_dram.rearrange("q h c -> h q c")).then_inc(chunk_in, 16)
                        sp.wait_ge(carry_made, 1)
                        sp.dma_start(carry_dram.rearrange("q h c -> h q c"), carry[:]).then_inc(carry_out, 16)
                        sp.wait_ge(carry_out, 16)
                        sp.dma_start(back[:], carry_dram.rearrange("q h (b t) -> b q h t", t=TP)).then_inc(carry_in, 16)

                    @block.vector
                    def _(dve):
                        v = nc.vector
                        step = serial(dve, own)
                        step(v.memset(LT[:], -1.0))
                        step(v.memset(ST[:], -BIG))
                        if SE is not None:
                            step(v.memset(ET[:], -BIG))
                        v.memset(KT[:], -5.0).then_inc(cleared, 1)
                        for i, (_, b) in enumerate(jobs):
                            w = width(b)
                            dve.wait_ge(turned, i + 1)
                            to = ST if i < NB else ET
                            v.tensor_copy(to[0:w, b, :], pT[0:w, i % PB, 0:P]).then_inc(freed, 1)
                        dve.wait_ge(freed, n_in)
                        dve.wait_ge(keys_in, 16 * 4 * H)
                        step(v.tensor_scalar(LT[:], LT[:], 0.0, -BIG, ALU.is_lt, ALU.mult))
                        if SE is not None:
                            step(v.tensor_tensor(t2[:], ST[:], ET[:], ALU.max))
                            step(v.tensor_tensor(t2[:], t2[:], LT[:], ALU.add))
                            held = t2
                        else:
                            step(v.tensor_tensor(ST[:], ST[:], LT[:], ALU.add))
                            held = ST
                        step(v.memset(t1[:, :, 0:1], 1.0))
                        step(v.tensor_tensor(t1[:, :, 1:P], KT[:, :, 1:P], KT[:, :, 0:P - 1], ALU.not_equal))
                        step(v.tensor_scalar(t1[:], t1[:], -BIG, None, ALU.mult))
                        step(v.tensor_tensor_scan(flat(fwd), flat(t1), flat(held), -BIG, ALU.add, ALU.max))
                        step(v.memset(t1[:, :, P - 1:P], 1.0))
                        step(v.tensor_tensor(t1[:, :, 0:P - 1], KT[:, :, 0:P - 1], KT[:, :, 1:P], ALU.not_equal))
                        step(v.tensor_scalar(t1[:], t1[:], -BIG, None, ALU.mult))
                        step(v.tensor_tensor_scan(flat(bwd)[:, ::-1], flat(t1)[:, ::-1], flat(held)[:, ::-1], -BIG, ALU.add, ALU.max))
                        step(v.tensor_copy(ends[:, 0, :], KT[:, :, 0]))
                        step(v.tensor_copy(ends[:, 1, :], KT[:, :, P - 1]))
                        step(v.tensor_copy(ends[:, 2, :], fwd[:, :, P - 1]))
                        step(v.tensor_copy(ends[:, 3, :], bwd[:, :, 0]))
                        dve.sem_inc(ends_made, 1)
                        for q in range(4):
                            dve.wait_ge(turned, n_in + q + 1)
                            step(v.tensor_copy(pack[:, q, :, :], pT[0:NB, q, 0:P].rearrange("p (t h) -> p h t", h=H)))
                        dve.sem_inc(packed, 1)
                        step(v.tensor_tensor(fwd[:], fwd[:], bwd[:], ALU.max))
                        step(v.tensor_tensor(bwd[:], KT[:], KT[:, :, 0:1].to_broadcast([P, NB, P]), ALU.not_equal))
                        step(v.tensor_scalar(bwd[:], bwd[:], -BIG, None, ALU.mult))
                        step(v.tensor_tensor(t1[:], KT[:], KT[:, :, P - 1:P].to_broadcast([P, NB, P]), ALU.not_equal))
                        step(v.tensor_scalar(t1[:], t1[:], -BIG, None, ALU.mult))
                        dve.wait_ge(chunk_in, 16)
                        K0, K1, LF, FB = (chunk[:, q, :] for q in range(4))
                        m = NCH - 1
                        step(v.memset(links[:], 1.0))
                        step(v.tensor_tensor(links[:, 0, 1:], K1[:, 1:], K1[:, 0:m], ALU.not_equal))
                        step(v.tensor_tensor(links[:, 1, 1:], K0[:, 1:], K1[:, 0:m], ALU.not_equal))
                        step(v.tensor_tensor(links[:, 2, 0:m], K0[:, 0:m], K0[:, 1:], ALU.not_equal))
                        step(v.tensor_tensor(links[:, 3, 0:m], K1[:, 0:m], K0[:, 1:], ALU.not_equal))
                        step(v.tensor_scalar(links[:], links[:], -BIG, None, ALU.mult))
                        step(v.tensor_tensor_scan(scans[:, 0, :], links[:, 0, :], LF, -BIG, ALU.add, ALU.max))
                        step(v.tensor_tensor_scan(scans[:, 1, ::-1], links[:, 2, ::-1], FB[:, ::-1], -BIG, ALU.add, ALU.max))
                        step(v.memset(carry[:], -BIG))
                        step(v.tensor_tensor(carry[:, 0, 1:], scans[:, 0, 0:m], links[:, 1, 1:], ALU.add))
                        step(v.tensor_tensor(carry[:, 1, 0:m], scans[:, 1, 1:], links[:, 3, 0:m], ALU.add))
                        dve.sem_inc(carry_made, 1)
                        dve.wait_ge(carry_in, 16)
                        for q in range(2):
                            step(v.tensor_copy(back_p[:, q, :].rearrange("p (t h) -> p h t", h=H), back[:, q, :, :]))
                        dve.sem_inc(perm_made, 1)
                        for q, near_run in ((0, bwd), (1, t1)):
                            dve.wait_ge(turned, n_in + 4 + q + 1)
                            step(v.tensor_tensor(near_run[:], near_run[:],
                                                 pT[:, q, 0:NB].unsqueeze(2).to_broadcast([P, NB, P]), ALU.add))
                            step(v.tensor_tensor(fwd[:], fwd[:], near_run[:], ALU.max))
                        if floor is not None:
                            step(v.tensor_scalar(fwd[:], fwd[:], floor, None, ALU.max))
                        step(v.tensor_tensor(ST[:], ST[:], fwd[:], ALU.subtract))
                        if SE is not None:
                            step(v.tensor_tensor(ET[:], ET[:], fwd[:], ALU.subtract))
                            step(v.tensor_scalar(ST[:], ST[:], 0.0, None, ALU.min))
                            step(v.tensor_scalar(ET[:], ET[:], 0.0, None, ALU.min))
                        dve.sem_inc(maxed, 1)
                        for i, (_, b) in enumerate(jobs):
                            w = width(b)
                            dve.wait_ge(turned, n_in + 6 + i + 1)
                            to = S if i < NB else SX
                            v.tensor_copy(to[:].rearrange("p t h -> p (t h)")[:, b * P:b * P + w], pT[:, i % PB, 0:w]).then_inc(freed, 1)

                    @block.scalar
                    def _(act):
                        act.wait_ge(maxed, 1)
                        nc.scalar.activation(ST[:], ST[:], ACT.Exp).then_inc(exped, 1)
                        if SE is not None:
                            nc.scalar.activation(ET[:], ET[:], ACT.Exp).then_inc(exped, 1)

                    @block.tensor
                    def _(pe):
                        for i, (frm, b) in enumerate(jobs):
                            w = width(b)
                            if i >= PB:
                                pe.wait_ge(freed, i - PB + 1)
                            nc.tensor.transpose(pT[0:w, i % PB, 0:P], frm[:].rearrange("p t h -> p (t h)")[:, b * P:b * P + w],
                                                ident[:]).then_inc(turned, 1)
                        pe.wait_ge(ends_made, 1)
                        pe.wait_ge(freed, n_in)
                        for q in range(4):
                            nc.tensor.transpose(pT[0:NB, q, 0:P], ends[:, q, :], ident[:]).then_inc(turned, 1)
                        pe.wait_ge(perm_made, 1)
                        for q in range(2):
                            nc.tensor.transpose(pT[:, q, 0:NB], back_p[:, q, :], ident[:NB, :NB]).then_inc(turned, 1)
                        pe.wait_ge(exped, 1 if SE is None else 2)
                        for i, (_, b) in enumerate(jobs):
                            w = width(b)
                            if i >= PB:
                                pe.wait_ge(freed, n_in + i - PB + 1)
                            frm = ST if i < NB else ET
                            nc.tensor.transpose(pT[:, i % PB, 0:w], frm[0:w, b, :], ident[:w, :w]).then_inc(turned, 1)

        def project(x_in, width, w, n_out, to, bias=None, relu=False):
            BT = 5
            STR = 1 << (n_out - 1).bit_length()
            with ExitStack() as c, nc.Block() as block:
                xs = sbuf("x_slot", [P, BT, width], ctx=c)
                xT = sbuf("xT", [width, BT, P], ctx=c)
                pT = psum("pT", [P, BT, P], c)
                pO = psum("pO", [P, BT, STR], c)
                slot, turned, copied, made, own = (sem(s, c) for s in ("slot", "turned", "copied", "made", "own"))
                begun = sem("begun", c)

                @block.vector
                def _(dve):
                    with dve.Fori(0, NT // BT) as i:
                        nc.vector.tensor_copy(xs[:], x_in[:, bass.ds(i * BT, BT), 0:width]).then_inc(slot, 1)
                        dve.wait_ge(turned, i + 1)
                        nc.vector.tensor_copy(xT[:], pT[0:width, :, :]).then_inc(copied, 1)
                        dve.wait_ge(made, i + 1)
                        o = to[:, bass.ds(i * BT, BT), 0:n_out]
                        if bias is None:
                            nc.vector.tensor_copy(o, pO[:, :, 0:n_out]).then_inc(own, 1)
                        else:
                            nc.vector.tensor_tensor(o, pO[:, :, 0:n_out],
                                                    bias[:].unsqueeze(1).to_broadcast([P, BT, n_out]), ALU.add).then_inc(own, 1)
                        dve.wait_ge(own, i + 1)
                    if relu:
                        nc.vector.tensor_scalar(to[:], to[:], 0.0, None, ALU.max).then_inc(own, 1)
                        dve.wait_ge(own, NT // BT + 1)

                @block.tensor
                def _(pe):
                    with pe.Fori(0, NT // BT) as i:
                        pe.wait_ge(slot, i + 1)
                        pe.sem_inc(begun, 1)
                        for t in range(BT):
                            ins = nc.tensor.transpose(pT[0:width, t, :], xs[:, t, :], ident[:])
                        ins.then_inc(turned, 1)
                        pe.wait_ge(copied, i + 1)
                        pe.wait_ge(own, i)
                        for t in range(BT):
                            ins = nc.tensor.matmul(pO[:, t, 0:n_out], xT[:, t, :], w[:], start=True, stop=True)
                        ins.then_inc(made, 1)

        def wide(v):
            return v.unsqueeze(2).to_broadcast([P, NT, D])

        def rowwise(v, m=D):
            return v.unsqueeze(1).to_broadcast([P, NT, m])

        def layernorm(step, X, sq, mean, var, affine=None):
            v = nc.vector
            step(v.tensor_reduce(mean[:], X[:], AX.X, ALU.add))
            step(v.tensor_scalar(mean[:], mean[:], 1.0 / D, None, ALU.mult))
            step(v.tensor_tensor(X[:], X[:], wide(mean[:]), ALU.subtract))
            step(v.tensor_tensor(sq[:], X[:], X[:], ALU.mult))
            step(v.tensor_reduce(var[:], sq[:], AX.X, ALU.add))
            step(v.tensor_scalar(var[:], var[:], 1.0 / D, EPS, ALU.mult, ALU.add))
            step.root()
            step(v.reciprocal(var[:], var[:]))
            step(v.tensor_tensor(X[:], X[:], wide(var[:]), ALU.mult))
            if affine is not None:
                step(v.tensor_tensor(X[:], X[:], rowwise(affine[0][:]), ALU.mult))
                step(v.tensor_tensor(X[:], X[:], rowwise(affine[1][:]), ALU.add))

        def node_math(body, norms=1):
            with ExitStack() as c, nc.Block() as block:
                sq = sbuf("node_sq", [P, NT, D], ctx=c)
                a, b = sbuf("node_a", [P, NT], ctx=c), sbuf("node_b", [P, NT], ctx=c)
                own, var_ready, root_ready = sem("own", c), sem("var_ready", c), sem("root_ready", c)

                @block.vector
                def _(dve):
                    step = serial(dve, own)
                    asked = [0]

                    def root():
                        asked[0] += 1
                        dve.sem_inc(var_ready, 1)
                        dve.wait_ge(root_ready, asked[0])
                    step.root = root
                    body(step, sq, a, b)

                @block.scalar
                def _(act):
                    for i in range(norms):
                        act.wait_ge(var_ready, i + 1)
                        nc.scalar.activation(b[:], b[:], ACT.Sqrt).then_inc(root_ready, 1)

        def store(pairs):
            with ExitStack() as c, nc.Block() as block:
                kept = [sem("kept", c) for _ in pairs]

                @block.sync
                def _(sp):
                    for (to, frm), s in zip(pairs, kept):
                        sp.dma_start(to, frm).then_inc(s, 16)
                    for s in kept:
                        sp.wait_ge(s, 16)

        def load_weights(X, pairs):
            with ExitStack() as c, nc.Block() as block:
                s = sem("weights_in", c)

                @block.sync
                def _(sp):
                    sp.dma_start(X[:], x.rearrange("(t p) d -> p t d", p=P)).then_inc(s, 16)
                    for to, frm in pairs:
                        sp.dma_start(to[:], frm).then_inc(s, 16)
                    sp.wait_ge(s, 16 * (len(pairs) + 1))

        nodes_dram = {k: dram(f"nodes_{k}", [NPAD, w]) for k, w in (("x3", D), ("y2", D), ("kv", 2 * D), ("xl", D))}
        kept_rows = dram("kept_rows", [P, TILES * D])
        dma_rows = lambda t, a, b: t[:, :, a:b]

        X = sbuf("X", [P, NT, D])
        acc = sbuf("acc", [P, NT, D + HEADS])
        deg = sbuf("deg", [P, NT])

        def bc(v):
            return v.to_broadcast([P, v.shape[1]])
        wq_s, bq_s = sbuf("wqkv_s", [D, 3 * D]), sbuf("bqkv_s", [P, 3 * D])
        weT_s, be_s, lt_s = sbuf("weT_s", [DE, HEADS]), sbuf("be_s", [P, HEADS]), sbuf("lt_s", [P, HEADS])
        wo_s, bo_s, ga_s, bt_s = sbuf("wo_s", [D, D]), sbuf("bo_s", [P, D]), sbuf("ga_s", [P, D]), sbuf("bt_s", [P, D])
        wlr_s, att_s, bias2_s = sbuf("wlr_s", [D, 2 * D]), sbuf("att_s", [P, D]), sbuf("bias2_s", [P, D])
        w1_s, b1_s, w2_s, b2_s = sbuf("w1_s", [D, HID]), sbuf("b1_s", [P, HID]), sbuf("w2_s", [HID, D]), sbuf("b2_s", [P, D])

        setup()
        load_weights(X, [(wq_s, wqkv), (bq_s, bc(bqkv)), (weT_s, weT), (be_s, bc(be)), (lt_s, bc(log_temp)), (wo_s, woT),
                         (bo_s, bc(bo)), (ga_s, bc(gamma)), (bt_s, bc(beta)), (wlr_s, wlr), (att_s, bc(att)),
                         (bias2_s, bc(bias2)), (w1_s, w1), (b1_s, bc(b1)), (w2_s, w2), (b2_s, bc(b2))])
        rank()
        staircase("dst", rec_dram.rearrange("(k e) r -> k (e r)", e=GROUP)[:, GROUP * REC - REC + 1:GROUP * REC - REC + 2])
        with ExitStack() as c:
            w_dst = sbuf("w_dst", [P, TILES], ctx=c)
            place_dst = sbuf("place_dst", [P, TILES], ctx=c)
            ends_dst = sbuf("ends_dst", [P, TILES, 2], ctx=c)
            rows_by_cell()
            messages()
        staircase("src", msg_dram.rearrange("(k e) r -> k (e r)", e=GROUP)[:, GROUP * MSG - MSG + D + 1:GROUP * MSG - MSG + D + 2])
        aggregate("src", acc, D + 1)

        def layer0(step, sq, a, b):
            step(nc.vector.tensor_scalar(deg[:], acc[:, :, D], 1.0, None, ALU.max))
            step(nc.vector.reciprocal(deg[:], deg[:]))
            step(nc.vector.tensor_tensor(X[:], X[:], acc[:, :, 0:D], ALU.add))
            layernorm(step, X, sq, a, b)
        node_math(layer0)

        node_view = lambda k: nodes_dram[k].rearrange("(t p) d -> p t d", p=P)
        with ExitStack() as c:
            S = sbuf("S", [P, TILES, HEADS], ctx=c)
            with ExitStack() as c1:
                qkv = sbuf("qkv", [P, NT, 3 * D], ctx=c1)
                project(X, D, wq_s, 3 * D, qkv, bias=bq_s)
                store([(node_view("kv"), qkv[:, :, D:3 * D])])

                def attention(step, picked, rows, a, b, bias, at):
                    v = nc.vector
                    step(v.tensor_tensor(a, picked, rows[:, :, 0:D], ALU.mult))
                    step(v.tensor_reduce(b[:, :, 0:HEADS], a.rearrange("p t (h d) -> p t h d", h=HEADS), AX.X, ALU.add))
                    step(v.scalar_tensor_tensor(S[:, bass.ds(at, TB), :], b[:, :, 0:HEADS], DH ** -0.5,
                                                bias.rearrange("p (t h) -> p t h", h=HEADS), ALU.mult, ALU.add))
                attention.steps = 3
                edge_scores(nodes_dram["kv"], 2 * D, D, qkv, D, attention, ef=True)

            with ExitStack() as b_, nc.Block() as block:
                own, temp = sem("own", b_), sem("temp", b_)

                @block.scalar
                def _(act):
                    nc.scalar.activation(lt_s[:], lt_s[:], ACT.Exp).then_inc(temp, 1)

                @block.vector
                def _(dve):
                    step = serial(dve, own)
                    heads = lambda t: t[:].unsqueeze(1).to_broadcast([P, TILES, HEADS])
                    step(nc.vector.tensor_tensor(S[:], S[:], heads(be_s), ALU.add))
                    dve.wait_ge(temp, 1)
                    step(nc.vector.tensor_tensor(S[:], S[:], heads(lt_s), ALU.mult))
            softmax_exp(S, HEADS, floor=-1.0e9)
            aggregate("dst", acc, D + HEADS, stream=kept_rows, weights=S, extra=S)
        with ExitStack() as c:
            O = sbuf("O", [P, NT, D], ctx=c)
            den = sbuf("den", [P, NT, HEADS], ctx=c)

            def attended(step, sq, a, b):
                v = nc.vector
                step(v.tensor_scalar(den[:], acc[:, :, D:D + HEADS], 1e-10, None, ALU.add))
                step(v.reciprocal(den[:], den[:]))
                for h in range(HEADS):
                    part_h = slice(h * DH, (h + 1) * DH)
                    step(v.tensor_tensor(O[:, :, part_h], acc[:, :, part_h], den[:, :, h:h + 1].to_broadcast([P, NT, DH]), ALU.mult))
            node_math(attended, norms=0)
            Z = sbuf("Z", [P, NT, D], ctx=c)
            project(O, D, wo_s, D, Z, bias=bo_s)

            def layer1(step, sq, a, b):
                v = nc.vector
                step(v.tensor_tensor(Z[:], Z[:], X[:], ALU.add))
                layernorm(step, Z, sq, a, b, affine=(ga_s, bt_s))
                step(v.tensor_tensor(X[:], X[:], Z[:], ALU.add))
                layernorm(step, X, sq, a, b)
            node_math(layer1, norms=2)

        with ExitStack() as c:
            near = sbuf("xr_self", [P, NT, D + 1], ctx=c)
            xl = sbuf("xl", [P, NT, D], ctx=c)
            S = sbuf("S2", [P, TILES, 1], ctx=c)
            SE = sbuf("SE", [P, TILES, 1], ctx=c)
            with ExitStack() as c1:
                lr = sbuf("lr", [P, NT, 2 * D], ctx=c1)
                project(X, D, wlr_s, 2 * D, lr)

                def own_scores(step, sq, a, b):
                    v = nc.vector
                    step(v.tensor_copy(xl[:], lr[:, :, 0:D]))
                    step(v.tensor_copy(near[:, :, 0:D], lr[:, :, D:2 * D]))
                    step(v.tensor_tensor(sq[:], lr[:, :, 0:D], lr[:, :, D:2 * D], ALU.add))
                    step(v.scalar_tensor_tensor(sq[:], sq[:], 0.2, sq[:], ALU.mult, ALU.max))
                    step(v.tensor_tensor(sq[:], sq[:], rowwise(att_s[:]), ALU.mult))
                    step(v.tensor_reduce(near[:, :, D], sq[:], AX.X, ALU.add))
                node_math(own_scores, norms=0)
                store([(node_view("xl"), xl[:])])

            def gat(step, picked, rows, a, b, bias, at):
                v = nc.vector
                step(v.tensor_tensor(a, picked[:, :, 0:D], rows, ALU.add))
                step(v.scalar_tensor_tensor(b, a, 0.2, a, ALU.mult, ALU.max))
                step(v.tensor_tensor(a, b, att_s[:].unsqueeze(1).to_broadcast([P, TB, D]), ALU.mult))
                step(v.tensor_reduce(S[:, bass.ds(at, TB), 0], a, AX.X, ALU.add))
                step(v.tensor_copy(SE[:, bass.ds(at, TB), 0], picked[:, :, D]))
            gat.steps = 5
            edge_scores(nodes_dram["xl"], D, 0, near, D + 1, gat)
            SX = sbuf("SX", [P, TILES, 2], ctx=c)
            softmax_exp(S, 1, SE=SE, SX=SE)
            with ExitStack() as b_, nc.Block() as block:
                own = sem("own", b_)

                @block.vector
                def _(dve):
                    step = serial(dve, own)
                    step(nc.vector.tensor_copy(SX[:, :, 0:1], S[:]))
                    step(nc.vector.tensor_copy(SX[:, :, 1:2], SE[:]))
            aggregate("dst", acc, D + 3, stream=kept_rows, weights=S, extra=SX)
            own_w = sbuf("own_w", [P, NT], ctx=c)

            def layer2(step, sq, a, b):
                v = nc.vector
                step(v.tensor_scalar(a[:], acc[:, :, D + 2], 1.0, None, ALU.max))
                step(v.reciprocal(a[:], a[:]))
                step(v.tensor_tensor(own_w[:], acc[:, :, D + 1], a[:], ALU.mult))
                step(v.tensor_scalar(a[:], acc[:, :, D + 2], 0.0, None, ALU.is_equal))
                step(v.tensor_tensor(own_w[:], own_w[:], a[:], ALU.add))
                step(v.tensor_tensor(b[:], acc[:, :, D], own_w[:], ALU.add))
                step(v.reciprocal(b[:], b[:]))
                step(v.tensor_tensor(sq[:], xl[:], wide(own_w[:]), ALU.mult))
                step(v.tensor_tensor(sq[:], sq[:], acc[:, :, 0:D], ALU.add))
                step(v.tensor_tensor(sq[:], sq[:], wide(b[:]), ALU.mult))
                step(v.tensor_tensor(sq[:], sq[:], rowwise(bias2_s[:]), ALU.add))
                step(v.tensor_tensor(X[:], X[:], sq[:], ALU.add))
                layernorm(step, X, sq, a, b)
            node_math(layer2)

        node_table = lambda k: nodes_dram[k].rearrange("(t p) d -> p t d", p=P)
        store([(node_table("x3"), X[:])])
        aggregate("src", acc, D, table=nodes_dram["x3"])
        with ExitStack() as c:
            Y = sbuf("Y", [P, NT, D], ctx=c)
            Hd = sbuf("H", [P, NT, HID], ctx=c)

            def mean3(step, sq, a, b):
                step(nc.vector.tensor_tensor(Y[:], acc[:, :, 0:D], wide(deg[:]), ALU.mult))
                step(nc.vector.tensor_tensor(Y[:], Y[:], X[:], ALU.add))
            node_math(mean3, norms=0)
            project(Y, D, w1_s, HID, Hd, bias=b1_s, relu=True)
            project(Hd, HID, w2_s, D, Y)
            store([(node_table("y2"), Y[:])])
            aggregate("src", acc, D, table=nodes_dram["y2"])

            def last3(step, sq, a, b):
                step(nc.vector.tensor_tensor(sq[:], acc[:, :, 0:D], wide(deg[:]), ALU.mult))
                step(nc.vector.tensor_tensor(Y[:], Y[:], sq[:], ALU.add))
                step(nc.vector.tensor_tensor(Y[:], Y[:], rowwise(b2_s[:]), ALU.add))
                step(nc.vector.tensor_tensor(X[:], X[:], Y[:], ALU.add))
                layernorm(step, X, sq, a, b)
            node_math(last3)
        full = NODES // P
        store([(out[0:full * P, :].rearrange("(t p) d -> p t d", p=P), X[:, 0:full, :]),
               (out[full * P:NODES, :], X[0:NODES - full * P, full, :])])


def layout(inp):
    import numpy as np
    a = {k: np.ascontiguousarray(v) for k, v in inp.items()}

    def padded(v, n, fill):
        o = np.full((n,) + v.shape[1:], fill, v.dtype)
        o[:v.shape[0]] = v
        return o
    g1, g2, g3 = "L1_gnn_", "L2_gnn_", "L3_gnn_"
    row = lambda v: np.ascontiguousarray(v.reshape(1, -1))
    return {
        "x_in": padded(a["x"], NPAD, 0),
        "src_in": padded(a["src"], EPAD, NPAD - 1),
        "dst_in": padded(a["dst"], EPAD, NPAD - 1),
        "weight_in": padded(a["edge_weight"], EPAD, 0),
        "efT_in": np.ascontiguousarray(padded(a["edge_attr_32"], EPAD, 0).T),
        "wqkv_in": np.ascontiguousarray(np.concatenate([a[g1 + "Wq"].T, a[g1 + "Wk"].T, a[g1 + "Wv"].T], 1)),
        "bqkv_in": row(np.concatenate([a[g1 + "bq"], a[g1 + "bk"], a[g1 + "bv"]])),
        "weT_in": np.ascontiguousarray(a[g1 + "We"].T),
        "be_in": row(a[g1 + "be"]),
        "woT_in": np.ascontiguousarray(a[g1 + "Wo"].T),
        "bo_in": row(a[g1 + "bo"]),
        "gamma_in": row(a[g1 + "ln_gamma"]),
        "beta_in": row(a[g1 + "ln_beta"]),
        "log_temp_in": row(a[g1 + "log_temp"]),
        "wlr_in": np.ascontiguousarray(np.concatenate([a[g2 + "W_l"], a[g2 + "W_r"]], 1)),
        "att_in": row(a[g2 + "att"]),
        "bias2_in": row(a[g2 + "bias"]),
        "w1_in": a[g3 + "W1"],
        "b1_in": row(a[g3 + "b1"]),
        "w2_in": a[g3 + "W2"],
        "b2_in": row(a[g3 + "b2"]),
    }


def kernel(**inputs):
    import numpy as np
    import concourse.bacc as bacc
    from concourse.bass_utils import run_bass_kernel_spmd as run
    nc = bacc.Bacc("TRN2", target_bir_lowering=False, num_devices=1)
    arrays = layout(inputs)
    args = [nc.dram_tensor(n, a.shape, mybir.dt.from_np(a.dtype), kind="ExternalInput").ap() for n, a in arrays.items()]
    out = nc.dram_tensor("out", (NODES, D), F32, kind="ExternalOutput").ap()
    gnn(nc, *args, out)
    r = run(nc, [arrays], core_ids=[0])
    return r.results[0]["out"]
```

```python
import concourse.bass as bass
from concourse import mybir
from contextlib import ExitStack

F32 = mybir.dt.float32
I32 = mybir.dt.int32
EngineType = mybir.EngineType
BF16 = mybir.dt.bfloat16
ALU = mybir.AluOpType
ACT = mybir.ActivationFunctionType
AX = mybir.AxisListType

NODES, EDGES, D, DE, HEADS, HID = 3125, 100000, 64, 32, 4, 128
DH = D // HEADS
P = 128
NT = -(-NODES // P)
NPAD = NT * P
GROUP = 2 * P
GROUPS = -(-EDGES // GROUP)
EPAD = GROUPS * GROUP
CHUNK = EPAD // P
BODY = 4
TB = 2 * BODY
CELLS = -(-(GROUPS + NT - 1) // (2 * BODY)) * 2 * BODY
STEPS = CELLS // BODY
BPER = -(-(GROUPS + NT * NT - 1) // STEPS)
BFIRST, BSECOND = BPER * 2 // 5, BPER - BPER * 2 // 5
BCELLS = BPER * STEPS
BCB = -(-BCELLS // P)
BSTEP = 13
assert BCELLS % (4 * BSTEP) == 0
TILES = 2 * CELLS
CB = -(-CELLS // P)
REC = 4
NS = 4
MSG = D + 4
NOWHERE = float(1 << 18)
BIG = 1.0e30
EPS = 1e-5


def serial(eng, sem, base=0):
    n = [0]

    def step(ins):
        n[0] += 1
        ins.then_inc(sem, 1)
        eng.wait_ge(sem, base + n[0])
    return step


def gnn(nc, x, src, dst, weight, efT, wqkv, bqkv, weT, be, woT, bo, gamma, beta, log_temp,
        wlr, att, bias2, w1, b1, w2, b2, out):
    top = ExitStack()
    with top:
        used = {}

        def fresh(name):
            used[name] = used.get(name, 0) + 1
            return f"{name}_{used[name]}"

        def sbuf(name, shape, dt=F32, ctx=top):
            return ctx.enter_context(nc.sbuf_tensor(fresh(name), shape, dt))

        def psum(name, shape, ctx):
            return ctx.enter_context(nc.psum_tensor(fresh(name), shape, F32))

        live = {}

        def sem(name, ctx):
            if id(ctx) not in live:
                live[id(ctx)] = []

                def release():
                    nc.clear_and_free_semaphores(live.pop(id(ctx)))
                    nc.all_engine_barrier()
                ctx.callback(release)
            live[id(ctx)].append(nc.alloc_semaphore(fresh(name)))
            return live[id(ctx)][-1]

        def dram(name, shape, dt=F32):
            return nc.dram_tensor(name, shape, dt, kind="Internal").ap()

        rec_dram = dram("rec_by_dst", [EPAD, REC])
        msg_dram = dram("msg_by_src", [EPAD, MSG])
        loc_dram = dram("loc_by_cell", [CELLS, GROUP])
        key_dram = dram("clamped_dst", [CELLS, GROUP])
        k_dram = {o: dram(f"k_{o}", [CB * P], I32) for o in ("dst", "src")}
        n_dram = {o: dram(f"n_{o}", [CB * P], I32) for o in ("dst", "src")}
        block_dram = dram("block_cells", [BCB * P, 2], I32)
        ends_dram = dram("ends_by_place", [EPAD, 2])
        counts_dram = dram("cell_counts", [P, BCELLS * P], BF16)

        ident = sbuf("ident", [P, P])
        ones = sbuf("ones", [P, P])
        before = sbuf("before", [P, P])
        lane = sbuf("lane", [P, P])
        part = sbuf("part", [P, 1])
        gather_id = sbuf("gather_id", [P, TILES + NS * TB])
        loc = sbuf("loc", [P, TILES])
        k_i = sbuf("k_i", [P, CB], I32)
        k_f = sbuf("k_f", [P, CB])
        n_f = sbuf("n_f", [P, CB])
        n_all = sbuf("n_all", [P, CELLS])
        n_row = {o: sbuf(f"n_row_{o}", [1, BODY + CELLS], I32) for o in ("dst", "src")}
        k_row = {o: sbuf(f"k_row_{o}", [1, CELLS], I32) for o in ("dst", "src")}

        def setup():
            with ExitStack() as c, nc.Block() as block:
                made, done = sem("iota_made", c), sem("consts", c)

                @block.gpsimd
                def _(pool):
                    nc.gpsimd.iota(lane[:], [[1, P]], base=0, channel_multiplier=0,
                                   allow_small_or_imprecise_dtypes=True).then_inc(made, 1)
                    nc.gpsimd.iota(part[:], [[1, 1]], base=0, channel_multiplier=1,
                                   allow_small_or_imprecise_dtypes=True).then_inc(made, 1)

                @block.vector
                def _(dve):
                    nc.vector.memset(ones[:], 1.0)
                    nc.vector.memset(gather_id[:, TILES:], 0.0)
                    for o in ("dst", "src"):
                        nc.vector.memset(n_row[o][:, 0:BODY], 0)
                    dve.wait_ge(made, 2)
                    nc.vector.tensor_scalar(ident[:], lane[:], part[:], None, ALU.is_equal)
                    nc.vector.tensor_scalar(before[:], lane[:], part[:], None, ALU.is_gt).then_inc(done, 1)

        def several(words, engine, below):
            return nc.values_load_multi_w_load_instructions(
                words, engines=(engine,), min_val=0, max_val=below - 1,
                skip_runtime_bounds_check_because="the staircases bound their groups and tiles")[1]

        def rank():
            with ExitStack() as r:
                rec = sbuf("rec", [P, CHUNK, REC], ctx=r)
                s_i = sbuf("src_i", [P, CHUNK], I32, ctx=r)
                d_i = sbuf("dst_i", [P, CHUNK], I32, ctx=r)
                w_f = sbuf("w_f", [P, CHUNK], ctx=r)
                tile = sbuf("src_tile", [P, CHUNK], ctx=r)
                hit = sbuf("hit", [P, NT, CHUNK], BF16, ctx=r)
                run = sbuf("run", [P, NT, CHUNK], ctx=r)
                place = sbuf("place", [P, CHUNK], ctx=r)
                count = sbuf("count", [P, NT], ctx=r)
                total = sbuf("total", [P, NT], ctx=r)
                upto = sbuf("upto", [P, NT], ctx=r)
                base = sbuf("base", [P, NT], ctx=r)
                ahead = psum("ahead", [P, 512], r)
                with nc.Block() as block:
                    loaded = [sem(f"loaded{i}", r) for i in range(3)]
                    filled, stored = sem("rec_filled", r), sem("rec_stored", r)
                    ew, counted, summed = sem("exp_w", r), sem("counted", r), sem("summed", r)
                    own, scanned = sem("dve_own", r), sem("scanned", r)

                    @block.sync
                    def _(sp):
                        for i, (to, frm) in enumerate(((s_i, src), (d_i, dst), (w_f, weight))):
                            sp.dma_start(to[:], frm.rearrange("(p j) -> p j", p=P)).then_inc(loaded[i], 16)
                        sp.wait_ge(filled, 1)
                        sp.wait_ge(ew, 1)
                        sp.dma_start(rec_dram.rearrange("(p j) r -> p (j r)", p=P),
                                     rec[:].rearrange("p j r -> p (j r)")).then_inc(stored, 16)
                        sp.wait_ge(stored, 16)

                    @block.scalar
                    def _(act):
                        act.wait_ge(loaded[2], 16)
                        nc.scalar.activation(rec[:, :, 2], w_f[:], ACT.Exp, scale=-1.0).then_inc(ew, 1)

                    @block.vector
                    def _(dve):
                        step = serial(dve, own)
                        dve.wait_ge(loaded[0], 16)
                        step(nc.vector.tensor_copy(rec[:, :, 0], s_i[:]))
                        dve.wait_ge(loaded[1], 16)
                        step(nc.vector.tensor_copy(rec[:, :, 1], d_i[:]))
                        step(nc.vector.tensor_single_scalar(s_i[:], s_i[:], 7, op=ALU.arith_shift_right))
                        step(nc.vector.tensor_copy(tile[:], s_i[:]))
                        step(nc.vector.tensor_tensor(hit[:], tile[:].unsqueeze(1).to_broadcast([P, NT, CHUNK]),
                                                     lane[:, 0:NT].unsqueeze(2).to_broadcast([P, NT, CHUNK]), ALU.is_equal))
                        step(nc.vector.tensor_reduce(count[:], hit[:], AX.X, ALU.add))
                        dve.sem_inc(counted, 1)
                        dve.wait_ge(summed, 1)
                        step(nc.vector.tensor_copy(total[:], ahead[:, 64:64 + NT]))
                        step(nc.vector.tensor_tensor_scan(upto[:], total[:], total[:], 0.0, ALU.add, ALU.max))
                        step(nc.vector.tensor_tensor(upto[:], upto[:], total[:], ALU.subtract))
                        step(nc.vector.scalar_tensor_tensor(base[:], upto[:], -1.0, ahead[:, 0:NT], ALU.add, ALU.add))
                        with dve.Fori(0, NT // 5) as i:
                            for q in range(5):
                                v = i * 5 + q
                                nc.vector.tensor_tensor_scan(
                                    run[:, bass.ds(v, 1), :].rearrange("p a e -> p (a e)"), ones[:, 0:1].to_broadcast([P, CHUNK]),
                                    hit[:, bass.ds(v, 1), :].rearrange("p a e -> p (a e)"), base[:, bass.ds(v, 1)],
                                    ALU.mult, ALU.add).then_inc(scanned, 1)
                        dve.wait_ge(scanned, NT)
                        step(nc.vector.tensor_tensor(run[:], run[:], hit[:], ALU.mult))
                        step(nc.vector.tensor_reduce(place[:], run[:].rearrange("p v e -> p e v"), AX.X, ALU.add))
                        nc.vector.tensor_copy(rec[:, :, 3], place[:]).then_inc(filled, 1)

                    @block.tensor
                    def _(pe):
                        pe.wait_ge(counted, 1)
                        nc.tensor.matmul(ahead[:, 0:NT], before[:], count[:], start=True, stop=True)
                        nc.tensor.matmul(ahead[:, 64:64 + NT], ones[:], count[:], start=True,
                                         stop=True).then_inc(summed, 1)

        def staircase(order, keys):
            with ExitStack() as c, nc.Block() as block:
                last = sbuf("last_key", [P, CB], ctx=c)
                last_i = sbuf("last_i", [P, CB], I32, ctx=c)
                diag = sbuf("diag", [P, CB, P], ctx=c)
                ends = sbuf("ends", [P, CB * P], ctx=c)
                kk = sbuf("kk", [P, CB * P], ctx=c)
                less = sbuf("less", [P, CB * P], ctx=c)
                cell = sbuf("cell", [P, CB], ctx=c)
                n_c = sbuf("n_c", [P, CB], ctx=c)
                n_i = sbuf("n_i", [P, CB], I32, ctx=c)
                n_r = sbuf("n_r", [1, CELLS], ctx=c)
                pB = psum("ends_all", [P, CB * P], c)
                pN = psum("n_all", [P, CB * P], c)
                loaded, iotas, own = sem("last_loaded", c), sem("iotas", c), sem("own", c)
                cleared = sem("last_cleared", c)
                diag_made, spread = sem("diag_made", c), sem("spread", c)
                k_made, row_made, n_spread = sem("k_made", c), sem("row_made", c), sem("n_spread", c)
                put, back = [sem(f"put{i}", c) for i in range(2)], sem("back", c)
                full = GROUPS // P
                rest = GROUPS - full * P

                @block.sync
                def _(sp):
                    sp.wait_ge(cleared, 1)
                    with nc.allow_non_contiguous_dma(reason="one key of each group"):
                        for b in range(CB):
                            m = P if b < full else rest
                            sp.dma_start(last[:m, b:b + 1], keys[b * P:b * P + m, :]).then_inc(loaded, 16)
                    sp.wait_ge(k_made, 1)
                    with nc.allow_non_contiguous_dma(reason="one word of each cell"):
                        sp.dma_start(k_dram[order].rearrange("(b p) -> p b", p=P), k_i[:]).then_inc(put[0], 16)
                        sp.dma_start(n_dram[order].rearrange("(b p) -> p b", p=P), n_i[:]).then_inc(put[1], 16)
                    sp.wait_ge(put[0], 16)
                    sp.wait_ge(put[1], 16)
                    sp.dma_start(k_row[order][:], k_dram[order][0:CELLS].rearrange("(a k) -> a k", a=1)).then_inc(back, 16)
                    sp.dma_start(n_row[order][:, BODY:], n_dram[order][0:CELLS].rearrange("(a k) -> a k", a=1)).then_inc(back, 16)
                    sp.wait_ge(back, 32)

                @block.gpsimd
                def _(pool):
                    nc.gpsimd.iota(kk[:], [[1, CB * P]], base=0, channel_multiplier=0,
                                   allow_small_or_imprecise_dtypes=True).then_inc(iotas, 1)
                    nc.gpsimd.iota(cell[:], [[P, CB]], base=0, channel_multiplier=1,
                                   allow_small_or_imprecise_dtypes=True).then_inc(iotas, 1)

                @block.vector
                def _(dve):
                    step = serial(dve, own)
                    nc.vector.memset(last[:], 0.0).then_inc(cleared, 1)
                    dve.wait_ge(loaded, 16 * CB)
                    step(nc.vector.tensor_copy(last_i[:], last[:]))
                    step(nc.vector.tensor_single_scalar(last_i[:], last_i[:], 7, op=ALU.arith_shift_right))
                    step(nc.vector.tensor_copy(last[:], last_i[:]))
                    for b in range(CB):
                        ins = nc.vector.tensor_scalar(diag[:, b, :], ident[:], last[:, b:b + 1], None, ALU.mult)
                    ins.then_inc(diag_made, 1)
                    dve.wait_ge(iotas, 2)
                    dve.wait_ge(spread, 1)
                    step(nc.vector.tensor_tensor(ends[:], pB[:], kk[:], ALU.add))
                    step(nc.vector.memset(ends[:, GROUPS:], 1.0e6))
                    for b in range(CB):
                        step(nc.vector.tensor_scalar(less[:], ends[:], cell[:, b:b + 1], None, ALU.is_lt))
                        step(nc.vector.tensor_reduce(k_f[:, b:b + 1], less[:], AX.X, ALU.add))
                    step(nc.vector.tensor_scalar(k_f[:], k_f[:], float(GROUPS - 1), None, ALU.min))
                    step(nc.vector.tensor_tensor(n_f[:], cell[:], k_f[:], ALU.subtract))
                    step(nc.vector.tensor_scalar(n_c[:], n_f[:], float(NT - 1), None, ALU.min))
                    step(nc.vector.tensor_copy(n_i[:], n_c[:]))
                    step(nc.vector.tensor_copy(k_i[:], k_f[:]))
                    step(nc.vector.tensor_scalar(n_f[:], n_f[:], float(P), None, ALU.mult))
                    for b in range(CB):
                        ins = nc.vector.tensor_scalar(diag[:, b, :], ident[:], n_f[:, b:b + 1], None, ALU.mult)
                    ins.then_inc(k_made, 1)
                    dve.wait_ge(n_spread, 1)
                    step(nc.vector.tensor_copy(n_all[:], pN[:, 0:CELLS]))

                @block.tensor
                def _(pe):
                    pe.wait_ge(diag_made, 1)
                    nc.tensor.matmul(pB[:], ones[:], diag[:].rearrange("p b q -> p (b q)"), start=True,
                                     stop=True).then_inc(spread, 1)
                    pe.wait_ge(k_made, 1)
                    nc.tensor.matmul(pN[:], ones[:], diag[:].rearrange("p b q -> p (b q)"), start=True,
                                     stop=True).then_inc(n_spread, 1)

        def rows_by_cell():
            with ExitStack() as c, nc.Block() as block:
                R = sbuf("cell_recs", [P, CB, GROUP, REC], ctx=c)
                L = sbuf("cell_loc", [P, CB, GROUP], ctx=c)
                K = sbuf("cell_key", [P, CB, GROUP], ctx=c)
                V = sbuf("cell_valid", [P, CB, GROUP], ctx=c)
                pT = [psum(f"turned{i}", [P, 512], c) for i in range(4)]
                got = [sem(f"got{b}", c) for b in range(CB)]
                rows_made, turned, freed, own = sem("rows_made", c), sem("turned", c), sem("freed", c), sem("own", c)
                put = [sem(f"put{i}", c) for i in range(2)]
                rows_in = [min(P, CELLS - b * P) for b in range(CB)]
                turns = [(b, g, q) for b in range(CB) for g in range(2) for q in range(5)]

                @block.sync
                def _(sp):
                    sp.wait_ge(rows_made, 1)
                    for b in range(CB):
                        m = rows_in[b]
                        sp.dma_start(loc_dram[b * P:b * P + m, :], L[:m, b, :]).then_inc(put[0], 16)
                        sp.dma_start(key_dram[b * P:b * P + m, :], K[:m, b, :]).then_inc(put[1], 16)
                    sp.wait_ge(put[0], 16 * CB)
                    sp.wait_ge(put[1], 16 * CB)

                @block.gpsimd
                def _(pool):
                    view = rec_dram.rearrange("(k e) r -> k (e r)", e=GROUP)
                    for b in range(CB):
                        m = rows_in[b]
                        pool.indirect_dma_start(
                            out=R[:m, b, :, :].rearrange("p e r -> p (e r)"), out_offset=None, in_=view,
                            in_offset=bass.IndirectOffsetOnAxis(ap=k_i[:m, b:b + 1], axis=0)).then_inc(got[b], 16)

                @block.vector
                def _(dve):
                    v = nc.vector
                    step = serial(dve, own)
                    for b in range(CB):
                        m = rows_in[b]
                        dve.wait_ge(got[b], 16)
                        Lb, Kb, Vb, Rp = L[:m, b, :], K[:m, b, :], V[:m, b, :], R[:m, b, :, 3]
                        step(v.tensor_scalar(Lb, R[:m, b, :, 1], n_f[:m, b:b + 1], None, ALU.subtract))
                        step(v.tensor_scalar(Kb, Lb, 0.0, float(P - 1), ALU.max, ALU.min))
                        step(v.tensor_tensor(Vb, Lb, Kb, ALU.is_equal))
                        step(v.scalar_tensor_tensor(Lb, Lb, 1.0, Vb, ALU.add, ALU.mult))
                        step(v.tensor_scalar(Lb, Lb, -1.0, None, ALU.add))
                        step(v.tensor_scalar(Kb, Kb, n_f[:m, b:b + 1], None, ALU.add))
                        step(v.scalar_tensor_tensor(Rp, Rp, -NOWHERE, Vb, ALU.add, ALU.mult))
                        step(v.tensor_scalar(Rp, Rp, NOWHERE, None, ALU.add))
                    dve.sem_inc(rows_made, 1)
                    for i, (b, g, q) in enumerate(turns):
                        m = rows_in[b]
                        dve.wait_ge(turned, i + 1)
                        to = (gather_id[:, 0:TILES], loc[:], w_dst[:], place_dst[:], ends_dst[:, :, 1])[q]
                        to = to.rearrange("p (c g) -> p c g", g=2)[:, b * P:b * P + m, g]
                        v.tensor_copy(to, pT[i % 4][:, 0:m]).then_inc(freed, 1)
                    dve.wait_ge(freed, len(turns))
                    step(v.tensor_copy(ends_dst[:, :, 0], gather_id[:, 0:TILES]))

                @block.tensor
                def _(pe):
                    pe.wait_ge(rows_made, 1)
                    for i, (b, g, q) in enumerate(turns):
                        m = rows_in[b]
                        half = slice(g * P, (g + 1) * P)
                        if i >= 4:
                            pe.wait_ge(freed, i - 3)
                        frm = (R[:m, b, half, 0], L[:m, b, half], R[:m, b, half, 2], R[:m, b, half, 3], K[:m, b, half])[q]
                        nc.tensor.transpose(pT[i % 4][:, 0:m], frm, ident[:m, :m]).then_inc(turned, 1)

        def messages():
            with ExitStack() as c, nc.Block() as block:
                rows = sbuf("message", [P, NS, TB, MSG], ctx=c)
                ids = sbuf("place_slot", [P, NS, TB], I32, ctx=c)
                loc_all = sbuf("loc_all", [P, NS, TB * P], ctx=c)
                hotT = sbuf("hotT", [P, NS, TB, P], ctx=c)
                picked = psum("picked", [P, NS, TB, D], c)
                ring = lambda name: [sem(f"{name}{s}", c) for s in range(NS)]
                loc_in, hot_made, products, filled, beside, sent = map(
                    ring, ("loc_in", "hot_made", "products", "filled", "beside", "sent"))
                taken, cleared = sem("taken", c), sem("cleared", c)
                loc_flat = loc_dram.rearrange("(a c) e -> a (c e)", a=1)

                @block.sync
                def _(sp):
                    with sp.Fori(0, STEPS // NS) as i:
                        for s in range(NS):
                            sp.wait_ge(hot_made[s], i + 1)
                            sp.dma_start(loc_all[:, s, :], loc_flat[:, bass.ds((i * NS + s) * (TB * P), TB * P)]
                                         .to_broadcast([P, TB * P])).then_inc(loc_in[s], 16)

                @block.vector
                def _(dve):
                    for s in range(NS):
                        dve.sem_inc(hot_made[s], 1)
                        dve.sem_inc(filled[s], 1)
                    nc.vector.memset(rows[:, :, :, D:D + 1], 1.0).then_inc(cleared, 1)
                    nc.vector.memset(rows[:, :, :, D + 3:MSG], 0.0).then_inc(cleared, 1)
                    dve.wait_ge(cleared, 2)

                    def fill(i, s):
                        at = (i * NS + s) * TB
                        dve.wait_ge(products[s], i + 2)
                        dve.wait_ge(beside[s], i * 2 + 2)
                        nc.vector.tensor_tensor(rows[:, s, :, 0:D], picked[:, s, :, :],
                                                w_dst[:, bass.ds(at, TB)].unsqueeze(2).to_broadcast([P, TB, D]),
                                                ALU.mult).then_inc(filled[s], 1)
                    with dve.Fori(0, STEPS // NS) as i:
                        for s in range(NS):
                            dve.wait_ge(loc_in[s], i * 16 + 16)
                            dve.wait_ge(products[s], i + 1)
                            nc.vector.tensor_scalar(hotT[:, s, :, :].rearrange("p t e -> p (t e)"), loc_all[:, s, :],
                                                    part[:], None, ALU.is_equal).then_inc(hot_made[s], 1)
                            if s > 0:
                                fill(i, s - 1)
                        fill(i, NS - 1)

                @block.tensor
                def _(pe):
                    for s in range(NS):
                        pe.sem_inc(products[s], 1)
                    with pe.Fori(0, STEPS // NS) as i:
                        for s in range(NS):
                            pe.wait_ge(hot_made[s], i + 2)
                            pe.wait_ge(filled[s], i + 1)
                            ns = several(n_row["dst"][0:1, bass.ds((i * NS + s) * BODY + BODY, BODY)], EngineType.PE, NT)
                            for q, n in enumerate(ns):
                                for g in range(2):
                                    ins = nc.tensor.matmul(picked[:, s, 2 * q + g, :], hotT[:, s, 2 * q + g, :],
                                                           X[:, bass.ds(n, 1), :].rearrange("p a c -> p (a c)"),
                                                           start=True, stop=True)
                            ins.then_inc(products[s], 1)

                @block.scalar
                def _(act):
                    def body(i):
                        for s in range(NS):
                            at = (i * NS + s) * TB
                            if not (isinstance(i, int) and i == 0):
                                act.wait_ge(sent[s], i * (16 * TB))
                            nc.scalar.copy(ids[:, s, :], place_dst[:, bass.ds(at, TB)]).then_inc(beside[s], 1)
                            nc.scalar.copy(rows[:, s, :, D + 1:D + 3], ends_dst[:, bass.ds(at, TB), :]).then_inc(beside[s], 1)
                    body(0)
                    with act.Fori(1, STEPS // NS) as i:
                        body(i)

                @block.gpsimd
                def _(pool):
                    with pool.Fori(0, STEPS // NS) as i:
                        for s in range(NS):
                            pool.wait_ge(beside[s], i * 2 + 2)
                            pool.wait_ge(filled[s], i + 2)
                            pool.sem_inc(taken, 1)
                            for t in range(TB):
                                pool.indirect_dma_start(
                                    out=msg_dram, out_offset=bass.IndirectOffsetOnAxis(ap=ids[:, s, t:t + 1], axis=0),
                                    in_=rows[:, s, t, :], in_offset=None, bounds_check=EPAD - 1,
                                    oob_is_err=False).then_inc(sent[s], 16)
                    for s in range(NS):
                        pool.wait_ge(sent[s], (STEPS // NS) * (16 * TB))

        def aggregate(order, acc, cols, stream=None, weights=None, extra=None):
            by_group = stream is None
            with ExitStack() as c, nc.Block() as block:
                RS = 2 * NS
                LOOPS = STEPS // RS
                n_extra = 0 if extra is None else extra.shape[2]
                rows = sbuf("rows", [P, RS, TB, MSG if by_group else D], ctx=c)
                mixed = rows if by_group else sbuf("mixed", [P, RS, TB, cols], ctx=c)
                left = sbuf("left", [P, RS, TB, cols], ctx=c)
                parts = sbuf("parts3", [P, RS, 3, TB, cols], BF16, ctx=c)
                lane_h = sbuf("lane_hot", [P, P, TB], BF16, ctx=c)
                hot = sbuf("hot", [P, RS, P, TB], BF16, ctx=c)
                loc_h = sbuf("loc_h", [P, RS if by_group else STEPS, TB], BF16, ctx=c)
                accs = sbuf("accs", [P, BODY, NT, cols], ctx=c)
                part_sum = psum("part_sum", [P, RS, BODY, P], c)
                ring = lambda name: [sem(f"{name}{s}", c) for s in range(RS)]
                arrived, mixed_made, beside, located, hot_made = map(
                    ring, ("arrived", "mixed_made", "beside", "located", "hot_made"))
                high_made, left_made, middle_made, low_made, summed, added = map(
                    ring, ("high_made", "left_made", "middle_made", "low_made", "summed", "added"))
                ready, own, own_add = (sem(n, c) for n in ("ready", "own", "own_add"))
                PER = 16 * BODY if by_group else 16

                def behind(i, s, d):
                    return (i + (s - d) // RS, (s - d) % RS)

                def run(eng, step, last=0, peel=0):
                    for s in range(RS):
                        step(0, s)
                    with eng.Fori(1, LOOPS - peel) as i:
                        for s in range(RS):
                            step(i, s)
                    for i in range(LOOPS - peel, LOOPS):
                        for s in range(RS):
                            step(i, s)
                    for s in range(last):
                        step(LOOPS, s)
                exists = lambda u: not isinstance(u, int) or 0 <= u < LOOPS

                def load_groups(eng, engine, i, s, cells):
                    eng.wait_ge(left_made[s], i + 1)
                    eng.wait_ge(located[s], i + 1)
                    groups = msg_dram.rearrange("(k g p) r -> p (k g) r", g=2, p=P)
                    ks = several(k_row[order][0:1, bass.ds((i * RS + s) * BODY + cells[0], len(cells))], engine, GROUPS)
                    for q, k in zip(cells, ks):
                        eng.dma_start(rows[:, s, 2 * q:2 * q + 2, :], groups[:, bass.ds(k * 2, 2), :]).then_inc(arrived[s], 16)

                @block.sync
                def _(sp):
                    for s in range(RS):
                        if by_group:
                            sp.sem_inc(left_made[s], 1)
                            sp.sem_inc(located[s], 1)

                    def step(i, s):
                        if by_group:
                            load_groups(sp, EngineType.SP, i, s, range(BODY - 1))
                        else:
                            sp.wait_ge(mixed_made[s], i + 1)
                            sp.dma_start(rows[:, s, :, :].rearrange("p t d -> p (t d)"),
                                         stream[:, bass.ds((i * RS + s) * (TB * D), TB * D)]).then_inc(arrived[s], 16)
                    run(sp, step)

                @block.gpsimd
                def _(pool):
                    for s in range(RS):
                        pool.sem_inc(low_made[s], 1)
                        if not by_group:
                            pool.sem_inc(mixed_made[s], 1)

                    def low(u, r):
                        pool.wait_ge(middle_made[r], u + 2)
                        pool.wait_ge(left_made[r], u + 2)
                        pool.wait_ge(summed[r], u + 1)
                        nc.gpsimd.tensor_tensor(parts[:, r, 2, :, :], left[:, r, :, :], parts[:, r, 1, :, :],
                                                ALU.subtract).then_inc(low_made[r], 1)

                    def step(i, s):
                        if exists(i):
                            pool.wait_ge(arrived[s], i * PER + PER)
                            if by_group:
                                pool.wait_ge(hot_made[s], i + 1)
                                cells = n_all[:, bass.ds((i * RS + s) * BODY, BODY)].unsqueeze(2).to_broadcast([P, BODY, 2])
                                nc.gpsimd.tensor_tensor(loc_h[:, s, :].rearrange("p (b g) -> p b g", g=2),
                                                        rows[:, s, :, D + 1].rearrange("p (b g) -> p b g", g=2), cells,
                                                        ALU.subtract).then_inc(located[s], 1)
                            else:
                                pool.wait_ge(left_made[s], i + 1)
                                wt = weights[:, bass.ds((i * RS + s) * TB, TB), :]
                                k = wt.shape[2]
                                nc.gpsimd.tensor_tensor(
                                    mixed[:, s, :, 0:D].rearrange("p t (k d) -> p t k d", k=k),
                                    rows[:, s, :, :].rearrange("p t (k d) -> p t k d", k=k),
                                    wt.unsqueeze(3).to_broadcast([P, TB, k, D // k]), ALU.mult).then_inc(mixed_made[s], 1)
                        u, r = behind(i, s, 3)
                        if exists(u):
                            low(u, r)
                    run(pool, step, 3)

                @block.scalar
                def _(act):
                    for s in range(RS):
                        act.sem_inc(high_made[s], 1)
                        act.sem_inc(middle_made[s], 1)
                        if n_extra:
                            act.sem_inc(beside[s], 1)
                    act.wait_ge(ready, 1)
                    if by_group:
                        for s in range(4):
                            load_groups(act, EngineType.Activation, 0, s, [BODY - 1])

                    def step(i, s):
                        u, r = behind(i, s, -4)
                        if by_group and exists(u):
                            load_groups(act, EngineType.Activation, u, r, [BODY - 1])
                        if exists(i):
                            if by_group:
                                act.wait_ge(arrived[s], i * PER + PER)
                            else:
                                act.wait_ge(left_made[s], i + 1)
                                nc.scalar.copy(mixed[:, s, :, D:D + n_extra],
                                               extra[:, bass.ds((i * RS + s) * TB, TB), :]).then_inc(beside[s], 1)
                                act.wait_ge(beside[s], i + 2)
                                act.wait_ge(mixed_made[s], i + 2)
                            act.wait_ge(summed[s], i + 1)
                            nc.scalar.copy(parts[:, s, 0, :, :], mixed[:, s, :, 0:cols]).then_inc(high_made[s], 1)
                        u, r = behind(i, s, 2)
                        if exists(u):
                            act.wait_ge(left_made[r], u + 2)
                            act.wait_ge(summed[r], u + 1)
                            nc.scalar.copy(parts[:, r, 1, :, :], left[:, r, :, :]).then_inc(middle_made[r], 1)
                    run(act, step, 2, peel=1)

                @block.vector
                def _(dve):
                    clear = serial(dve, own)
                    clear(nc.vector.memset(accs[:], 0.0))
                    clear(nc.vector.tensor_copy(lane_h[:], lane[:].unsqueeze(2).to_broadcast([P, P, TB])))
                    if not by_group:
                        clear(nc.vector.tensor_copy(loc_h[:].rearrange("p j t -> p (j t)"), loc[:]))
                        if cols > D + n_extra:
                            clear(nc.vector.memset(mixed[:, :, :, D + n_extra:cols], 1.0))
                    dve.sem_inc(ready, 1)
                    for s in range(RS):
                        dve.sem_inc(hot_made[s], 1)
                        dve.sem_inc(added[s], 1)
                        if not by_group:
                            dve.sem_inc(left_made[s], 1)

                    def add(u, r):
                        j = u * RS + r
                        ns = several(n_row[order][0:1, bass.ds(j * BODY + BODY, BODY)], EngineType.DVE, NT)
                        dve.wait_ge(summed[r], u + 2)
                        if not (isinstance(j, int) and j == 0):
                            dve.wait_ge(own_add, j * BODY)
                        for b in range(BODY):
                            to = accs[:, b, bass.ds(ns[b], 1), :].rearrange("p a c -> p (a c)")
                            nc.vector.tensor_tensor(to, to, part_sum[:, r, b, 0:cols], ALU.add).then_inc(own_add, 1)
                        dve.wait_ge(own_add, (j + 1) * BODY)
                        dve.sem_inc(added[r], 1)

                    def step(i, s):
                        if exists(i):
                            dve.wait_ge(summed[s], i + 1)
                            if by_group:
                                dve.wait_ge(located[s], i + 2)
                                at = loc_h[:, s, :]
                            else:
                                at = loc_h[:, bass.ds(i * RS + s, 1), :].rearrange("p a t -> p (a t)")
                            nc.vector.tensor_tensor(hot[:, s, :, :], lane_h[:], at.unsqueeze(1).to_broadcast([P, P, TB]),
                                                    ALU.is_equal).then_inc(hot_made[s], 1)
                        u, r = behind(i, s, 1)
                        if exists(u):
                            dve.wait_ge(high_made[r], u + 2)
                            dve.wait_ge(low_made[r], u + 1)
                            nc.vector.tensor_tensor(left[:, r, :, :], mixed[:, r, :, 0:cols], parts[:, r, 0, :, :],
                                                    ALU.subtract).then_inc(left_made[r], 1)
                        u, r = behind(i, s, 5)
                        if exists(u):
                            add(u, r)
                    run(dve, step, 5)
                    last = serial(dve, own, 4 if cols > D + n_extra and not by_group else 2 if by_group else 3)
                    last(nc.vector.tensor_tensor(accs[:, 0, :, :], accs[:, 0, :, :], accs[:, 1, :, :], ALU.add))
                    last(nc.vector.tensor_tensor(accs[:, 2, :, :], accs[:, 2, :, :], accs[:, 3, :, :], ALU.add))
                    last(nc.vector.tensor_tensor(acc[:, :, 0:cols], accs[:, 0, :, :], accs[:, 2, :, :], ALU.add))

                @block.tensor
                def _(pe):
                    for s in range(RS):
                        pe.sem_inc(summed[s], 1)

                    def step(i, s):
                        pe.wait_ge(hot_made[s], i + 2)
                        pe.wait_ge(high_made[s], i + 2)
                        pe.wait_ge(middle_made[s], i + 2)
                        pe.wait_ge(low_made[s], i + 2)
                        pe.wait_ge(added[s], i + 1)
                        for b in range(BODY):
                            for m in range(6):
                                t = 2 * b + m // 3
                                ins = nc.tensor.matmul(part_sum[:, s, b, 0:cols], hot[:, s, :, t],
                                                       parts[:, s, m % 3, t, :], start=m == 0, stop=m == 5)
                        ins.then_inc(summed[s], 1)
                    run(pe, step)

        def copy_ends():
            with nc.Block() as block:
                @block.sync
                def _(sp):
                    part_of = EPAD // 17
                    for q in range(17):
                        sp.dma_start(ends_dram[q * part_of:(q + 1) * part_of, :].rearrange("(a e) r -> a e r", a=16),
                                     msg_dram[q * part_of:(q + 1) * part_of, D + 1:D + 3].rearrange("(a e) r -> a e r", a=16)
                                     ).then_inc(ends_copied, 16)

        def block_staircase():
            with ExitStack() as c, nc.Block() as block:
                G4 = -(-GROUPS // P)
                last = sbuf("last_ends", [P, G4, 2], ctx=c)
                last_i = sbuf("last_i", [P, G4, 2], I32, ctx=c)
                key = sbuf("block_key", [P, G4], ctx=c)
                diag = sbuf("diag", [P, G4, P], ctx=c)
                ends = sbuf("ends", [P, G4 * P], ctx=c)
                kk = sbuf("kk", [P, G4 * P], ctx=c)
                less = sbuf("less", [P, G4 * P], ctx=c)
                cell, k_b, blk, s_t, d_t, hit = (sbuf(n, [P, BCB], ctx=c) for n in ("cell", "k_b", "blk", "s_t", "d_t", "hit"))
                k_of = sbuf("block_k", [P, BCB], I32, ctx=c)
                ints = sbuf("block_ints", [P, BCB, 2], I32, ctx=c)
                tiles = sbuf("block_tiles", [P, 2, BCB], ctx=c)
                R = sbuf("cell_ends", [P, BCB, GROUP, 2], ctx=c)
                pB = psum("ends_all", [P, G4 * P], c)
                pT = [psum(f"turned{i}", [P, 512], c) for i in range(4)]
                loaded, iotas, own, cleared, diag_made, spread, k_made, turned, freed, rows_made = (
                    sem(n, c) for n in ("loaded", "iotas", "own", "cleared", "diag_made", "spread", "k_made", "turned", "freed", "rows_made"))
                put, back = sem("put", c), sem("back", c)
                got = [sem(f"got{b}", c) for b in range(BCB)]
                full = GROUPS // P
                rest = GROUPS - full * P
                turns = [(b, g, q) for b in range(BCB) for g in range(2) for q in range(2)]

                @block.sync
                def _(sp):
                    sp.wait_ge(cleared, 1)
                    sp.wait_ge(ends_copied, 16 * 17)
                    ends_of = ends_dram.rearrange("(k e) r -> k (e r)", e=GROUP)[:, (GROUP - 1) * 2:GROUP * 2]
                    for b in range(G4):
                        m = P if b < full else rest
                        sp.dma_start(last[:m, b, :], ends_of[b * P:b * P + m, :]).then_inc(loaded, 16)
                    sp.wait_ge(k_made, 1)
                    sp.dma_start(block_dram.rearrange("(b p) q -> p b q", p=P), ints[:]).then_inc(put, 16)
                    sp.wait_ge(put, 16)
                    sp.dma_start(block_row[:], block_dram[0:BCELLS, :].rearrange("(a c) q -> a c q", a=1)).then_inc(back, 16)
                    sp.wait_ge(back, 16)

                @block.gpsimd
                def _(pool):
                    nc.gpsimd.iota(kk[:], [[1, G4 * P]], base=0, channel_multiplier=0,
                                   allow_small_or_imprecise_dtypes=True).then_inc(iotas, 1)
                    nc.gpsimd.iota(cell[:], [[P, BCB]], base=0, channel_multiplier=1,
                                   allow_small_or_imprecise_dtypes=True).then_inc(iotas, 1)
                    pool.wait_ge(k_made, 1)
                    view = ends_dram.rearrange("(k e) r -> k (e r)", e=GROUP)
                    for b in range(BCB):
                        pool.indirect_dma_start(
                            out=R[:, b, :, :].rearrange("p e r -> p (e r)"), out_offset=None, in_=view,
                            in_offset=bass.IndirectOffsetOnAxis(ap=k_of[:, b:b + 1], axis=0)).then_inc(got[b], 16)

                @block.vector
                def _(dve):
                    v = nc.vector
                    step = serial(dve, own)
                    v.memset(last[:], 0.0).then_inc(cleared, 1)
                    dve.wait_ge(loaded, 16 * G4)
                    step(v.tensor_copy(last_i[:], last[:]))
                    step(v.tensor_single_scalar(last_i[:], last_i[:], 7, op=ALU.arith_shift_right))
                    step(v.tensor_copy(last[:], last_i[:]))
                    step(v.scalar_tensor_tensor(key[:], last[:, :, 0], float(NT), last[:, :, 1], ALU.mult, ALU.add))
                    for b in range(G4):
                        ins = v.tensor_scalar(diag[:, b, :], ident[:], key[:, b:b + 1], None, ALU.mult)
                    ins.then_inc(diag_made, 1)
                    dve.wait_ge(iotas, 2)
                    dve.wait_ge(spread, 1)
                    step(v.tensor_tensor(ends[:], pB[:], kk[:], ALU.add))
                    step(v.memset(ends[:, GROUPS:], 1.0e6))
                    for b in range(BCB):
                        step(v.tensor_scalar(less[:], ends[:], cell[:, b:b + 1], None, ALU.is_lt))
                        step(v.tensor_reduce(k_b[:, b:b + 1], less[:], AX.X, ALU.add))
                    step(v.tensor_scalar(k_b[:], k_b[:], float(GROUPS - 1), None, ALU.min))
                    step(v.tensor_tensor(blk[:], cell[:], k_b[:], ALU.subtract))
                    step(v.memset(s_t[:], 0.0))
                    for t in range(1, NT + 1):
                        step(v.tensor_scalar(hit[:], blk[:], float(t * NT), None, ALU.is_ge))
                        step(v.tensor_tensor(s_t[:], s_t[:], hit[:], ALU.add))
                    step(v.scalar_tensor_tensor(d_t[:], s_t[:], -float(NT), blk[:], ALU.mult, ALU.add))
                    step(v.tensor_scalar(tiles[:, 0, :], s_t[:], float(P), None, ALU.mult))
                    step(v.tensor_scalar(tiles[:, 1, :], d_t[:], float(P), None, ALU.mult))
                    step(v.tensor_scalar(s_t[:], s_t[:], float(NT - 1), None, ALU.min))
                    step(v.tensor_copy(k_of[:], k_b[:]))
                    step(v.tensor_copy(ints[:, :, 0], s_t[:]))
                    v.tensor_copy(ints[:, :, 1], d_t[:]).then_inc(k_made, 1)
                    for b in range(BCB):
                        dve.wait_ge(got[b], 16)
                        for q in range(2):
                            step(v.tensor_scalar(R[:, b, :, q], R[:, b, :, q], tiles[:, q, b:b + 1], None, ALU.subtract))
                        dve.sem_inc(rows_made, 1)
                    for i, (b, g, q) in enumerate(turns):
                        dve.wait_ge(turned, i + 1)
                        to = block_loc[:, q, :].rearrange("p (c g) -> p c g", g=2)[:, b * P:(b + 1) * P, g]
                        v.tensor_copy(to, pT[i % 4][:, 0:P]).then_inc(freed, 1)

                @block.tensor
                def _(pe):
                    pe.wait_ge(diag_made, 1)
                    nc.tensor.matmul(pB[:], ones[:], diag[:].rearrange("p b q -> p (b q)"), start=True,
                                     stop=True).then_inc(spread, 1)
                    for i, (b, g, q) in enumerate(turns):
                        pe.wait_ge(rows_made, b + 1)
                        if i >= 4:
                            pe.wait_ge(freed, i - 3)
                        nc.tensor.transpose(pT[i % 4][:, 0:P], R[:, b, g * P:(g + 1) * P, q], ident[:]).then_inc(turned, 1)

        def split3(step, V, parts, r1):
            v = nc.vector
            step(v.tensor_copy(parts[:, :, 0:D], V[:]))
            step(v.tensor_tensor(r1[:], V[:], parts[:, :, 0:D], ALU.subtract))
            step(v.tensor_copy(parts[:, :, D:2 * D], r1[:]))
            step(v.tensor_tensor(r1[:], r1[:], parts[:, :, D:2 * D], ALU.subtract))
            step(v.tensor_copy(parts[:, :, 2 * D:3 * D], r1[:]))

        def adjacency_product(parts, acc):
            STEP = BSTEP
            with ExitStack() as c, nc.Block() as block:
                counts = sbuf("counts_in", [P, NS, STEP, P], BF16, ctx=c)
                nothing = sbuf("nothing", [P, 4 * 2 * D], BF16, ctx=c)
                sums_p = psum("sums", [P, -(-NT // 4) * 4, 2 * D], c)
                ring = lambda name: [sem(f"{name}{s}", c) for s in range(NS)]
                loaded, summed = map(ring, ("loaded", "summed"))
                cleared, all_summed, own = sem("cleared", c), sem("all_summed", c), sem("own", c)
                LOOPS = BCELLS // STEP // NS

                @block.sync
                def _(sp):
                    with sp.Fori(0, LOOPS) as i:
                        for s in range(NS):
                            sp.wait_ge(summed[s], i + 1)
                            sp.dma_start(counts[:, s, :, :].rearrange("p b q -> p (b q)"),
                                         counts_dram[:, bass.ds((i * NS + s) * (STEP * P), STEP * P)]).then_inc(loaded[s], 16)

                @block.tensor
                def _(pe):
                    for s in range(NS):
                        pe.sem_inc(summed[s], 1)
                    pe.wait_ge(cleared, 1)

                    def zeros(start, stop):
                        for n in range(0, NT, 4):
                            ins = nc.tensor.matmul(sums_p[:, n:n + 4, :].rearrange("p a c -> p (a c)"), nothing[:, 0:P],
                                                   nothing[:], start=start, stop=stop)
                        return ins
                    zeros(True, False)
                    with pe.Fori(0, LOOPS) as i:
                        for s in range(NS):
                            at = (i * NS + s) * STEP
                            nm = several(block_row[0:1, bass.ds(at, STEP), :].rearrange("a c q -> a (c q)"), EngineType.PE, NT)
                            ns, ms = nm[0::2], nm[1::2]
                            pe.wait_ge(loaded[s], i * 16 + 16)
                            for b in range(STEP):
                                to = sums_p[:, bass.ds(ns[b], 1), :].rearrange("p a c -> p (a c)")
                                of = parts[:, bass.ds(ms[b], 1), :].rearrange("p a c -> p (a c)")
                                nc.tensor.matmul(to, counts[:, s, b, :], of[:, 0:2 * D], start=False, stop=False)
                                ins = nc.tensor.matmul(to[:, 0:D], counts[:, s, b, :], of[:, 2 * D:3 * D], start=False, stop=False)
                            ins.then_inc(summed[s], 1)
                    zeros(False, True).then_inc(all_summed, 1)

                @block.vector
                def _(dve):
                    nc.vector.memset(nothing[:], 0.0).then_inc(cleared, 1)
                    dve.wait_ge(all_summed, 1)
                    step = serial(dve, own)
                    step(nc.vector.tensor_copy(acc[:, :, 0:D], sums_p[:, 0:NT, 0:D]))
                    step(nc.vector.tensor_tensor(acc[:, :, 0:D], acc[:, :, 0:D], sums_p[:, 0:NT, D:2 * D], ALU.add))

        def edge_scores(table, width, kept_from, near, near_cols, finish, ef=False, counted_cells=(0, BFIRST)):
            with ExitStack() as c, nc.Block() as block:
                rows = sbuf("rows", [P, NS, TB, width], ctx=c)
                ids = sbuf("id_slot", [P, NS, TB], I32, ctx=c)
                loc_all = sbuf("loc_all", [P, NS, TB * P], ctx=c)
                hotT = sbuf("hotT", [P, NS, TB, P], ctx=c)
                a = sbuf("score_a", [P, TB, D], ctx=c)
                b = sbuf("score_b", [P, TB, D], ctx=c)
                efs = sbuf("ef_slot", [DE, NS, BODY, GROUP], ctx=c) if ef else None
                NP = 2
                picked = psum("picked", [P, NP, TB, near_cols if near_cols <= D else 2 * D], c)
                bias = psum("ef_bias", [P, NP, 512], c) if ef else None
                ring = lambda name, n=NS: [sem(f"{name}{s}", c) for s in range(n)]
                ids_made, arrived, loc_in, ef_in, hot_made, products, kept = map(
                    ring, ("ids_made", "arrived", "loc_in", "ef_in", "hot_made", "products", "kept"))
                scored = ring("scored", NP)
                taken, own, lanes = sem("taken", c), sem("own", c), sem("lanes", c)
                loc_flat = loc_dram.rearrange("(a c) e -> a (c e)", a=1)
                LOOPS = STEPS // NS
                USES = NS // NP
                count_from, BBODY = counted_cells
                BT = 2 * BBODY
                lane_h = sbuf("lane_h", [P, P, BT], BF16, ctx=c)
                hot_b = sbuf("hot_blocks", [P, NP, 2, P, BT], BF16, ctx=c)
                counts = sbuf("counts", [P, NP, BBODY, P], BF16, ctx=c)
                counts_p = psum("counts_p", [P, NP, -(-BBODY // 4) * 4, P], c)
                hot_b_made, counted, copied, counts_kept = (
                    ring(n, NP) for n in ("hot_b_made", "counted", "copied", "counts_kept"))

                @block.gpsimd
                def _(pool):
                    with pool.Fori(0, LOOPS) as i:
                        for s in range(NS):
                            pool.wait_ge(ids_made[s], i + 1)
                            pool.sem_inc(taken, 1)
                            for t in range(TB):
                                pool.indirect_dma_start(
                                    out=rows[:, s, t, :], out_offset=None, in_=table,
                                    in_offset=bass.IndirectOffsetOnAxis(ap=ids[:, s, t:t + 1], axis=0)
                                ).then_inc(arrived[s], 16)

                @block.sync
                def _(sp):
                    with sp.Fori(0, LOOPS) as i:
                        for s in range(NS):
                            j = i * NS + s
                            sp.wait_ge(hot_made[s], i + 1)
                            sp.dma_start(loc_all[:, s, :], loc_flat[:, bass.ds(j * (TB * P), TB * P)].to_broadcast([P, TB * P])
                                         ).then_inc(loc_in[s], 16)
                            if ef:
                                sp.wait_ge(products[s], i + 1)
                                ks = several(k_row["dst"][0:1, bass.ds(j * BODY, BODY)], EngineType.SP, GROUPS)
                                for q, k in enumerate(ks):
                                    sp.dma_start(efs[:, s, q, :], efT[:, bass.ds(k * GROUP, GROUP)]).then_inc(ef_in[s], 16)

                @block.scalar
                def _(act):
                    for r in range(NP):
                        act.sem_inc(copied[r], 1)
                        act.sem_inc(counts_kept[r], 16)
                    with act.Fori(0, LOOPS) as i:
                        for s in range(NS):
                            r, use = s % NP, i * USES + s // NP
                            act.wait_ge(counts_kept[r], use * 16 + 16)
                            act.wait_ge(counted[r], use + 2)
                            nc.scalar.copy(counts[:, r, :, :], counts_p[:, r, 0:BBODY, :]).then_inc(copied[r], 1)
                            act.wait_ge(copied[r], use + 2)
                            act.dma_start(counts_dram[:, bass.ds((i * NS + s) * (BBODY * P) + count_from * P, BBODY * P)],
                                          counts[:, r, :, :].rearrange("p b q -> p (b q)")).then_inc(counts_kept[r], 16)
                            at = (i * NS + s) * TB
                            act.wait_ge(arrived[s], i * (16 * TB) + 16 * TB)
                            act.dma_start(kept_rows[:, bass.ds(at * D, TB * D)].rearrange("p (t d) -> p t d", t=TB),
                                          rows[:, s, :, kept_from:kept_from + D]).then_inc(kept[s], 16)
                    for r in range(NP):
                        act.wait_ge(counts_kept[r], LOOPS * USES * 16 + 16)

                @block.vector
                def _(dve):
                    nc.vector.tensor_copy(lane_h[:], lane[:].unsqueeze(2).to_broadcast([P, P, BT])).then_inc(lanes, 1)
                    dve.wait_ge(lanes, 1)
                    for s in range(NS):
                        dve.sem_inc(hot_made[s], 1)
                        dve.sem_inc(kept[s], 16)
                    for s in range(2):
                        nc.vector.tensor_copy(ids[:, s, :], gather_id[:, s * TB:(s + 1) * TB]).then_inc(ids_made[s], 1)
                    for s in range(NP):
                        dve.sem_inc(scored[s], 1)
                    with dve.Fori(0, LOOPS) as i:
                        step = serial(dve, own, i * (NS * finish.steps))

                        def score(s):
                            dve.wait_ge(arrived[s], i * (16 * TB) + 16 * TB)
                            dve.wait_ge(products[s], i + 2)
                            finish(step, picked[:, s % NP, :, :], rows[:, s, :, :], a[:], b[:],
                                   bias[:, s % NP, 0:TB * HEADS] if ef else None, (i * NS + s) * TB)
                            dve.sem_inc(scored[s % NP], 1)

                        def next_ids(s):
                            to = (s + 2) % NS
                            dve.wait_ge(kept[to], i * 16 + (16 if s < 2 else 32))
                            nc.vector.tensor_copy(ids[:, to, :], gather_id[:, bass.ds((i * NS + (s + 2)) * TB, TB)]
                                                  ).then_inc(ids_made[to], 1)
                        for s in range(NS):
                            dve.wait_ge(loc_in[s], i * 16 + 16)
                            dve.wait_ge(products[s], i + 1)
                            nc.vector.tensor_scalar(hotT[:, s, :, :].rearrange("p t e -> p (t e)"), loc_all[:, s, :],
                                                    part[:], None, ALU.is_equal).then_inc(hot_made[s], 1)
                            if s > 0:
                                score(s - 1)
                            next_ids(s)
                            r = s % NP
                            dve.wait_ge(counted[r], i * USES + s // NP + 1)
                            for q in range(2):
                                nc.vector.tensor_tensor(
                                    hot_b[:, r, q, :, :], lane_h[:],
                                    block_loc[:, q, bass.ds((i * NS + s) * BT + 2 * count_from, BT)].unsqueeze(1).to_broadcast([P, P, BT]),
                                    ALU.is_equal).then_inc(hot_b_made[r], 1)
                        score(NS - 1)
                    for s in range(2, NS):
                        dve.wait_ge(kept[s], LOOPS * 16 + 16)

                @block.tensor
                def _(pe):
                    for s in range(NS):
                        pe.sem_inc(products[s], 1)
                    for r in range(NP):
                        pe.sem_inc(counted[r], 1)
                    with pe.Fori(0, LOOPS) as i:
                        for s in range(NS):
                            pe.wait_ge(hot_made[s], i + 2)
                            pe.wait_ge(scored[s % NP], i * USES + s // NP + 1)
                            if ef:
                                pe.wait_ge(ef_in[s], i * (16 * BODY) + 16 * BODY)
                            ns = several(n_row["dst"][0:1, bass.ds((i * NS + s) * BODY + BODY, BODY)], EngineType.PE, NT)
                            for q, n in enumerate(ns):
                                for g in range(2):
                                    t = 2 * q + g
                                    ins = nc.tensor.matmul(picked[:, s % NP, t, 0:near_cols], hotT[:, s, t, :],
                                                           near[:, bass.ds(n, 1), 0:near_cols].rearrange("p a c -> p (a c)"),
                                                           start=True, stop=True)
                                    if ef:
                                        ins = nc.tensor.matmul(bias[:, s % NP, t * HEADS:(t + 1) * HEADS],
                                                               efs[:, s, q, g * P:(g + 1) * P], weT_s[:],
                                                               start=True, stop=True)
                            ins.then_inc(products[s], 1)
                            r, use = s % NP, i * USES + s // NP
                            pe.wait_ge(hot_b_made[r], use * 2 + 2)
                            pe.wait_ge(copied[r], use + 1)
                            for t in range(BT):
                                ins = nc.tensor.matmul(counts_p[:, r, t // 2, :], hot_b[:, r, 1, :, t], hot_b[:, r, 0, :, t],
                                                       start=t % 2 == 0, stop=t % 2 == 1)
                            ins.then_inc(counted[r], 1)

        def softmax_exp(S, H, SE=None, SX=None, floor=None):
            NB = -(-TILES * H // P)
            TP = P // H
            NCH = NB * TP
            tail = TILES - (NB - 1) * TP
            with ExitStack() as c:
                def big(name):
                    return sbuf(name, [P, NB, P], ctx=c)
                ST, KT, LT, fwd, bwd, t1, t2 = (big(n) for n in ("ST", "KT", "LT", "fwd", "bwd", "t1", "t2"))
                ET = big("ET") if SE is not None else None
                ends = sbuf("chunk_ends", [P, 4, NB], ctx=c)
                pack = sbuf("pack", [NB, 4, H, TP], ctx=c)
                chunk = sbuf("chunk", [H, 4, NCH], ctx=c)
                links = sbuf("links", [H, 4, NCH], ctx=c)
                scans = sbuf("scans", [H, 2, NCH], ctx=c)
                carry = sbuf("carry", [H, 2, NCH], ctx=c)
                back = sbuf("carry_back", [NB, 2, H, TP], ctx=c)
                back_p = sbuf("carry_perm", [NB, 2, P], ctx=c)
                chunk_dram = dram(f"chunk_dram{H}", [4, H, NCH])
                carry_dram = dram(f"carry_dram{H}", [2, H, NCH])
                flat = lambda t: t[:].rearrange("p b e -> p (b e)")
                with nc.Block() as block:
                    PB = 4
                    pT = psum("pT", [P, PB, 512], c)
                    cleared, keys_in, turned, freed = (sem(n, c) for n in ("cleared", "keys_in", "turned", "freed"))
                    ends_made, packed, sent, chunk_in = (sem(n, c) for n in ("ends_made", "packed", "sent", "chunk_in"))
                    carry_made, carry_out, carry_in, perm_made = (sem(n, c) for n in ("carry_made", "carry_out", "carry_in", "perm_made"))
                    maxed, exped, own = (sem(n, c) for n in ("maxed", "exped", "own"))
                    jobs = [(S, b) for b in range(NB)] + ([(SE, b) for b in range(NB)] if SE is not None else [])
                    n_in = len(jobs)
                    width = lambda b: P if b < NB - 1 else tail * H

                    @block.sync
                    def _(sp):
                        sp.wait_ge(cleared, 1)
                        for frm, to in ((key_dram, KT), (loc_dram, LT)):
                            rows = frm.rearrange("c (g e) -> (c g) e", g=2)
                            for h in range(H):
                                lead = slice(h, P, H)
                                if NB > 1:
                                    sp.dma_start(to[lead, 0:NB - 1, :], rows[0:(NB - 1) * TP, :].rearrange("(b t) e -> t b e", t=TP)
                                                 ).then_inc(keys_in, 16)
                                lead = slice(h, h + (tail - 1) * H + 1, H)
                                sp.dma_start(to[lead, NB - 1, :], rows[(NB - 1) * TP:TILES, :]).then_inc(keys_in, 16)
                        sp.wait_ge(packed, 1)
                        sp.dma_start(chunk_dram.rearrange("q h (b t) -> b q h t", t=TP), pack[:]).then_inc(sent, 16)
                        sp.wait_ge(sent, 16)
                        sp.dma_start(chunk[:], chunk_dram.rearrange("q h c -> h q c")).then_inc(chunk_in, 16)
                        sp.wait_ge(carry_made, 1)
                        sp.dma_start(carry_dram.rearrange("q h c -> h q c"), carry[:]).then_inc(carry_out, 16)
                        sp.wait_ge(carry_out, 16)
                        sp.dma_start(back[:], carry_dram.rearrange("q h (b t) -> b q h t", t=TP)).then_inc(carry_in, 16)

                    @block.vector
                    def _(dve):
                        v = nc.vector
                        step = serial(dve, own)
                        step(v.memset(LT[:], -1.0))
                        step(v.memset(ST[:], -BIG))
                        if SE is not None:
                            step(v.memset(ET[:], -BIG))
                        v.memset(KT[:], -5.0).then_inc(cleared, 1)
                        for i, (_, b) in enumerate(jobs):
                            w = width(b)
                            dve.wait_ge(turned, i + 1)
                            to = ST if i < NB else ET
                            v.tensor_copy(to[0:w, b, :], pT[0:w, i % PB, 0:P]).then_inc(freed, 1)
                        dve.wait_ge(freed, n_in)
                        dve.wait_ge(keys_in, 16 * 4 * H)
                        step(v.tensor_scalar(LT[:], LT[:], 0.0, -BIG, ALU.is_lt, ALU.mult))
                        if SE is not None:
                            step(v.tensor_tensor(t2[:], ST[:], ET[:], ALU.max))
                            step(v.tensor_tensor(t2[:], t2[:], LT[:], ALU.add))
                            held = t2
                        else:
                            step(v.tensor_tensor(ST[:], ST[:], LT[:], ALU.add))
                            held = ST
                        step(v.memset(t1[:, :, 0:1], 1.0))
                        step(v.tensor_tensor(t1[:, :, 1:P], KT[:, :, 1:P], KT[:, :, 0:P - 1], ALU.not_equal))
                        step(v.tensor_scalar(t1[:], t1[:], -BIG, None, ALU.mult))
                        step(v.tensor_tensor_scan(flat(fwd), flat(t1), flat(held), -BIG, ALU.add, ALU.max))
                        step(v.memset(t1[:, :, P - 1:P], 1.0))
                        step(v.tensor_tensor(t1[:, :, 0:P - 1], KT[:, :, 0:P - 1], KT[:, :, 1:P], ALU.not_equal))
                        step(v.tensor_scalar(t1[:], t1[:], -BIG, None, ALU.mult))
                        step(v.tensor_tensor_scan(flat(bwd)[:, ::-1], flat(t1)[:, ::-1], flat(held)[:, ::-1], -BIG, ALU.add, ALU.max))
                        step(v.tensor_copy(ends[:, 0, :], KT[:, :, 0]))
                        step(v.tensor_copy(ends[:, 1, :], KT[:, :, P - 1]))
                        step(v.tensor_copy(ends[:, 2, :], fwd[:, :, P - 1]))
                        step(v.tensor_copy(ends[:, 3, :], bwd[:, :, 0]))
                        dve.sem_inc(ends_made, 1)
                        for q in range(4):
                            dve.wait_ge(turned, n_in + q + 1)
                            step(v.tensor_copy(pack[:, q, :, :], pT[0:NB, q, 0:P].rearrange("p (t h) -> p h t", h=H)))
                        dve.sem_inc(packed, 1)
                        step(v.tensor_tensor(fwd[:], fwd[:], bwd[:], ALU.max))
                        step(v.tensor_tensor(bwd[:], KT[:], KT[:, :, 0:1].to_broadcast([P, NB, P]), ALU.not_equal))
                        step(v.tensor_scalar(bwd[:], bwd[:], -BIG, None, ALU.mult))
                        step(v.tensor_tensor(t1[:], KT[:], KT[:, :, P - 1:P].to_broadcast([P, NB, P]), ALU.not_equal))
                        step(v.tensor_scalar(t1[:], t1[:], -BIG, None, ALU.mult))
                        dve.wait_ge(chunk_in, 16)
                        K0, K1, LF, FB = (chunk[:, q, :] for q in range(4))
                        m = NCH - 1
                        step(v.memset(links[:], 1.0))
                        step(v.tensor_tensor(links[:, 0, 1:], K1[:, 1:], K1[:, 0:m], ALU.not_equal))
                        step(v.tensor_tensor(links[:, 1, 1:], K0[:, 1:], K1[:, 0:m], ALU.not_equal))
                        step(v.tensor_tensor(links[:, 2, 0:m], K0[:, 0:m], K0[:, 1:], ALU.not_equal))
                        step(v.tensor_tensor(links[:, 3, 0:m], K1[:, 0:m], K0[:, 1:], ALU.not_equal))
                        step(v.tensor_scalar(links[:], links[:], -BIG, None, ALU.mult))
                        step(v.tensor_tensor_scan(scans[:, 0, :], links[:, 0, :], LF, -BIG, ALU.add, ALU.max))
                        step(v.tensor_tensor_scan(scans[:, 1, ::-1], links[:, 2, ::-1], FB[:, ::-1], -BIG, ALU.add, ALU.max))
                        step(v.memset(carry[:], -BIG))
                        step(v.tensor_tensor(carry[:, 0, 1:], scans[:, 0, 0:m], links[:, 1, 1:], ALU.add))
                        step(v.tensor_tensor(carry[:, 1, 0:m], scans[:, 1, 1:], links[:, 3, 0:m], ALU.add))
                        dve.sem_inc(carry_made, 1)
                        dve.wait_ge(carry_in, 16)
                        for q in range(2):
                            step(v.tensor_copy(back_p[:, q, :].rearrange("p (t h) -> p h t", h=H), back[:, q, :, :]))
                        dve.sem_inc(perm_made, 1)
                        for q, near_run in ((0, bwd), (1, t1)):
                            dve.wait_ge(turned, n_in + 4 + q + 1)
                            step(v.tensor_tensor(near_run[:], near_run[:],
                                                 pT[:, q, 0:NB].unsqueeze(2).to_broadcast([P, NB, P]), ALU.add))
                            step(v.tensor_tensor(fwd[:], fwd[:], near_run[:], ALU.max))
                        if floor is not None:
                            step(v.tensor_scalar(fwd[:], fwd[:], floor, None, ALU.max))
                        step(v.tensor_tensor(ST[:], ST[:], fwd[:], ALU.subtract))
                        if SE is not None:
                            step(v.tensor_tensor(ET[:], ET[:], fwd[:], ALU.subtract))
                            step(v.tensor_scalar(ST[:], ST[:], 0.0, None, ALU.min))
                            step(v.tensor_scalar(ET[:], ET[:], 0.0, None, ALU.min))
                        dve.sem_inc(maxed, 1)
                        for i, (_, b) in enumerate(jobs):
                            w = width(b)
                            dve.wait_ge(turned, n_in + 6 + i + 1)
                            to = S if i < NB else SX
                            v.tensor_copy(to[:].rearrange("p t h -> p (t h)")[:, b * P:b * P + w], pT[:, i % PB, 0:w]).then_inc(freed, 1)

                    @block.scalar
                    def _(act):
                        act.wait_ge(maxed, 1)
                        nc.scalar.activation(ST[:], ST[:], ACT.Exp).then_inc(exped, 1)
                        if SE is not None:
                            nc.scalar.activation(ET[:], ET[:], ACT.Exp).then_inc(exped, 1)

                    @block.tensor
                    def _(pe):
                        for i, (frm, b) in enumerate(jobs):
                            w = width(b)
                            if i >= PB:
                                pe.wait_ge(freed, i - PB + 1)
                            nc.tensor.transpose(pT[0:w, i % PB, 0:P], frm[:].rearrange("p t h -> p (t h)")[:, b * P:b * P + w],
                                                ident[:]).then_inc(turned, 1)
                        pe.wait_ge(ends_made, 1)
                        pe.wait_ge(freed, n_in)
                        for q in range(4):
                            nc.tensor.transpose(pT[0:NB, q, 0:P], ends[:, q, :], ident[:]).then_inc(turned, 1)
                        pe.wait_ge(perm_made, 1)
                        for q in range(2):
                            nc.tensor.transpose(pT[:, q, 0:NB], back_p[:, q, :], ident[:NB, :NB]).then_inc(turned, 1)
                        pe.wait_ge(exped, 1 if SE is None else 2)
                        for i, (_, b) in enumerate(jobs):
                            w = width(b)
                            if i >= PB:
                                pe.wait_ge(freed, n_in + i - PB + 1)
                            frm = ST if i < NB else ET
                            nc.tensor.transpose(pT[:, i % PB, 0:w], frm[0:w, b, :], ident[:w, :w]).then_inc(turned, 1)

        def project(x_in, width, w, n_out, to, bias=None, relu=False):
            FIVE = 5
            GROUPS_OF_5 = NT // FIVE
            STR = 1 << (n_out - 1).bit_length()
            tiles_of = lambda i: range(i * FIVE, (i + 1) * FIVE)
            with ExitStack() as c, nc.Block() as block:
                xT = sbuf("xT", [width, 2, FIVE, P], ctx=c)
                pT = psum("pT", [P, 2, 8, P], c)
                pO = psum("pO", [P, FIVE, STR], c)
                turned, copied, made, own = (sem(s, c) for s in ("turned", "copied", "made", "own"))

                @block.scalar
                def _(act):
                    for i in range(GROUPS_OF_5):
                        act.wait_ge(turned, i + 1)
                        if i >= 2:
                            act.wait_ge(made, i - 1)
                        nc.scalar.copy(xT[:, i % 2, :, :], pT[0:width, i % 2, 0:FIVE, :]).then_inc(copied, 1)

                @block.vector
                def _(dve):
                    for i in range(GROUPS_OF_5):
                        dve.wait_ge(made, i + 1)
                        o = to[:, i * FIVE:(i + 1) * FIVE, 0:n_out]
                        if bias is None:
                            nc.vector.tensor_copy(o, pO[:, :, 0:n_out]).then_inc(own, 1)
                        else:
                            nc.vector.tensor_tensor(o, pO[:, :, 0:n_out],
                                                    bias[:].unsqueeze(1).to_broadcast([P, FIVE, n_out]), ALU.add).then_inc(own, 1)
                    if relu:
                        dve.wait_ge(own, GROUPS_OF_5)
                        nc.vector.tensor_scalar(to[:], to[:], 0.0, None, ALU.max).then_inc(own, 1)

                @block.tensor
                def _(pe):
                    for i in range(GROUPS_OF_5 + 1):
                        if i < GROUPS_OF_5:
                            if i >= 2:
                                pe.wait_ge(copied, i - 1)
                            for t in tiles_of(i):
                                ins = nc.tensor.transpose(pT[0:width, i % 2, t % FIVE, :], x_in[:, t, 0:width], ident[:])
                            ins.then_inc(turned, 1)
                        if i >= 1:
                            pe.wait_ge(copied, i)
                            if i >= 2:
                                pe.wait_ge(own, i - 1)
                            for t in tiles_of(i - 1):
                                ins = nc.tensor.matmul(pO[:, t % FIVE, 0:n_out], xT[:, (i - 1) % 2, t % FIVE, :], w[:],
                                                       start=True, stop=True)
                            ins.then_inc(made, 1)

        def wide(v):
            return v.unsqueeze(2).to_broadcast([P, NT, D])

        def rowwise(v, m=D):
            return v.unsqueeze(1).to_broadcast([P, NT, m])

        def layernorm(step, X, sq, mean, var, affine=None):
            v = nc.vector
            step(v.tensor_reduce(mean[:], X[:], AX.X, ALU.add))
            step(v.tensor_scalar(mean[:], mean[:], 1.0 / D, None, ALU.mult))
            step(v.tensor_tensor(X[:], X[:], wide(mean[:]), ALU.subtract))
            step(v.tensor_tensor(sq[:], X[:], X[:], ALU.mult))
            step(v.tensor_reduce(var[:], sq[:], AX.X, ALU.add))
            step(v.tensor_scalar(var[:], var[:], 1.0 / D, EPS, ALU.mult, ALU.add))
            step.root()
            step(v.reciprocal(var[:], var[:]))
            step(v.tensor_tensor(X[:], X[:], wide(var[:]), ALU.mult))
            if affine is not None:
                step(v.tensor_tensor(X[:], X[:], rowwise(affine[0][:]), ALU.mult))
                step(v.tensor_tensor(X[:], X[:], rowwise(affine[1][:]), ALU.add))

        def node_math(body, norms=1):
            with ExitStack() as c, nc.Block() as block:
                sq = sbuf("node_sq", [P, NT, D], ctx=c)
                a, b = sbuf("node_a", [P, NT], ctx=c), sbuf("node_b", [P, NT], ctx=c)
                own, var_ready, root_ready = sem("own", c), sem("var_ready", c), sem("root_ready", c)

                @block.vector
                def _(dve):
                    step = serial(dve, own)
                    asked = [0]

                    def root():
                        asked[0] += 1
                        dve.sem_inc(var_ready, 1)
                        dve.wait_ge(root_ready, asked[0])
                    step.root = root
                    body(step, sq, a, b)

                @block.scalar
                def _(act):
                    for i in range(norms):
                        act.wait_ge(var_ready, i + 1)
                        nc.scalar.activation(b[:], b[:], ACT.Sqrt).then_inc(root_ready, 1)

        def store(pairs):
            with ExitStack() as c, nc.Block() as block:
                kept = [sem("kept", c) for _ in pairs]

                @block.sync
                def _(sp):
                    for (to, frm), s in zip(pairs, kept):
                        sp.dma_start(to, frm).then_inc(s, 16)
                    for s in kept:
                        sp.wait_ge(s, 16)

        def load_weights(X, pairs):
            with ExitStack() as c, nc.Block() as block:
                s = sem("weights_in", c)

                @block.sync
                def _(sp):
                    sp.dma_start(X[:], x.rearrange("(t p) d -> p t d", p=P)).then_inc(s, 16)
                    for to, frm in pairs:
                        sp.dma_start(to[:], frm).then_inc(s, 16)
                    sp.wait_ge(s, 16 * (len(pairs) + 1))

        nodes_dram = {k: dram(f"nodes_{k}", [NPAD, w]) for k, w in (("kv", 2 * D), ("xl", D))}
        kept_rows = dram("kept_rows", [P, TILES * D])

        X = sbuf("X", [P, NT, D])
        block_row = sbuf("block_row", [1, BCELLS, 2], I32)
        block_loc = sbuf("block_loc", [P, 2, 2 * BCB * P], BF16)
        ends_copied = sem("ends_copied", top)
        acc = sbuf("acc", [P, NT, D + HEADS])
        deg = sbuf("deg", [P, NT])

        def bc(v):
            return v.to_broadcast([P, v.shape[1]])
        wq_s, bq_s = sbuf("wqkv_s", [D, 3 * D]), sbuf("bqkv_s", [P, 3 * D])
        weT_s, be_s, lt_s = sbuf("weT_s", [DE, HEADS]), sbuf("be_s", [P, HEADS]), sbuf("lt_s", [P, HEADS])
        wo_s, bo_s, ga_s, bt_s = sbuf("wo_s", [D, D]), sbuf("bo_s", [P, D]), sbuf("ga_s", [P, D]), sbuf("bt_s", [P, D])
        wlr_s, att_s, bias2_s = sbuf("wlr_s", [D, 2 * D]), sbuf("att_s", [P, D]), sbuf("bias2_s", [P, D])
        w1_s, b1_s, w2_s, b2_s = sbuf("w1_s", [D, HID]), sbuf("b1_s", [P, HID]), sbuf("w2_s", [HID, D]), sbuf("b2_s", [P, D])

        setup()
        load_weights(X, [(wq_s, wqkv), (bq_s, bc(bqkv)), (weT_s, weT), (be_s, bc(be)), (lt_s, bc(log_temp)), (wo_s, woT),
                         (bo_s, bc(bo)), (ga_s, bc(gamma)), (bt_s, bc(beta)), (wlr_s, wlr), (att_s, bc(att)),
                         (bias2_s, bc(bias2)), (w1_s, w1), (b1_s, bc(b1)), (w2_s, w2), (b2_s, bc(b2))])
        rank()
        staircase("dst", rec_dram.rearrange("(k e) r -> k (e r)", e=GROUP)[:, GROUP * REC - REC + 1:GROUP * REC - REC + 2])
        with ExitStack() as c:
            w_dst = sbuf("w_dst", [P, TILES], ctx=c)
            place_dst = sbuf("place_dst", [P, TILES], ctx=c)
            ends_dst = sbuf("ends_dst", [P, TILES, 2], ctx=c)
            rows_by_cell()
            messages()
        staircase("src", msg_dram.rearrange("(k e) r -> k (e r)", e=GROUP)[:, GROUP * MSG - MSG + D + 1:GROUP * MSG - MSG + D + 2])
        copy_ends()
        aggregate("src", acc, D + 1)

        def layer0(step, sq, a, b):
            step(nc.vector.tensor_scalar(deg[:], acc[:, :, D], 1.0, None, ALU.max))
            step(nc.vector.reciprocal(deg[:], deg[:]))
            step(nc.vector.tensor_tensor(X[:], X[:], acc[:, :, 0:D], ALU.add))
            layernorm(step, X, sq, a, b)
        node_math(layer0)

        block_staircase()

        node_view = lambda k: nodes_dram[k].rearrange("(t p) d -> p t d", p=P)
        with ExitStack() as c:
            S = sbuf("S", [P, TILES, HEADS], ctx=c)
            with ExitStack() as c1:
                qkv = sbuf("qkv", [P, NT, 3 * D], ctx=c1)
                project(X, D, wq_s, 3 * D, qkv, bias=bq_s)
                store([(node_view("kv"), qkv[:, :, D:3 * D])])

                def attention(step, picked, rows, a, b, bias, at):
                    v = nc.vector
                    step(v.tensor_tensor(a, picked, rows[:, :, 0:D], ALU.mult))
                    step(v.tensor_reduce(b[:, :, 0:HEADS], a.rearrange("p t (h d) -> p t h d", h=HEADS), AX.X, ALU.add))
                    step(v.scalar_tensor_tensor(S[:, bass.ds(at, TB), :], b[:, :, 0:HEADS], DH ** -0.5,
                                                bias.rearrange("p (t h) -> p t h", h=HEADS), ALU.mult, ALU.add))
                attention.steps = 3
                edge_scores(nodes_dram["kv"], 2 * D, D, qkv, D, attention, ef=True, counted_cells=(0, BFIRST))

            with ExitStack() as b_, nc.Block() as block:
                own, temp = sem("own", b_), sem("temp", b_)

                @block.scalar
                def _(act):
                    nc.scalar.activation(lt_s[:], lt_s[:], ACT.Exp).then_inc(temp, 1)

                @block.vector
                def _(dve):
                    step = serial(dve, own)
                    heads = lambda t: t[:].unsqueeze(1).to_broadcast([P, TILES, HEADS])
                    step(nc.vector.tensor_tensor(S[:], S[:], heads(be_s), ALU.add))
                    dve.wait_ge(temp, 1)
                    step(nc.vector.tensor_tensor(S[:], S[:], heads(lt_s), ALU.mult))
            softmax_exp(S, HEADS, floor=-1.0e9)
            aggregate("dst", acc, D + HEADS, stream=kept_rows, weights=S, extra=S)
        with ExitStack() as c:
            O = sbuf("O", [P, NT, D], ctx=c)
            den = sbuf("den", [P, NT, HEADS], ctx=c)

            def attended(step, sq, a, b):
                v = nc.vector
                step(v.tensor_scalar(den[:], acc[:, :, D:D + HEADS], 1e-10, None, ALU.add))
                step(v.reciprocal(den[:], den[:]))
                for h in range(HEADS):
                    part_h = slice(h * DH, (h + 1) * DH)
                    step(v.tensor_tensor(O[:, :, part_h], acc[:, :, part_h], den[:, :, h:h + 1].to_broadcast([P, NT, DH]), ALU.mult))
            node_math(attended, norms=0)
            Z = sbuf("Z", [P, NT, D], ctx=c)
            project(O, D, wo_s, D, Z, bias=bo_s)

            def layer1(step, sq, a, b):
                v = nc.vector
                step(v.tensor_tensor(Z[:], Z[:], X[:], ALU.add))
                layernorm(step, Z, sq, a, b, affine=(ga_s, bt_s))
                step(v.tensor_tensor(X[:], X[:], Z[:], ALU.add))
                layernorm(step, X, sq, a, b)
            node_math(layer1, norms=2)

        with ExitStack() as c:
            near = sbuf("xr_self", [P, NT, D + 1], ctx=c)
            xl = sbuf("xl", [P, NT, D], ctx=c)
            S = sbuf("S2", [P, TILES, 1], ctx=c)
            SE = sbuf("SE", [P, TILES, 1], ctx=c)
            with ExitStack() as c1:
                lr = sbuf("lr", [P, NT, 2 * D], ctx=c1)
                project(X, D, wlr_s, 2 * D, lr)

                def own_scores(step, sq, a, b):
                    v = nc.vector
                    step(v.tensor_copy(xl[:], lr[:, :, 0:D]))
                    step(v.tensor_copy(near[:, :, 0:D], lr[:, :, D:2 * D]))
                    step(v.tensor_tensor(sq[:], lr[:, :, 0:D], lr[:, :, D:2 * D], ALU.add))
                    step(v.scalar_tensor_tensor(sq[:], sq[:], 0.2, sq[:], ALU.mult, ALU.max))
                    step(v.tensor_tensor(sq[:], sq[:], rowwise(att_s[:]), ALU.mult))
                    step(v.tensor_reduce(near[:, :, D], sq[:], AX.X, ALU.add))
                node_math(own_scores, norms=0)
                store([(node_view("xl"), xl[:])])

            def gat(step, picked, rows, a, b, bias, at):
                v = nc.vector
                step(v.tensor_tensor(a, picked[:, :, 0:D], rows, ALU.add))
                step(v.scalar_tensor_tensor(b, a, 0.2, a, ALU.mult, ALU.max))
                step(v.tensor_tensor(a, b, att_s[:].unsqueeze(1).to_broadcast([P, TB, D]), ALU.mult))
                step(v.tensor_reduce(S[:, bass.ds(at, TB), 0], a, AX.X, ALU.add))
                step(v.tensor_copy(SE[:, bass.ds(at, TB), 0], picked[:, :, D]))
            gat.steps = 5
            edge_scores(nodes_dram["xl"], D, 0, near, D + 1, gat, counted_cells=(BFIRST * STEPS, BSECOND))
            SX = sbuf("SX", [P, TILES, 2], ctx=c)
            softmax_exp(S, 1, SE=SE, SX=SE)
            with ExitStack() as b_, nc.Block() as block:
                own = sem("own", b_)

                @block.vector
                def _(dve):
                    step = serial(dve, own)
                    step(nc.vector.tensor_copy(SX[:, :, 0:1], S[:]))
                    step(nc.vector.tensor_copy(SX[:, :, 1:2], SE[:]))
            aggregate("dst", acc, D + 3, stream=kept_rows, weights=S, extra=SX)
            own_w = sbuf("own_w", [P, NT], ctx=c)

            def layer2(step, sq, a, b):
                v = nc.vector
                step(v.tensor_scalar(a[:], acc[:, :, D + 2], 1.0, None, ALU.max))
                step(v.reciprocal(a[:], a[:]))
                step(v.tensor_tensor(own_w[:], acc[:, :, D + 1], a[:], ALU.mult))
                step(v.tensor_scalar(a[:], acc[:, :, D + 2], 0.0, None, ALU.is_equal))
                step(v.tensor_tensor(own_w[:], own_w[:], a[:], ALU.add))
                step(v.tensor_tensor(b[:], acc[:, :, D], own_w[:], ALU.add))
                step(v.reciprocal(b[:], b[:]))
                step(v.tensor_tensor(sq[:], xl[:], wide(own_w[:]), ALU.mult))
                step(v.tensor_tensor(sq[:], sq[:], acc[:, :, 0:D], ALU.add))
                step(v.tensor_tensor(sq[:], sq[:], wide(b[:]), ALU.mult))
                step(v.tensor_tensor(sq[:], sq[:], rowwise(bias2_s[:]), ALU.add))
                step(v.tensor_tensor(X[:], X[:], sq[:], ALU.add))
                layernorm(step, X, sq, a, b)
            node_math(layer2)

        with ExitStack() as c:
            Y = sbuf("Y", [P, NT, D], ctx=c)
            Hd = sbuf("H", [P, NT, HID], ctx=c)
            parts = sbuf("parts", [P, NT, 3 * D], BF16, ctx=c)
            node_math(lambda step, sq, a, b: split3(step, X, parts, sq), norms=0)
            adjacency_product(parts, acc)

            def mean3(step, sq, a, b):
                step(nc.vector.tensor_tensor(Y[:], acc[:, :, 0:D], wide(deg[:]), ALU.mult))
                step(nc.vector.tensor_tensor(Y[:], Y[:], X[:], ALU.add))
            node_math(mean3, norms=0)
            project(Y, D, w1_s, HID, Hd, bias=b1_s, relu=True)
            project(Hd, HID, w2_s, D, Y)
            node_math(lambda step, sq, a, b: split3(step, Y, parts, sq), norms=0)
            adjacency_product(parts, acc)

            def last3(step, sq, a, b):
                step(nc.vector.tensor_tensor(sq[:], acc[:, :, 0:D], wide(deg[:]), ALU.mult))
                step(nc.vector.tensor_tensor(Y[:], Y[:], sq[:], ALU.add))
                step(nc.vector.tensor_tensor(Y[:], Y[:], rowwise(b2_s[:]), ALU.add))
                step(nc.vector.tensor_tensor(X[:], X[:], Y[:], ALU.add))
                layernorm(step, X, sq, a, b)
            node_math(last3)
        full = NODES // P
        store([(out[0:full * P, :].rearrange("(t p) d -> p t d", p=P), X[:, 0:full, :]),
               (out[full * P:NODES, :], X[0:NODES - full * P, full, :])])


def layout(inp):
    import numpy as np
    a = {k: np.ascontiguousarray(v) for k, v in inp.items()}

    def padded(v, n, fill):
        o = np.full((n,) + v.shape[1:], fill, v.dtype)
        o[:v.shape[0]] = v
        return o
    g1, g2, g3 = "L1_gnn_", "L2_gnn_", "L3_gnn_"
    row = lambda v: np.ascontiguousarray(v.reshape(1, -1))
    return {
        "x_in": padded(a["x"], NPAD, 0),
        "src_in": padded(a["src"], EPAD, NPAD - 1),
        "dst_in": padded(a["dst"], EPAD, NPAD - 1),
        "weight_in": padded(a["edge_weight"], EPAD, 0),
        "efT_in": np.ascontiguousarray(padded(a["edge_attr_32"], EPAD, 0).T),
        "wqkv_in": np.ascontiguousarray(np.concatenate([a[g1 + "Wq"].T, a[g1 + "Wk"].T, a[g1 + "Wv"].T], 1)),
        "bqkv_in": row(np.concatenate([a[g1 + "bq"], a[g1 + "bk"], a[g1 + "bv"]])),
        "weT_in": np.ascontiguousarray(a[g1 + "We"].T),
        "be_in": row(a[g1 + "be"]),
        "woT_in": np.ascontiguousarray(a[g1 + "Wo"].T),
        "bo_in": row(a[g1 + "bo"]),
        "gamma_in": row(a[g1 + "ln_gamma"]),
        "beta_in": row(a[g1 + "ln_beta"]),
        "log_temp_in": row(a[g1 + "log_temp"]),
        "wlr_in": np.ascontiguousarray(np.concatenate([a[g2 + "W_l"], a[g2 + "W_r"]], 1)),
        "att_in": row(a[g2 + "att"]),
        "bias2_in": row(a[g2 + "bias"]),
        "w1_in": a[g3 + "W1"],
        "b1_in": row(a[g3 + "b1"]),
        "w2_in": a[g3 + "W2"],
        "b2_in": row(a[g3 + "b2"]),
    }


def kernel(**inputs):
    import numpy as np
    import concourse.bacc as bacc
    from concourse.bass_utils import run_bass_kernel_spmd as run
    nc = bacc.Bacc("TRN2", target_bir_lowering=False, num_devices=1)
    arrays = layout(inputs)
    args = [nc.dram_tensor(n, a.shape, mybir.dt.from_np(a.dtype), kind="ExternalInput").ap() for n, a in arrays.items()]
    out = nc.dram_tensor("out", (NODES, D), F32, kind="ExternalOutput").ap()
    gnn(nc, *args, out)
    r = run(nc, [arrays], core_ids=[0])
    return r.results[0]["out"]
```
